# Optimizing a Trainium2 kernel written in Bass

```python
import numpy as np
import jax
import jax.numpy as jnp

def _softmax(x, axis=-1):
    return jax.nn.softmax(x, axis=axis)

def _gelu(x):
    return jax.nn.gelu(x, approximate=True)

def _silu(x):
    return jax.nn.silu(x)

def _sigmoid(x):
    return jax.nn.sigmoid(x)

def _layernorm(x, axis=-1, eps=1e-05):
    m = jnp.mean(x, axis=axis, keepdims=True)
    v = jnp.var(x, axis=axis, keepdims=True)
    return (x - m) / jnp.sqrt(v + eps)

def _scatter_add(tgt, idx, src, axis=0):
    return tgt.at[idx].add(src)

def _segment_sum(src, seg, n):
    return jax.ops.segment_sum(src, seg, n)
kernel_name = 'mk_adaln_d1_jaxref_r8_dc369e'

def setup_inputs(seed: int=0):
    np.random.seed(seed)
    _w = jnp.asarray

    def _L0_attn_setup():
        import jax, jax.numpy as jnp
        import numpy as np
        D_MODEL = 128
        N_HEADS = 16
        D_K = D_MODEL // N_HEADS

        def _rope_cache(T, dtype):
            half = D_K // 2
            freq = 1.0 / 10000.0 ** (2.0 * jnp.arange(half, dtype=dtype) / D_K)
            angles = jnp.arange(T, dtype=dtype)[:, None] * freq[None, :]
            return (jnp.cos(angles), jnp.sin(angles))

        def _apply_rope(x, cos, sin):
            half = x.shape[-1] // 2
            x1, x2 = (x[..., :half], x[..., half:])
            return jnp.concatenate([x1 * cos - x2 * sin, x1 * sin + x2 * cos], axis=-1)
        key = jax.random.key(seed)
        ks = jax.random.split(key, 9)
        s = 0.02
        return {'x': jax.random.normal(ks[0], (4, 256, D_MODEL), dtype=jnp.float32), 'WQ_w': jax.random.normal(ks[1], (D_MODEL, D_MODEL), dtype=jnp.float32) * s, 'WQ_b': jax.random.normal(ks[2], (D_MODEL,), dtype=jnp.float32) * s, 'WK_w': jax.random.normal(ks[3], (D_MODEL, D_MODEL), dtype=jnp.float32) * s, 'WK_b': jax.random.normal(ks[4], (D_MODEL,), dtype=jnp.float32) * s, 'WV_w': jax.random.normal(ks[5], (D_MODEL, D_MODEL), dtype=jnp.float32) * s, 'WV_b': jax.random.normal(ks[6], (D_MODEL,), dtype=jnp.float32) * s, 'Wo_w': jax.random.normal(ks[7], (D_MODEL, D_MODEL), dtype=jnp.float32) * s, 'Wo_b': jax.random.normal(ks[8], (D_MODEL,), dtype=jnp.float32) * s}
    _L0_attn_in = _L0_attn_setup()

    def _L0_ffn_setup():
        import math
        import jax, jax.numpy as jnp
        import numpy as np
        TOP_K = 2
        _GELU_C = math.sqrt(2.0 / math.pi)

        def gelu_new(x):
            return 0.5 * x * (1.0 + jnp.tanh(_GELU_C * (x + 0.044715 * x * x * x)))
        key = jax.random.key(seed)
        ks = jax.random.split(key, 6)
        B, T, C, E, H = (2, 256, 128, 8, 512)
        s_in = 1.0 / math.sqrt(C)
        s_hid = 1.0 / math.sqrt(H)
        return {'x': jax.random.normal(ks[0], (B, T, C), dtype=jnp.float32), 'router_w': jax.random.normal(ks[1], (E, C), dtype=jnp.float32) * s_in, 'w_fc': jax.random.normal(ks[2], (E, C, H), dtype=jnp.float32) * s_in, 'b_fc': jax.random.normal(ks[3], (E, H), dtype=jnp.float32) * 0.02, 'w_proj': jax.random.normal(ks[4], (E, H, C), dtype=jnp.float32) * s_hid, 'b_proj': jax.random.normal(ks[5], (E, C), dtype=jnp.float32) * 0.02}
    _L0_ffn_in = _L0_ffn_setup()
    _L0_c = _w((lambda *s: np.random.randn(*s).astype(np.float32) * 0.05)(16, 128))
    _L0_wmod = _w((lambda *s: np.random.randn(*s).astype(np.float32) * 0.05)(128, 6 * 128) * 128 ** (-0.5))
    _d = {'L0_attn_x': _L0_attn_in['x'], 'L0_attn_WQ_w': _L0_attn_in['WQ_w'], 'L0_attn_WQ_b': _L0_attn_in['WQ_b'], 'L0_attn_WK_w': _L0_attn_in['WK_w'], 'L0_attn_WK_b': _L0_attn_in['WK_b'], 'L0_attn_WV_w': _L0_attn_in['WV_w'], 'L0_attn_WV_b': _L0_attn_in['WV_b'], 'L0_attn_Wo_w': _L0_attn_in['Wo_w'], 'L0_attn_Wo_b': _L0_attn_in['Wo_b'], 'L0_ffn_router_w': _L0_ffn_in['router_w'], 'L0_ffn_w_fc': _L0_ffn_in['w_fc'], 'L0_ffn_b_fc': _L0_ffn_in['b_fc'], 'L0_ffn_w_proj': _L0_ffn_in['w_proj'], 'L0_ffn_b_proj': _L0_ffn_in['b_proj'], 'L0_c': _L0_c, 'L0_wmod': _L0_wmod}
    _x0 = _d['L0_attn_x']
    _d['L0_attn_x'] = jax.random.normal(jax.random.fold_in(jax.random.key(seed), 1), (16, 256, 128), dtype=_x0.dtype)
    del _x0
    return _d

def reference(L0_attn_x, L0_attn_WQ_w, L0_attn_WQ_b, L0_attn_WK_w, L0_attn_WK_b, L0_attn_WV_w, L0_attn_WV_b, L0_attn_Wo_w, L0_attn_Wo_b, L0_ffn_router_w, L0_ffn_w_fc, L0_ffn_b_fc, L0_ffn_w_proj, L0_ffn_b_proj, L0_c, L0_wmod):

    def _L0_attn_ref(x, WQ_w, WQ_b, WK_w, WK_b, WV_w, WV_b, Wo_w, Wo_b):
        import jax, jax.numpy as jnp
        import numpy as np
        D_MODEL = 128
        N_HEADS = 16
        D_K = D_MODEL // N_HEADS

        def _rope_cache(T, dtype):
            half = D_K // 2
            freq = 1.0 / 10000.0 ** (2.0 * jnp.arange(half, dtype=dtype) / D_K)
            angles = jnp.arange(T, dtype=dtype)[:, None] * freq[None, :]
            return (jnp.cos(angles), jnp.sin(angles))

        def _apply_rope(x, cos, sin):
            half = x.shape[-1] // 2
            x1, x2 = (x[..., :half], x[..., half:])
            return jnp.concatenate([x1 * cos - x2 * sin, x1 * sin + x2 * cos], axis=-1)
        B, T, D = x.shape

        def proj(w, b):
            y = jnp.einsum('btd,ed->bte', x, w) + b
            return y.reshape(B, T, N_HEADS, D_K).transpose(0, 2, 1, 3)
        q = proj(WQ_w, WQ_b)
        k = proj(WK_w, WK_b)
        v = proj(WV_w, WV_b)
        cos, sin = _rope_cache(T, x.dtype)
        q = _apply_rope(q, cos, sin)
        k = _apply_rope(k, cos, sin)
        scores = jnp.einsum('bhqd,bhkd->bhqk', q, k) / jnp.sqrt(jnp.asarray(D_K, x.dtype))
        causal = jnp.tril(jnp.ones((T, T), dtype=bool))
        scores = jnp.where(causal[None, None, :, :], scores, -jnp.inf)
        attn = jax.nn.softmax(scores, axis=-1)
        out = jnp.einsum('bhqk,bhkd->bhqd', attn, v)
        out = out.transpose(0, 2, 1, 3).reshape(B, T, D)
        return jnp.einsum('btd,ed->bte', out, Wo_w) + Wo_b

    def _L0_ffn_ref(x, router_w, w_fc, b_fc, w_proj, b_proj):
        import math
        import jax, jax.numpy as jnp
        import numpy as np
        TOP_K = 2
        _GELU_C = math.sqrt(2.0 / math.pi)

        def gelu_new(x):
            return 0.5 * x * (1.0 + jnp.tanh(_GELU_C * (x + 0.044715 * x * x * x)))
        B, T, C = x.shape
        E = router_w.shape[0]
        N = B * T
        xf = x.reshape(N, C)
        logits = xf @ router_w.T
        probs = jax.nn.softmax(logits, axis=-1)
        topk_probs, topk_idx = jax.lax.top_k(probs, TOP_K)
        topk_probs = topk_probs / jnp.sum(topk_probs, axis=-1, keepdims=True)
        combine = jnp.zeros((N, E), dtype=x.dtype).at[jnp.arange(N)[:, None], topk_idx].add(topk_probs)
        h = gelu_new(jnp.einsum('nc,ech->neh', xf, w_fc) + b_fc)
        out = jnp.einsum('neh,ehc->nec', h, w_proj) + b_proj
        y = jnp.einsum('nec,ne->nc', out, combine)
        return y.reshape(B, T, C)
    x = L0_attn_x
    mod = (_silu(L0_c) @ L0_wmod).reshape(L0_c.shape[0], 6, 1, -1)
    sa, ca, ga, sb, cb, gb = (mod[:, 0], mod[:, 1], mod[:, 2], mod[:, 3], mod[:, 4], mod[:, 5])
    ga = (2 * (ga >= 0) - 1) * jnp.maximum(jnp.abs(ga), 0.25)
    gb = (2 * (gb >= 0) - 1) * jnp.maximum(jnp.abs(gb), 0.25)
    h = _layernorm(x, axis=-1) * (1 + ca) + sa
    x = x + ga * _L0_attn_ref(h, L0_attn_WQ_w, L0_attn_WQ_b, L0_attn_WK_w, L0_attn_WK_b, L0_attn_WV_w, L0_attn_WV_b, L0_attn_Wo_w, L0_attn_Wo_b)
    h = _layernorm(x, axis=-1) * (1 + cb) + sb
    x = x + gb * _L0_ffn_ref(h, L0_ffn_router_w, L0_ffn_w_fc, L0_ffn_b_fc, L0_ffn_w_proj, L0_ffn_b_proj)
    return x

_drawn_inputs = setup_inputs


def setup_inputs(seed=0):
    import zlib

    import numpy as np

    out = dict(_drawn_inputs(seed))
    spreads = {}
    factors = {'L0_attn_WQ_w': 8.0,
     'L0_attn_WQ_b': 8.0,
     'L0_attn_WK_w': 8.0,
     'L0_attn_WK_b': 8.0,
     'L0_attn_WV_w': 8.0,
     'L0_attn_WV_b': 8.0,
     'L0_attn_Wo_w': 8.0,
     'L0_attn_Wo_b': 7.085,
     'L0_ffn_b_fc': 24.527,
     'L0_ffn_b_proj': 8.0}
    for name, (base, spread) in spreads.items():
        noise = np.random.default_rng([zlib.crc32(name.encode()), seed]).standard_normal(out[name].shape)
        drawn = base * np.exp(spread * noise) if base else spread * noise
        out[name] = jnp.asarray(drawn.astype(out[name].dtype))
    for name, factor in factors.items():
        out[name] = (out[name] * factor).astype(out[name].dtype)
    return out
```

```python
from contextlib import ExitStack

import numpy as np

import concourse.bass as bass
from concourse import mybir

F32 = mybir.dt.float32
F32R = mybir.dt.float32r
BF16 = mybir.dt.bfloat16
U32 = mybir.dt.uint32
ALU = mybir.AluOpType
ACT = mybir.ActivationFunctionType
AX = mybir.AxisListType.X

B, T, D = 16, 256, 128
HEADS, DK = 16, 8
P = 128
TILES = T // P
GROUPS = HEADS // 4
ROWS = 32
PARTS = 3 * DK
EXPERTS, HID = 8, 512
HC = HID // P
CHUNK = 512
NTILES = B * TILES
EPS = 1e-5
SCALE = float(DK) ** -0.5
MASKED = -1.0e30

FIRST, LAST = 4, 14
assert (LAST - FIRST) % 2 == 0


class Step:

    def __init__(self, t, i=None, u=0):
        self.t, self.i, self.u = t, i, u

    def has(self, d):
        return 0 <= self.t + d < B

    def value(self, d, per, n):
        first = (self.t + d) * per + n
        if self.i is None:
            return first
        return self.i * (2 * per) + first

    def wait(self, eng, sem, d, per, n):
        if self.t + d >= 0:
            eng.wait_ge(sem, self.value(d, per, n))

    def slot_wait(self, eng, sems, d):
        b = self.t + d
        n = 16 * (b // 2 + 1)
        eng.wait_ge(sems[b % 2], n if self.i is None else self.i * 16 + n)

    def hold(self, eng, sem, d, per, n, passed):
        if self.t + d >= 0:
            eng.wait_ge(sem, self.value(d, per, n))
            if self.i is not None:
                eng.sem_inc(passed, 1)

    def pick(self, ap, axis, d):
        b = self.t + d
        if self.i is None:
            index = [slice(None)] * len(ap.shape)
            index[axis] = b
            return ap[tuple(index)]
        names = [f"x{n}" for n in range(len(ap.shape))]
        left = " ".join("(tt uu)" if n == axis else x for n, x in enumerate(names))
        right = " ".join("tt uu" if n == axis else x for n, x in enumerate(names))
        v = ap.rearrange(f"{left} -> {right}", uu=2)
        index = [slice(None)] * len(v.shape)
        index[axis] = bass.ds(self.i + b // 2, 1)
        index[axis + 1] = b % 2
        v = v[tuple(index)]
        names = [f"y{n}" for n in range(len(v.shape))]
        new = names[:axis] + [f"(y{axis} y{axis + 1})"] + names[axis + 2:]
        return v.rearrange(f"{' '.join(names)} -> {' '.join(new)}")


def steps(eng, emit):
    for t in range(-1, FIRST):
        emit(Step(t))
    with eng.Fori(0, (LAST - FIRST) // 2) as i:
        for u in range(2):
            emit(Step(FIRST + u, i, u))
    for t in range(LAST, B + 2):
        emit(Step(t))


MISC = [
    ("qm0", -1), ("qm1", -1), ("heads0", -2), ("heads1", -2),
    ("k0", 0), ("k1", 0), ("q0", 0), ("q1", 0),
    ("attnT", -2), ("zT", 1), ("wo", -2), ("qkv0", 1), ("qkv1", 1), ("z2T", -2), ("router", -2),
]
BANK = {name: n % 2 for n, (name, _) in enumerate(MISC)}


def before(name, s):
    at = [n for n, (x, _) in enumerate(MISC) if x == name][0]
    bank = at % 2
    for back in range(0, 3):
        for n in range(len(MISC) - 1, -1, -1):
            if n % 2 != bank or (back == 0 and n >= at):
                continue
            x, d = MISC[n]
            if 0 <= s.t - back + d < B:
                return x, d - back
    return None


def block_program(nc, x, c_t, wmod, wqkv, bqkv, wo, bo, router, w_fc, b_fc, w_proj, b_proj,
                  cos, sin, ident, causal, iota, out):
    with ExitStack() as ctx:
        def sb(name, shape, dt=F32):
            return ctx.enter_context(nc.sbuf_tensor(name, shape, dt))

        def psum(name):
            return ctx.enter_context(nc.psum_tensor(name, [P, 512], F32))

        def sem(name):
            return ctx.enter_context(nc.semaphore(name))

        ident_s = sb("ident_s", [P, P])
        ident_b = sb("ident_b", [P, P], BF16)
        causal_s = sb("causal_s", [P, 2, P])
        mask_q = sb("mask_q", [P, 2, P], BF16)
        mask_k = sb("mask_k", [P, 2, P], BF16)
        cos_s = sb("cos_s", [P, TILES, 256])
        sin_s = sb("sin_s", [P, TILES, 256])
        wqkv_s = sb("wqkv_s", [P, 384])
        bqkv_s = sb("bqkv_s", [P, 384])
        wo_s = sb("wo_s", [P, P])
        bo_s = sb("bo_s", [P, P])
        router_s = sb("router_s", [P, EXPERTS])
        wfc_s = sb("wfc_s", [P, EXPERTS, HID])
        bfc_s = sb("bfc_s", [P, EXPERTS, HC])
        wproj_s = sb("wproj_s", [P, EXPERTS, HC, P])
        bproj_s = sb("bproj_s", [P, EXPERTS, P])
        iota_s = sb("iota_s", [P, EXPERTS])
        half_s = sb("half_s", [P, TILES])
        wmod_s = sb("wmod_s", [P, 6 * D])
        c_s = sb("c_s", [P, B])
        c_exp = sb("c_exp", [P, B])
        c_den = sb("c_den", [P, B])
        c_sig = sb("c_sig", [P, B])
        c_silu = sb("c_silu", [P, B])
        mod = sb("mod", [P, B, 4])
        gate_sign = sb("gate_sign", [B, 2 * D])
        gate_neg = sb("gate_neg", [B, 2 * D])
        gate_size = sb("gate_size", [B, 2 * D])
        gate_row = sb("gate_row", [B, 2 * D])
        gates = sb("gates", [P, B, 2 * D])
        x_in = [sb(f"x_in{n}", [P, TILES, D]) for n in range(2)]
        stats = sb("stats", [P, TILES, 6])
        moments = sb("moments", [P, TILES, 2])
        var_eps = sb("var_eps", [P, TILES])
        rstd = sb("rstd", [P, TILES])
        z = sb("z", [P, TILES, D])
        h_t = sb("h_t", [P, T])
        qkv = sb("qkv", [P, TILES, 384])
        rope_a = sb("rope_a", [P, TILES, 256])
        rope_b = sb("rope_b", [P, TILES, 256])
        roped = sb("roped", [P, TILES, 256])
        q_parts = sb("q_parts", [P, TILES, HEADS, ROWS], F32R)
        k_parts = sb("k_parts", [P, TILES, HEADS, ROWS], F32R)
        v_wide = [sb(f"v_wide{n}", [P, TILES, HEADS, ROWS]) for n in range(2)]
        q_stack = sb("q_stack", [P, GROUPS, T], F32R)
        k_stack = [sb(f"k_stack{n}", [P, GROUPS, T], F32R) for n in range(2)]
        maxima = sb("maxima", [P, TILES, HEADS])
        qm_stack = sb("qm_stack", [P, GROUPS, T], F32R)
        probs = sb("probs", [P, 8, 384])
        heads_t = [sb(f"heads_t{n}", [P, GROUPS, T]) for n in range(2)]
        x_res = [sb(f"x_res{n}", [P, TILES, D]) for n in range(2)]
        rsum = sb("rsum", [P, TILES, HEADS])
        attn = sb("attn", [P, TILES, HEADS, DK])
        attn_t = sb("attn_t", [P, T])
        proj_b = sb("proj_b", [P, TILES, D])
        proj_g = sb("proj_g", [P, TILES, D])
        x1_now = sb("x1_now", [P, TILES, D])
        x1 = sb("x1", [P, B, TILES, D])
        stats2 = sb("stats2", [P, TILES, 6])
        moments2 = sb("moments2", [P, TILES, 2])
        var_eps2 = sb("var_eps2", [P, TILES])
        rstd2 = sb("rstd2", [P, TILES])
        z2 = sb("z2", [P, TILES, D])
        h2_now = sb("h2_now", [P, T])
        h2_t = sb("h2_t", [P, B, T])
        logits = sb("logits", [P, B, TILES * EXPERTS])
        top = sb("top", [P, NTILES, 8])
        top_at = sb("top_at", [P, NTILES, 8], U32)
        top_f = sb("top_f", [P, NTILES, 2])
        gap = sb("gap", [P, NTILES])
        gap_exp = sb("gap_exp", [P, NTILES])
        gap_den = sb("gap_den", [P, NTILES])
        share = sb("share", [P, 2, NTILES])
        hot = sb("hot", [P, 2, NTILES, EXPERTS])
        hot_w = sb("hot_w", [P, 2, NTILES, EXPERTS])
        combine = sb("combine", [P, NTILES, EXPERTS])
        act = sb("act", [P, 4, CHUNK])
        y = sb("y", [P, 2, CHUNK // P, D])

        misc = [psum(f"misc{n}") for n in range(2)]
        ps_max = [psum(f"ps_max{n}") for n in range(2)]
        ps_sc = [psum(f"ps_sc{n}") for n in range(2)]
        ps_pv = [psum(f"ps_pv{n}") for n in range(2)]

        gate_dram = nc.dram_tensor("gate_rows", [B, 2 * D], F32).ap()

        names = """loaded_a loaded_b loaded_c loaded_w gate_out gate_in written zeroed
        masks_ready c_exp_done c_den_done c_sig_done silu_done mod_mm gate_mm mod_done sign_done neg_done size_done gate_done
        stats_done moments_done eps_done rstd_done z_done zt_done ht_done qkv_mm qkv_done
        rope_done roped_done q_high k_high q_low k_low k_tr q_tr k_stacked q_stacked v_done
        max_mm max_done shift_high shifts_done qm_tr qm_stacked score_mm exp_done pv_mm heads_done
        heads_tr rsum_done attn_done attn_tr attn_t_done wo_mm wo_bias wo_gated x1_done x1_kept dve_passed pool_passed
        stats2_done moments2_done eps2_done rstd2_done z2_done z2_tr h2_done h2_kept router_mm logits_done
        top_done at_done gap_done gap_exp_done gap_den_done share_done hot_done hotw_done combine_done
        up_mm gelu_done down_mm y_done yg_done y_ready""".split()
        S = {n: sem(n) for n in names}
        x_loaded = [sem(f"x_loaded{n}") for n in range(2)]
        xres_loaded = [sem(f"xres_loaded{n}") for n in range(2)]

        freed = {
            "qm0": ("qm_stacked", 2, 1), "qm1": ("qm_stacked", 2, 2),
            "heads0": ("attn_done", 2, 1), "heads1": ("attn_done", 2, 2),
            "k0": ("k_stacked", 2, 1), "k1": ("k_stacked", 2, 2),
            "q0": ("q_stacked", 2, 1), "q1": ("q_stacked", 2, 2),
            "attnT": ("attn_t_done", 1, 1), "zT": ("ht_done", 1, 1), "wo": ("wo_bias", 1, 1),
            "qkv0": ("qkv_done", 2, 1), "qkv1": ("qkv_done", 2, 2),
            "z2T": ("h2_done", 1, 1), "router": ("logits_done", 1, 1),
        }

        block = ctx.enter_context(nc.Block())

        x_v = x.rearrange("b (a p) d -> b p a d", p=P)
        out_v = out.rearrange("b (a p) d -> p b a d", p=P)

        @block.sync
        def _(sp):
            for dst, src in ((c_s[:], c_t), (wmod_s[:], wmod)):
                sp.dma_start(dst, src).then_inc(S["loaded_a"], 16)
            sp.dma_start(ident_s[:], ident).then_inc(S["loaded_b"], 16)
            for dst, src in (
                (causal_s[:], causal), (wqkv_s[:], wqkv), (bqkv_s[:], bqkv.broadcast_to([P, 384])),
                (cos_s[:], cos), (sin_s[:], sin),
            ):
                sp.dma_start(dst, src).then_inc(S["loaded_b"], 16)

            def emit(s):
                if s.has(2):
                    s.wait(sp, S["z_done"], 0, 2, 2)
                    sp.dma_start(x_in[s.t % 2][:], s.pick(x_v, 0, 2)).then_inc(x_loaded[s.t % 2], 16)
                if s.has(-1):
                    s.wait(sp, S["x1_done"], -3, 1, 1)
                    sp.dma_start(x_res[(s.t - 1) % 2][:], s.pick(x_v, 0, -1)).then_inc(xres_loaded[(s.t - 1) % 2], 16)

            sp.dma_start(x_in[0][:], x_v[0]).then_inc(x_loaded[0], 16)
            for dst, src in ((wo_s[:], wo), (bo_s[:], bo.broadcast_to([P, D])), (router_s[:], router)):
                sp.dma_start(dst, src).then_inc(S["loaded_w"], 16)
            sp.wait_ge(S["gate_done"], 1)
            sp.dma_start(gate_dram, gate_row[:]).then_inc(S["gate_out"], 16)
            sp.wait_ge(S["gate_out"], 16)
            sp.dma_start(gates[:].rearrange("p b d -> p (b d)"),
                         gate_dram.rearrange("(o b) d -> o (b d)", o=1).broadcast_to([P, B * 2 * D])
                         ).then_inc(S["gate_in"], 16)
            for dst, src in (
                (wfc_s[:], w_fc), (bfc_s[:], b_fc), (wproj_s[:], w_proj), (iota_s[:], iota.broadcast_to([P, EXPERTS])),
                (bproj_s[:].rearrange("p e d -> p (e d)"), b_proj.broadcast_to([P, EXPERTS * D])),
            ):
                sp.dma_start(dst, src).then_inc(S["loaded_c"], 16)
            steps(sp, emit)
            n = CHUNK // T
            with sp.Fori(0, B // n // 2) as i:
                for u in range(2):
                    sp.wait_ge(S["y_ready"], i * 2 + (u + 1))
                    dst = out_v.rearrange("p (i u b) a d -> p i u (b a) d", u=2, b=n)
                    done = x1[:].rearrange("p (i k) a d -> p i (k a) d", k=2 * n)[:, bass.ds(i, 1), u * n * TILES:(u + 1) * n * TILES]
                    done = done.rearrange("p i t d -> p (i t) d")
                    sp.dma_start(dst[:, bass.ds(i, 1), u].rearrange("p i t d -> p (i t) d"),
                                 done).then_inc(S["written"], 16)
            sp.wait_ge(S["written"], 16 * B // n)

        @block.gpsimd
        def _(pool):
            for n, (t, v) in enumerate((
                (k_parts[:].bitcast(F32), 0.0), (q_parts[:].bitcast(F32), 0.0), (v_wide[0][:], 0.0), (v_wide[1][:], 0.0),
            )):
                nc.gpsimd.memset(t, v).then_inc(S["zeroed"], 1)
            nc.gpsimd.memset(half_s[:], -0.5).then_inc(S["zeroed"], 1)
            pool.wait_ge(S["zeroed"], 5)
            nc.gpsimd.memset(k_parts[:, :, :, PARTS:PARTS + 2].bitcast(F32), 1.0).then_inc(S["zeroed"], 1)
            nc.gpsimd.memset(v_wide[0][:, :, :, DK:DK + 1], 1.0).then_inc(S["zeroed"], 1)
            nc.gpsimd.memset(v_wide[1][:, :, :, DK:DK + 1], 1.0).then_inc(S["zeroed"], 1)
            pool.wait_ge(S["zeroed"], 8)

            def emit(s):
                if s.has(0):
                    s.wait(pool, S["qkv_done"], 0, 2, 2)
                    s.hold(pool, S["pv_mm"], -2, 4, 4, S["pool_passed"])
                    if s.t < 2:
                        pool.wait_ge(S["zeroed"], 8)
                    nc.gpsimd.tensor_copy(
                        v_wide[s.t % 2][:, :, :, 0:DK],
                        qkv[:, :, 256:384].rearrange("p a (h d) -> p a h d", h=HEADS)).then_inc(S["v_done"], 1)
                if s.has(1):
                    s.hold(pool, S["moments_done"], 1, 2, 2, S["pool_passed"])
                    nc.gpsimd.tensor_scalar_add(var_eps[:], moments[:, :, 1], EPS).then_inc(S["eps_done"], 1)
                    s.wait(pool, S["eps_done"], 1, 1, 1)
                    s.wait(pool, S["z_done"], 0, 2, 2)
                    nc.gpsimd.tensor_tensor(rstd[:], var_eps[:], half_s[:], ALU.pow).then_inc(S["rstd_done"], 1)
                if s.has(-2):
                    s.hold(pool, S["x1_done"], -2, 1, 1, S["pool_passed"])
                    nc.gpsimd.tensor_copy(s.pick(x1[:], 1, -2), x1_now[:]).then_inc(S["x1_kept"], 1)
                    s.hold(pool, S["moments2_done"], -2, 2, 2, S["pool_passed"])
                    nc.gpsimd.tensor_scalar_add(var_eps2[:], moments2[:, :, 1], EPS).then_inc(S["eps2_done"], 1)
                    s.wait(pool, S["eps2_done"], -2, 1, 1)
                    s.wait(pool, S["z2_done"], -3, 2, 2)
                    nc.gpsimd.tensor_tensor(rstd2[:], var_eps2[:], half_s[:], ALU.pow).then_inc(S["rstd2_done"], 1)
                if s.has(-2):
                    s.hold(pool, S["h2_done"], -2, 1, 1, S["pool_passed"])
                    nc.gpsimd.tensor_copy(s.pick(h2_t[:], 1, -2), h2_now[:]).then_inc(S["h2_kept"], 1)

            steps(pool, emit)

        @block.scalar
        def _(act_e):
            act_e.wait_ge(S["loaded_a"], 32)
            nc.scalar.activation(c_exp[:], c_s[:], ACT.Exp, scale=-1.0).then_inc(S["c_exp_done"], 1)

            def emit(s):
                if s.has(-1):
                    for n in range(2):
                        s.wait(act_e, S["qm_tr"], -1, 2, n + 1)
                        if n == 0:
                            s.wait(act_e, S["score_mm"], -2, 16, 16)
                        nc.scalar.activation(qm_stack[:, 2 * n:2 * n + 2, :].rearrange("p g t -> p (g t)"),
                                             misc[BANK[f"qm{n}"]][:], ACT.Copy).then_inc(S["qm_stacked"], 1)
                if s.has(0):
                    s.wait(act_e, S["roped_done"], 0, 1, 1)
                    for which, parts, slots, name, old, per in (
                        (0, q_parts, (0, 1), "q_high", "qm_tr", 2), (1, k_parts, (0, 2), "k_high", "k_tr", 2),
                    ):
                        s.wait(act_e, S[old], -1, per, per)
                        if s.t == 0:
                            act_e.wait_ge(S["zeroed"], 8)
                        src = roped[:].rearrange("p a (w h d) -> p a w h d", w=2, h=HEADS)[:, :, which]
                        for m, slot in enumerate(slots):
                            ins = nc.scalar.activation(parts[:, :, :, slot * DK:(slot + 1) * DK], src, ACT.Copy)
                            ins.then_inc(S[name], 1)

                def exp(h):
                    s.wait(act_e, S["score_mm"], -1, 16, h + 1)
                    if h >= 8:
                        s.wait(act_e, S["pv_mm"], -1, 4, h // 4 - 1)
                    else:
                        s.wait(act_e, S["pv_mm"], -2, 4, h // 4 + 3)
                    nc.scalar.activation(probs[:, h % 8, :], ps_sc[h % 2][:, 0:384], ACT.Exp,
                                         scale=SCALE).then_inc(S["exp_done"], 1)

                def heads_out(g):
                    s.wait(act_e, S["pv_mm"], -1, 4, g + 1)
                    s.wait(act_e, S["heads_tr"], -3, 2, 2)
                    nc.scalar.activation(heads_t[(s.t - 1) % 2][:, g, :], ps_pv[g % 2][:, 0:T],
                                         ACT.Copy).then_inc(S["heads_done"], 1)

                def stack(which, n):
                    s.wait(act_e, S[f"{which}_tr"], 0, 2, n + 1)
                    dst = k_stack[s.t % 2] if which == "k" else q_stack
                    if n == 0 and which == "k":
                        s.wait(act_e, S["score_mm"], -2, 16, 16)
                    if n == 0 and which == "q":
                        s.wait(act_e, S["max_mm"], -1, 8, 8)
                    nc.scalar.activation(dst[:, 2 * n:2 * n + 2, :].rearrange("p g t -> p (g t)"),
                                         misc[BANK[f"{which}{n}"]][:], ACT.Copy).then_inc(S[f"{which}_stacked"], 1)

                for h in range(HEADS):
                    if s.has(-1):
                        exp(h)
                        if h % 4 == 1 and h > 4:
                            heads_out(h // 4 - 1)
                    if s.has(0) and 4 <= h < 8:
                        stack("kkqq"[h - 4], h % 2)
                    if h == 8 and s.has(-2):
                        s.wait(act_e, S["attn_tr"], -2, 1, 1)
                        s.wait(act_e, S["wo_mm"], -3, 1, 1)
                        nc.scalar.activation(attn_t[:], misc[BANK["attnT"]][:, 0:T], ACT.Copy).then_inc(S["attn_t_done"], 1)
                    if h == 9 and s.has(1):
                        s.wait(act_e, S["zt_done"], 1, 1, 1)
                        s.wait(act_e, S["qkv_mm"], 0, 2, 2)
                        if s.t == -1:
                            act_e.wait_ge(S["mod_done"], 4)
                        m = s.pick(mod[:], 1, 1)
                        nc.scalar.activation(h_t[:], misc[BANK["zT"]][:, 0:T], ACT.Identity,
                                             bias=m[:, 0:1], scale=m[:, 1:2]).then_inc(S["ht_done"], 1)
                    if h == 14 and s.has(-2):
                        s.wait(act_e, S["z2_tr"], -2, 1, 1)
                        s.wait(act_e, S["router_mm"], -3, 1, 1)
                        s.wait(act_e, S["h2_kept"], -3, 1, 1)
                        m = s.pick(mod[:], 1, -2)
                        nc.scalar.activation(h2_now[:], misc[BANK["z2T"]][:, 0:T], ACT.Identity,
                                             bias=m[:, 2:3], scale=m[:, 3:4]).then_inc(S["h2_done"], 1)
                if s.has(-1):
                    heads_out(3)

            steps(act_e, emit)
            act_e.wait_ge(S["gap_done"], 1)
            nc.scalar.activation(gap_exp[:], gap[:], ACT.Exp).then_inc(S["gap_exp_done"], 1)
            n = CHUNK // T
            act_e.wait_ge(S["loaded_c"], 80)
            with act_e.Fori(0, B // n) as i:
                for e in range(EXPERTS):
                    for hc in range(HC):
                        k = e * HC + hc
                        act_e.wait_ge(S["up_mm"], i * (EXPERTS * HC) + (k + 1))
                        act_e.wait_ge(S["down_mm"], i * (EXPERTS * HC) + (k + 1))
                        nc.scalar.activation(act[:, k % 4, :], ps_sc[k % 2][:], ACT.Gelu_apprx_tanh,
                                             bias=bfc_s[:, e, hc:hc + 1]).then_inc(S["gelu_done"], 1)

        @block.vector
        def _(dve):
            dve.wait_ge(S["loaded_b"], 96)
            for n in range(2):
                nc.vector.tensor_copy(mask_q[:, n, :], causal_s[:, 0, :]).then_inc(S["masks_ready"], 1)
                nc.vector.tensor_copy(mask_k[:, n, :], causal_s[:, 1, :]).then_inc(S["masks_ready"], 1)
            nc.vector.tensor_copy(ident_b[:], ident_s[:]).then_inc(S["masks_ready"], 1)
            dve.wait_ge(S["c_exp_done"], 1)
            nc.vector.tensor_scalar_add(c_den[:], c_exp[:], 1.0).then_inc(S["c_den_done"], 1)
            dve.wait_ge(S["c_den_done"], 1)
            nc.vector.reciprocal(c_sig[:], c_den[:]).then_inc(S["c_sig_done"], 1)
            dve.wait_ge(S["c_sig_done"], 1)
            nc.vector.tensor_tensor(c_silu[:], c_s[:], c_sig[:], ALU.mult).then_inc(S["silu_done"], 1)
            dve.wait_ge(S["mod_mm"], 1)
            for n in range(4):
                nc.vector.tensor_scalar_add(mod[:, :, n], ps_max[0][:, n * B:(n + 1) * B],
                                            float(n % 2)).then_inc(S["mod_done"], 1)
            dve.wait_ge(S["gate_mm"], 1)
            g = ps_max[1][0:B, 0:2 * D]
            nc.vector.tensor_scalar(gate_sign[:], g, 0.0, 2.0, ALU.is_ge, ALU.mult).then_inc(S["sign_done"], 1)
            nc.vector.tensor_scalar(gate_neg[:], g, -1.0, 0.25, ALU.mult, ALU.max).then_inc(S["neg_done"], 1)
            dve.wait_ge(S["neg_done"], 1)
            nc.vector.tensor_tensor(gate_size[:], g, gate_neg[:], ALU.max).then_inc(S["size_done"], 1)
            dve.wait_ge(S["sign_done"], 1)
            dve.wait_ge(S["size_done"], 1)
            nc.vector.scalar_tensor_tensor(out=gate_row[:], in0=gate_sign[:], scalar=-1.0, in1=gate_size[:],
                                           op0=ALU.add, op1=ALU.mult).then_inc(S["gate_done"], 1)

            def norm(s, d, src, st, mo, rs, zz, names, readers):
                sd, md, rd, zd = names
                for a in range(TILES):
                    nc.vector.bn_stats(st[:, a, :], src[:, a, :]).then_inc(S[sd], 1)
                s.hold(dve, S[sd], d, 2, 2, S["dve_passed"])
                for a in range(TILES):
                    nc.vector.bn_aggr(mo[:, a, :], st[:, a, :]).then_inc(S[md], 1)
                s.wait(dve, S[rd], d, 1, 1)
                s.wait(dve, S[readers], d - 1, 1, 1)
                for a in range(TILES):
                    nc.vector.tensor_scalar(zz[:, a, :], src[:, a, :], mo[:, a, 0:1], rs[:, a:a + 1],
                                            ALU.subtract, ALU.mult).then_inc(S[zd], 1)

            def emit(s):
                if s.has(0):
                    s.wait(dve, S["qkv_done"], 0, 2, 2)
                    qk = qkv[:, :, 0:256]
                    nc.vector.tensor_tensor(rope_a[:], qk, cos_s[:], ALU.mult).then_inc(S["rope_done"], 1)
                    for n in range(2):
                        def half(t, m):
                            v = t if len(t.shape) == 3 else t[:]
                            return v.rearrange("p a (g f i) -> p a g f i", f=2, i=4)[:, :, :, m, :]
                        for a in range(TILES):
                            nc.vector.tensor_tensor(half(rope_b[:], n)[:, a], half(qk, 1 - n)[:, a], half(sin_s[:], n)[:, a],
                                                    ALU.mult).then_inc(S["rope_done"], 1)
                    s.wait(dve, S["rope_done"], 0, 5, 5)
                    s.wait(dve, S["k_high"], -1, 2, 2)
                    nc.vector.tensor_tensor(roped[:], rope_a[:], rope_b[:], ALU.add).then_inc(S["roped_done"], 1)
                    for which, parts, of, to, high, low in (
                        (0, q_parts, 0, 2, "q_high", "q_low"), (1, k_parts, 0, 1, "k_high", "k_low"),
                    ):
                        s.wait(dve, S[high], 0, 2, 2)
                        src = roped[:].rearrange("p a (w h d) -> p a w h d", w=2, h=HEADS)[:, :, which]
                        nc.vector.tensor_tensor(parts[:, :, :, to * DK:(to + 1) * DK], src,
                                                parts[:, :, :, of * DK:(of + 1) * DK].bitcast(F32),
                                                ALU.subtract).then_inc(S[low], 1)
                if s.has(-2):
                    for a in range(TILES):
                        s.wait(dve, S["heads_tr"], -2, 2, a + 1)
                        m = misc[BANK[f"heads{a}"]][:].rearrange("p (h r) -> p h r", h=HEADS)
                        nc.vector.reciprocal(rsum[:, a, :], m[:, :, DK]).then_inc(S["rsum_done"], 1)
                        s.wait(dve, S["rsum_done"], -2, 2, a + 1)
                        if a == 0:
                            s.wait(dve, S["attn_tr"], -3, 1, 1)
                        nc.vector.tensor_tensor(attn[:, a], m[:, :, 0:DK],
                                                rsum[:, a, :].rearrange("p (h o) -> p h o", o=1).broadcast_to([P, HEADS, DK]),
                                                ALU.mult).then_inc(S["attn_done"], 1)

                def maxima_of(n):
                    s.wait(dve, S["max_mm"], 0, 8, n + 1)
                    for w in range(2):
                        h = 2 * n + w
                        nc.vector.tensor_reduce(maxima[:, 0, h:h + 1], ps_max[w][:, 0:128], AX, ALU.max)
                        ins = nc.vector.tensor_reduce(maxima[:, 1, h:h + 1], ps_max[w][:, 128:384], AX, ALU.max)
                    ins.then_inc(S["max_done"], 1)

                if s.has(1):
                    s.slot_wait(dve, x_loaded, 1)
                    norm(s, 1, x_in[(s.t + 1) % 2], stats, moments, rstd, z,
                         ("stats_done", "moments_done", "rstd_done", "z_done"), "zt_done")
                for n in range(8):
                    if s.has(0):
                        maxima_of(n)
                    if n == 1 and s.has(-2):
                        s.wait(dve, S["wo_mm"], -2, 1, 1)
                        if s.t - 2 == 0:
                            dve.wait_ge(S["loaded_w"], 48)
                            dve.wait_ge(S["gate_in"], 16)
                        bias = bo_s[:].rearrange("p (o d) -> p o d", o=1).broadcast_to([P, TILES, D])
                        gate = s.pick(gates[:], 1, -2)[:, 0:D].rearrange("p (o d) -> p o d", o=1).broadcast_to([P, TILES, D])
                        nc.vector.tensor_tensor(proj_b[:], misc[BANK["wo"]][:, 0:T].rearrange("p (a d) -> p a d", a=TILES),
                                                bias, ALU.add).then_inc(S["wo_bias"], 1)
                        s.wait(dve, S["wo_bias"], -2, 1, 1)
                        nc.vector.tensor_tensor(proj_g[:], proj_b[:], gate, ALU.mult).then_inc(S["wo_gated"], 1)
                        s.wait(dve, S["wo_gated"], -2, 1, 1)
                        s.slot_wait(dve, xres_loaded, -2)
                        row = x1_now[:]
                        s.wait(dve, S["x1_kept"], -3, 1, 1)
                        nc.vector.tensor_tensor(row, proj_g[:], x_res[s.t % 2][:], ALU.add).then_inc(S["x1_done"], 1)
                        s.wait(dve, S["x1_done"], -2, 1, 1)
                        norm(s, -2, row, stats2, moments2, rstd2, z2,
                             ("stats2_done", "moments2_done", "rstd2_done", "z2_done"), "z2_tr")
                    if n in (4, 5) and s.has(1):
                        a = n - 4
                        s.wait(dve, S["qkv_mm"], 1, 2, a + 1)
                        s.wait(dve, S["v_done"], 0, 1, 1)
                        nc.vector.tensor_tensor(qkv[:, a, :], misc[BANK[f"qkv{a}"]][:, 0:384], bqkv_s[:],
                                                ALU.add).then_inc(S["qkv_done"], 1)
                if s.has(0):
                    s.wait(dve, S["max_done"], 0, 8, 8)
                    m = maxima[:].rearrange("p a (h o) -> p (a h) o", o=1)
                    v = q_parts[:].rearrange("p a h r -> p (a h) r")
                    nc.vector.tensor_scalar(v[:, :, PARTS:PARTS + 1], m, -1.0, None, ALU.mult).then_inc(S["shift_high"], 1)
                    s.wait(dve, S["shift_high"], 0, 1, 1)
                    nc.vector.scalar_tensor_tensor(out=v[:, :, PARTS + 1:PARTS + 2], in0=m, scalar=-1.0,
                                                   in1=v[:, :, PARTS:PARTS + 1].bitcast(F32),
                                                   op0=ALU.mult, op1=ALU.subtract).then_inc(S["shifts_done"], 1)
                if s.has(-2):
                    s.wait(dve, S["router_mm"], -2, 1, 1)
                    nc.vector.tensor_copy(s.pick(logits[:], 1, -2),
                                          misc[BANK["router"]][:, 0:TILES * EXPERTS]).then_inc(S["logits_done"], 1)

            steps(dve, emit)

            dve.wait_ge(S["logits_done"], B)
            lg = logits[:].rearrange("p b (a e) -> p (b a) e", a=TILES)
            for n in range(NTILES):
                nc.vector.max(top[:, n, :], lg[:, n, :]).then_inc(S["top_done"], 1)
            dve.wait_ge(S["top_done"], NTILES)
            nc.vector.tensor_tensor(gap[:], top[:, :, 1], top[:, :, 0], ALU.subtract).then_inc(S["gap_done"], 1)
            for n in range(NTILES):
                nc.vector.max_index(top_at[:, n, :], top[:, n, :], lg[:, n, :]).then_inc(S["at_done"], 1)
            dve.wait_ge(S["at_done"], NTILES)
            nc.vector.tensor_copy(top_f[:], top_at[:, :, 0:2]).then_inc(S["at_done"], 1)
            dve.wait_ge(S["gap_exp_done"], 1)
            nc.vector.tensor_scalar_add(gap_den[:], gap_exp[:], 1.0).then_inc(S["gap_den_done"], 1)
            dve.wait_ge(S["gap_den_done"], 1)
            nc.vector.reciprocal(share[:, 0, :], gap_den[:]).then_inc(S["share_done"], 1)
            dve.wait_ge(S["share_done"], 1)
            nc.vector.tensor_tensor(share[:, 1, :], share[:, 0, :], gap_exp[:], ALU.mult).then_inc(S["share_done"], 1)
            dve.wait_ge(S["loaded_c"], 80)
            dve.wait_ge(S["at_done"], NTILES + 1)
            dve.wait_ge(S["share_done"], 2)
            wide = [P, NTILES, EXPERTS]
            for k in range(2):
                nc.vector.tensor_tensor(hot[:, k], iota_s[:].rearrange("p (o e) -> p o e", o=1).broadcast_to(wide),
                                        top_f[:, :, k:k + 1].broadcast_to(wide), ALU.is_equal).then_inc(S["hot_done"], 1)
                dve.wait_ge(S["hot_done"], k + 1)
                nc.vector.tensor_tensor(hot_w[:, k], hot[:, k],
                                        share[:, k, :].rearrange("p (n o) -> p n o", o=1).broadcast_to(wide),
                                        ALU.mult).then_inc(S["hotw_done"], 1)
            dve.wait_ge(S["hotw_done"], 2)
            nc.vector.tensor_tensor(combine[:], hot_w[:, 0], hot_w[:, 1], ALU.add).then_inc(S["combine_done"], 1)
            dve.wait_ge(S["combine_done"], 1)

            n = CHUNK // T
            tt = CHUNK // P
            with dve.Fori(0, B // n // 2) as i:
                for u in range(2):
                    com = combine[:].rearrange("p (i u t) e -> p i u t e", u=2, t=tt)[:, bass.ds(i, 1), u]
                    com = com.rearrange("p i t e -> p (i t) e")
                    made = 0
                    total = tt * (2 * EXPERTS)
                    for e in range(EXPERTS):
                        for t in range(tt):
                            if e == 0:
                                ins = nc.vector.tensor_scalar(y[:, u, t, :], bproj_s[:, e, :], com[:, t, e:e + 1], None, ALU.mult)
                            else:
                                dve.wait_ge(S["y_done"], i * (2 * total) + (u * total + made - tt + 1))
                                ins = nc.vector.scalar_tensor_tensor(
                                    out=y[:, u, t, :], in0=bproj_s[:, e, :], scalar=com[:, t, e:e + 1],
                                    in1=y[:, u, t, :], op0=ALU.mult, op1=ALU.add)
                            ins.then_inc(S["y_done"], 1)
                            made += 1
                        dve.wait_ge(S["down_mm"], i * (2 * EXPERTS * HC) + (u * EXPERTS * HC + (e + 1) * HC + 4))
                        for t in range(tt):
                            dve.wait_ge(S["y_done"], i * (2 * total) + (u * total + made - tt + 1))
                            nc.vector.scalar_tensor_tensor(
                                out=y[:, u, t, :], in0=ps_pv[e % 2][:, t * D:(t + 1) * D], scalar=com[:, t, e:e + 1],
                                in1=y[:, u, t, :], op0=ALU.mult, op1=ALU.add).then_inc(S["y_done"], 1)
                            made += 1
                    dve.wait_ge(S["y_done"], i * (2 * total) + (u * total + total))
                    for b in range(n):
                        k = u * n + b
                        gate = gates[:].rearrange("p (i k) d -> p i k d", k=2 * n)[:, bass.ds(i, 1), k, D:2 * D]
                        nc.vector.tensor_tensor(y[:, u, b * TILES:(b + 1) * TILES, :], y[:, u, b * TILES:(b + 1) * TILES, :],
                                                gate.broadcast_to([P, TILES, D]), ALU.mult).then_inc(S["yg_done"], 1)
                    dve.wait_ge(S["yg_done"], i * (2 * n) + (u * n + n))
                    res = x1[:].rearrange("p (i k) a d -> p i k (a d)", k=2 * n)[:, bass.ds(i, 1), u * n:(u + 1) * n]
                    res = res.rearrange("p i k d -> p (i k d)")
                    nc.vector.tensor_tensor(res, y[:, u].rearrange("p t d -> p (t d)"), res, ALU.add).then_inc(S["y_ready"], 1)

        @block.tensor
        def _(pe):
            def take(name, s):
                prev = before(name, s)
                if prev:
                    who, d = prev
                    sem_name, per, k = freed[who]
                    s.wait(pe, S[sem_name], d, per, k)
                return misc[BANK[name]]

            pe.wait_ge(S["silu_done"], 1)
            for n, j in enumerate((0, 1, 3, 4)):
                last = nc.tensor.matmul(ps_max[0][:, n * B:(n + 1) * B], wmod_s[:, j * D:(j + 1) * D], c_silu[:],
                                        start=True, stop=True)
            last.then_inc(S["mod_mm"], 1)
            for n, j in enumerate((2, 5)):
                last = nc.tensor.matmul(ps_max[1][0:B, n * D:(n + 1) * D], c_silu[:], wmod_s[:, j * D:(j + 1) * D],
                                        start=True, stop=True)
            last.then_inc(S["gate_mm"], 1)
            pe.wait_ge(S["masks_ready"], 5)
            pe.wait_ge(S["zeroed"], 8)

            def emit(s):
                def spread(which, n, parts, sem_name, d):
                    bank = take(f"{which}{n}", s)
                    for g in range(2):
                        for a in range(TILES):
                            src = parts[:, a, 4 * (2 * n + g):4 * (2 * n + g) + 4, :].rearrange("p h r -> p (h r)").bitcast(F32)
                            last = nc.tensor.transpose(bank[:, g * T + a * P:g * T + (a + 1) * P], src, ident_s[:])
                    last.then_inc(S[sem_name], 1)

                def scores_for_max(n):
                    if n == 0:
                        s.wait(pe, S["max_done"], -1, 8, 8)
                        if s.t == 0:
                            pe.wait_ge(S["mod_done"], 4)
                            pe.wait_ge(S["size_done"], 1)
                    else:
                        s.wait(pe, S["max_done"], 0, 8, n)
                    if n == 0:
                        s.wait(pe, S["k_stacked"], 0, 2, 2)
                        s.wait(pe, S["q_stacked"], 0, 2, 2)
                    g = n // 2
                    for w in range(2):
                        r = ROWS * (2 * (n % 2) + w)
                        rows = slice(r, r + PARTS)
                        ks = k_stack[s.t % 2][rows, g, :]
                        bank = ps_max[w]
                        lo = bank[:].rearrange("p (c k) -> p c k", k=P)
                        nc.tensor.matmul(lo[:, 0:4:3, :], q_stack[rows, g, 0:P], ks.rearrange("p (c k) -> p c k", k=P),
                                         start=True, stop=False, skip_group_check=True)
                        nc.tensor.matmul(bank[:, P:3 * P], q_stack[rows, g, P:2 * P], ks,
                                         start=False, stop=False, skip_group_check=True)
                        last = nc.tensor.matmul(lo[:, 0:4:2, :], ident_b[:], mask_q[:],
                                                start=False, stop=True, skip_group_check=True)
                    last.then_inc(S["max_mm"], 1)

                def scores(h):
                    if h == 0:
                        s.wait(pe, S["qm_stacked"], -1, 2, 2)
                    if h >= 2:
                        s.wait(pe, S["exp_done"], -1, 16, h - 1)
                    else:
                        s.wait(pe, S["exp_done"], -2, 16, 15 + h)
                    g = h // 4
                    r = ROWS * (h % 4)
                    rows = slice(r, r + PARTS + 2)
                    ks = k_stack[(s.t - 1) % 2]
                    bank = ps_sc[h % 2]
                    nc.tensor.matmul(bank[:, 0:T], ks[rows, g, 0:P], qm_stack[rows, g, :],
                                     start=True, stop=False, skip_group_check=True)
                    late = qm_stack[rows, g, P:2 * P].rearrange("p (o q) -> p o q", o=1).broadcast_to([PARTS + 2, 2, P])
                    nc.tensor.matmul(bank[:, T:2 * T].rearrange("p (c k) -> p c k", k=P), ks[rows, g, P:2 * P], late,
                                     start=False, stop=False, skip_group_check=True)
                    nc.tensor.matmul(bank[:].rearrange("p (c k) -> p c k", k=P)[:, 0:4:2, :], ident_b[:], mask_k[:],
                                     start=False, stop=True, skip_group_check=True).then_inc(S["score_mm"], 1)

                def weigh(g):
                    s.wait(pe, S["exp_done"], -1, 16, 4 * g + 4)
                    if g == 0:
                        s.wait(pe, S["v_done"], -1, 1, 1)
                    if g >= 2:
                        s.wait(pe, S["heads_done"], -1, 4, g - 1)
                    else:
                        s.wait(pe, S["heads_done"], -2, 4, g + 3)
                    vw = v_wide[(s.t - 1) % 2]
                    for a in range(TILES):
                        for w in range(4):
                            h = 4 * g + w
                            rows = slice(ROWS * w, ROWS * (w + 1))
                            last = nc.tensor.matmul(
                                ps_pv[g % 2][rows, a * P:T], vw[:, a, h, :],
                                probs[:, h % 8, 0:T] if a == 0 else probs[:, h % 8, T:T + P],
                                start=(a == 0), stop=(a == 1), skip_group_check=True)
                    last.then_inc(S["pv_mm"], 1)

                if s.has(-1):
                    s.wait(pe, S["shifts_done"], -1, 1, 1)
                    for n in range(2):
                        spread("qm", n, q_parts, "qm_tr", -1)
                for h in range(HEADS):
                    if s.has(-1):
                        scores(h)
                        if h % 4 == 0 and h:
                            weigh(h // 4 - 1)
                    if h in (1, 2) and s.has(-2):
                        a = h - 1
                        if a == 0:
                            s.wait(pe, S["heads_done"], -2, 4, 4)
                        bank = take(f"heads{a}", s)
                        for g in range(GROUPS):
                            last = nc.tensor.transpose(bank[:, g * P:(g + 1) * P],
                                                       heads_t[s.t % 2][:, g, a * P:(a + 1) * P], ident_s[:])
                        last.then_inc(S["heads_tr"], 1)
                    if 4 <= h < 8 and s.has(0):
                        which = "kkqq"[h - 4]
                        if h == 4:
                            s.wait(pe, S["k_low"], 0, 1, 1)
                        if h == 6:
                            s.wait(pe, S["q_low"], 0, 1, 1)
                        spread(which, h % 2, k_parts if which == "k" else q_parts, f"{which}_tr", 0)
                    if h == 8 and s.has(-2):
                        s.wait(pe, S["attn_done"], -2, 2, 2)
                        bank = take("attnT", s)
                        for a in range(TILES):
                            last = nc.tensor.transpose(bank[:, a * P:(a + 1) * P],
                                                       attn[:, a].rearrange("p h d -> p (h d)"), ident_s[:])
                        last.then_inc(S["attn_tr"], 1)
                    if h == 9 and s.has(1):
                        s.wait(pe, S["z_done"], 1, 2, 2)
                        bank = take("zT", s)
                        for a in range(TILES):
                            last = nc.tensor.transpose(bank[:, a * P:(a + 1) * P], z[:, a, :], ident_s[:])
                        last.then_inc(S["zt_done"], 1)
                    if h == 10 and s.has(-2):
                        s.wait(pe, S["attn_t_done"], -2, 1, 1)
                        bank = take("wo", s)
                        if s.t - 2 == 0:
                            pe.wait_ge(S["loaded_w"], 48)
                        for a in range(TILES):
                            last = nc.tensor.matmul(bank[:, a * D:(a + 1) * D], attn_t[:, a * P:(a + 1) * P], wo_s[:],
                                                    start=True, stop=True)
                        last.then_inc(S["wo_mm"], 1)
                    if h in (11, 12) and s.has(1):
                        a = h - 11
                        if a == 0:
                            s.wait(pe, S["ht_done"], 1, 1, 1)
                        bank = take(f"qkv{a}", s)
                        nc.tensor.matmul(bank[:, 0:384], h_t[:, a * P:(a + 1) * P], wqkv_s[:],
                                         start=True, stop=True).then_inc(S["qkv_mm"], 1)
                    if h == 14 and s.has(-2):
                        s.wait(pe, S["z2_done"], -2, 2, 2)
                        bank = take("z2T", s)
                        for a in range(TILES):
                            last = nc.tensor.transpose(bank[:, a * P:(a + 1) * P], z2[:, a, :], ident_s[:])
                        last.then_inc(S["z2_tr"], 1)
                    if h >= 8 and s.has(0):
                        scores_for_max(h - 8)
                if s.has(-1):
                    weigh(3)
                if s.has(-2):
                    s.wait(pe, S["h2_done"], -2, 1, 1)
                    bank = take("router", s)
                    for a in range(TILES):
                        last = nc.tensor.matmul(bank[:, a * EXPERTS:(a + 1) * EXPERTS], h2_now[:, a * P:(a + 1) * P],
                                                router_s[:], start=True, stop=True)
                    last.then_inc(S["router_mm"], 1)

            steps(pe, emit)

            pe.wait_ge(S["loaded_c"], 80)
            pe.wait_ge(S["h2_kept"], B)
            pe.wait_ge(S["exp_done"], B * 16)
            pe.wait_ge(S["heads_done"], B * 4)
            n = CHUNK // T
            per = EXPERTS * HC
            total = (CHUNK // P) * (2 * EXPERTS)
            pe.sem_inc(S["down_mm"], 4)
            with pe.Fori(0, B // n) as i:
                rhs = h2_t[:].rearrange("p (i b) t -> p i (b t)", b=n)[:, bass.ds(i, 1), :].rearrange("p i t -> p (i t)")

                def up(k):
                    e, hc = divmod(k, HC)
                    if k >= 2:
                        pe.wait_ge(S["gelu_done"], i * per + (k - 1))
                    nc.tensor.matmul(ps_sc[k % 2][:], wfc_s[:, e, hc * P:(hc + 1) * P], rhs,
                                     start=True, stop=True).then_inc(S["up_mm"], 1)

                def down(k):
                    e, hc = divmod(k, HC)
                    pe.wait_ge(S["gelu_done"], i * per + (k + 1))
                    if hc == 0 and e >= 2:
                        pe.wait_ge(S["y_done"], i * total + (8 * (e - 1)))
                    for t in range(CHUNK // P):
                        last = nc.tensor.matmul(ps_pv[e % 2][:, t * D:(t + 1) * D], act[:, k % 4, t * P:(t + 1) * P],
                                                wproj_s[:, e, hc, :], start=(hc == 0 and t == 0),
                                                stop=(hc == HC - 1), skip_group_check=True)
                    last.then_inc(S["down_mm"], 1)

                up(0)
                for k in range(per):
                    if k + 1 < per:
                        up(k + 1)
                    down(k)
                pe.wait_ge(S["y_done"], i * total + total)


def kernel(**inputs):
    import concourse.bacc as _bacc
    from concourse.bass_utils import run_bass_kernel_spmd as _run

    f = {k: np.asarray(v) for k, v in inputs.items()}
    half = DK // 2
    freq = 1.0 / 10000.0 ** (2.0 * np.arange(half, dtype=np.float32) / DK)
    angles = np.arange(T, dtype=np.float32)[:, None] * freq[None, :].astype(np.float32)
    cos = np.cos(angles).astype(np.float32)
    sin = np.sin(angles).astype(np.float32)

    def table(first, second):
        row = np.concatenate([first, second], 1)
        return np.tile(row, (1, 2 * HEADS)).reshape(TILES, P, 256).transpose(1, 0, 2)

    after = np.triu(np.full((P, P), MASKED, np.float32), 1)
    arrays = {
        "x": f["L0_attn_x"],
        "c_t": f["L0_c"].T,
        "wmod": f["L0_wmod"],
        "wqkv": np.concatenate([f["L0_attn_WQ_w"].T, f["L0_attn_WK_w"].T, f["L0_attn_WV_w"].T], 1),
        "bqkv": np.concatenate([f["L0_attn_WQ_b"], f["L0_attn_WK_b"], f["L0_attn_WV_b"]])[None],
        "wo": f["L0_attn_Wo_w"].T,
        "bo": f["L0_attn_Wo_b"][None],
        "router": f["L0_ffn_router_w"].T,
        "w_fc": f["L0_ffn_w_fc"].transpose(1, 0, 2),
        "b_fc": f["L0_ffn_b_fc"].reshape(EXPERTS, HC, P).transpose(2, 0, 1),
        "w_proj": f["L0_ffn_w_proj"].reshape(EXPERTS, HC, P, D).transpose(2, 0, 1, 3),
        "b_proj": f["L0_ffn_b_proj"].reshape(1, EXPERTS * D),
        "cos": table(cos, cos),
        "sin": table(-sin, sin),
        "ident": np.eye(P, dtype=np.float32),
        "causal": np.stack([after, after.T], 1),
        "iota": np.arange(EXPERTS, dtype=np.float32)[None],
    }
    nc = _bacc.Bacc("TRN2", target_bir_lowering=False, num_devices=1)
    feeds, args = {}, []
    for name, a in arrays.items():
        a = np.ascontiguousarray(a)
        feeds[f"in_{name}"] = a
        args.append(nc.dram_tensor(f"in_{name}", a.shape, mybir.dt.from_np(a.dtype), kind="ExternalInput").ap())
    args.append(nc.dram_tensor("out", (B, T, D), F32, kind="ExternalOutput").ap())
    block_program(nc, *args)
    return _run(nc, [feeds], core_ids=[0]).results[0]["out"]
```

```python
from contextlib import ExitStack

import numpy as np

import concourse.bass as bass
from concourse import mybir

F32 = mybir.dt.float32
F32R = mybir.dt.float32r
BF16 = mybir.dt.bfloat16
U32 = mybir.dt.uint32
I32 = mybir.dt.int32
ALU = mybir.AluOpType
ACT = mybir.ActivationFunctionType
AX = mybir.AxisListType.X

B, T, D = 16, 256, 128
HEADS, DK = 16, 8
P = 128
TILES = T // P
GROUPS = HEADS // 4
ROWS = 32
PARTS = 3 * DK
EXPERTS, HID = 8, 512
HC = HID // P
NTILES = B * TILES
EPS = 1e-5
SCALE = float(DK) ** -0.5
MASKED = -1.0e30

FIRST, LAST = 4, 14
assert (LAST - FIRST) % 2 == 0

GROUP_B = (LAST - 2, B - (LAST - 2))
GROUP_TILES = [n * TILES for n in GROUP_B]
GROUP_FROM = [0, GROUP_TILES[0]]
ROW_TILES = [2 * n + EXPERTS - 1 for n in GROUP_TILES]
ROW_FROM = [0, ROW_TILES[0]]
ALL_ROW_TILES = sum(ROW_TILES)
RING = 6
ROUNDS = ALL_ROW_TILES // RING
assert ALL_ROW_TILES % RING == 0
FIRST_ROUNDS = (ROW_TILES[0] - 1) // RING
ROW = D + 2
SKIPPED = 1 << 20
ROUTE_LEN = EXPERTS + EXPERTS * EXPERTS + NTILES + ALL_ROW_TILES
RANKS_AT = 64
ROUTE_STEPS = 16
STAGE = HID + HC + D


class Step:

    def __init__(self, t, i=None, u=0):
        self.t, self.i, self.u = t, i, u

    def has(self, d):
        return 0 <= self.t + d < B

    def value(self, d, per, n):
        first = (self.t + d) * per + n
        if self.i is None:
            return first
        return self.i * (2 * per) + first

    def wait(self, eng, sem, d, per, n):
        if self.t + d >= 0:
            eng.wait_ge(sem, self.value(d, per, n))

    def slot_wait(self, eng, sems, d):
        b = self.t + d
        n = 16 * (b // 2 + 1)
        eng.wait_ge(sems[b % 2], n if self.i is None else self.i * 16 + n)

    def hold(self, eng, sem, d, per, n, passed):
        if self.t + d >= 0:
            eng.wait_ge(sem, self.value(d, per, n))
            if self.i is not None:
                eng.sem_inc(passed, 1)

    def pick(self, ap, axis, d):
        b = self.t + d
        if self.i is None:
            index = [slice(None)] * len(ap.shape)
            index[axis] = b
            return ap[tuple(index)]
        names = [f"x{n}" for n in range(len(ap.shape))]
        left = " ".join("(tt uu)" if n == axis else x for n, x in enumerate(names))
        right = " ".join("tt uu" if n == axis else x for n, x in enumerate(names))
        v = ap.rearrange(f"{left} -> {right}", uu=2)
        index = [slice(None)] * len(v.shape)
        index[axis] = bass.ds(self.i + b // 2, 1)
        index[axis + 1] = b % 2
        v = v[tuple(index)]
        names = [f"y{n}" for n in range(len(v.shape))]
        new = names[:axis] + [f"(y{axis} y{axis + 1})"] + names[axis + 2:]
        return v.rearrange(f"{' '.join(names)} -> {' '.join(new)}")


def steps(eng, emit):
    for t in range(-1, FIRST):
        emit(Step(t))
    with eng.Fori(0, (LAST - FIRST) // 2) as i:
        for u in range(2):
            emit(Step(FIRST + u, i, u))
    for t in range(LAST, B + 2):
        emit(Step(t))


USES = {
    -1: [("qm0", -1)], 0: [("heads0", -2)], 1: [("qm1", -1)], 2: [("heads1", -2)], 3: [("k0", 0)],
    4: [("k1", 0), ("q0", 0)], 5: [("q1", 0)], 6: [("attnT", -2), ("zT", 1)], 7: [("wo", -2)],
    9: [("qkv0", 1)], 10: [("qkv1", 1)], 11: [("z2T", -2)], 13: [("router", -2)],
}
MISC = [use for slot in sorted(USES) for use in USES[slot]]
MAX_FROM = 6
BANK = {name: n % 2 for n, (name, _) in enumerate(MISC)}


def before(name, s):
    at = [n for n, (x, _) in enumerate(MISC) if x == name][0]
    bank = at % 2
    for back in range(0, 3):
        for n in range(len(MISC) - 1, -1, -1):
            if n % 2 != bank or (back == 0 and n >= at):
                continue
            x, d = MISC[n]
            if 0 <= s.t - back + d < B:
                return x, d - back
    return None


def block_program(nc, x, c_t, wmod, wqkv, bqkv, wo, bo, router, w_fc, b_fc, w_proj, b_proj,
                  cos, sin, ident, causal, route, places, blank, out):
    with ExitStack() as ctx:
        def sb(name, shape, dt=F32):
            return ctx.enter_context(nc.sbuf_tensor(name, shape, dt))

        def psum(name):
            return ctx.enter_context(nc.psum_tensor(name, [P, 512], F32))

        def sem(name):
            return ctx.enter_context(nc.semaphore(name))

        def parted(name, shapes):
            sizes = [int(np.prod(shape)) for shape in shapes]
            whole = sb(name, [P, sum(sizes)])
            parts, at = [], 0
            for shape, size in zip(shapes, sizes):
                dims = [f"x{n}" for n in range(len(shape))]
                kw = {d: v for d, v in zip(dims[1:], shape[1:])}
                parts.append(whole[:, at:at + size].rearrange(f"p ({' '.join(dims)}) -> p {' '.join(dims)}", **kw))
                at += size
            return whole, parts

        early_a, (cos_s, rope_a, rope_b, roped) = parted("early_a", [(TILES, 256)] * 4)
        early_b, (sin_s, proj_b, proj_g) = parted("early_b", [(TILES, 256), (TILES, D), (TILES, D)])
        early_c, (z, z2, x1_now, h2_now) = parted("early_c", [(TILES, D)] * 3 + [(T,)])
        ident_s = sb("ident_s", [P, P])
        ident_b = sb("ident_b", [P, P], BF16)
        causal_s = sb("causal_s", [P, 2, P])
        mask_q = sb("mask_q", [P, 2, P], BF16)
        mask_k = sb("mask_k", [P, 2, P], BF16)
        wqkv_s = sb("wqkv_s", [P, 384])
        bqkv_s = sb("bqkv_s", [P, 384])
        wo_s = sb("wo_s", [P, P])
        bo_s = sb("bo_s", [P, P])
        router_s = sb("router_s", [P, EXPERTS])
        wfc_s = sb("wfc_s", [P, EXPERTS, STAGE])
        wproj_s = sb("wproj_s", [P, EXPERTS, HC, P])
        route_s = sb("route_s", [P, ROUTE_LEN])
        places_s = sb("places_s", [P, 2, NTILES], U32)
        blank_s = sb("blank_s", [P, ROW], U32)
        half_s = sb("half_s", [P, TILES])
        c_s = sb("c_s", [P, B])
        c_exp = sb("c_exp", [P, B])
        c_den = sb("c_den", [P, B])
        c_sig = sb("c_sig", [P, B])
        c_silu = sb("c_silu", [P, B])
        mod = sb("mod", [P, B, 4])
        gate_sign = sb("gate_sign", [B, 2 * D])
        gate_neg = sb("gate_neg", [B, 2 * D])
        gate_size = sb("gate_size", [B, 2 * D])
        gate_row = sb("gate_row", [B, 4 * D])
        gates = sb("gates", [P, B, 4 * D])
        x_in = [sb(f"x_in{n}", [P, TILES, D]) for n in range(2)]
        stats = sb("stats", [P, TILES, 6])
        moments = sb("moments", [P, TILES, 2])
        var_eps = sb("var_eps", [P, TILES])
        rstd = sb("rstd", [P, TILES])
        h_t = sb("h_t", [P, T])
        qkv = sb("qkv", [P, TILES, 384])
        q_parts = sb("q_parts", [P, TILES, HEADS, ROWS], F32R)
        k_parts = sb("k_parts", [P, TILES, HEADS, ROWS], F32R)
        v_wides = sb("v_wides", [P, 2, TILES, HEADS, ROWS])
        v_wide = [v_wides[:, n] for n in range(2)]
        q_stack = sb("q_stack", [P, GROUPS, T], F32R)
        k_stacks = sb("k_stacks", [P, 2, GROUPS, T], F32R)
        k_stack = [k_stacks[:, n] for n in range(2)]
        maxima = sb("maxima", [P, TILES, HEADS])
        qm_stack = sb("qm_stack", [P, GROUPS, T], F32R)
        probs = sb("probs", [P, 8, 384])
        heads_ts = sb("heads_ts", [P, 2, GROUPS, T])
        heads_t = [heads_ts[:, n] for n in range(2)]
        x_res = [sb(f"x_res{n}", [P, TILES, D]) for n in range(2)]
        rsum = sb("rsum", [P, TILES, HEADS])
        attn = sb("attn", [P, TILES, HEADS, DK])
        attn_t = sb("attn_t", [P, T])
        x1 = sb("x1", [P, B, TILES, D])
        stats2 = sb("stats2", [P, TILES, 6])
        moments2 = sb("moments2", [P, TILES, 2])
        var_eps2 = sb("var_eps2", [P, TILES])
        rstd2 = sb("rstd2", [P, TILES])
        row_scaled = sb("row_scaled", [P, TILES, D])
        rows = sb("rows", [P, NTILES, ROW])
        logits = sb("logits", [P, B, TILES * EXPERTS])
        top = sb("top", [P, NTILES, 8])
        top_at = sb("top_at", [P, NTILES, 8], U32)
        top_f = sb("top_f", [P, NTILES, 2])
        gap = sb("gap", [P, NTILES])
        gap_exp = sb("gap_exp", [P, NTILES])
        gap_den = sb("gap_den", [P, NTILES])
        share = sb("share", [P, 2, NTILES])
        hot = sb("hot", [P, 2, NTILES, EXPERTS])
        strict = sb("strict", [P, P], BF16)
        ones = sb("ones", [P, P], BF16)
        chosen = sb("chosen", [P, NTILES + 2, EXPERTS], BF16)
        ranks = sb("ranks", [P, NTILES + 2, EXPERTS])
        tiles_of = sb("tiles_of", [P, EXPERTS])
        ahead = sb("ahead", [P, EXPERTS, EXPERTS])
        base_0 = sb("base_0", [P, EXPERTS])
        base = sb("base", [P, EXPERTS])
        slot_all = sb("slot_all", [P, NTILES, EXPERTS])
        slot_hot = sb("slot_hot", [P, 2, NTILES, EXPERTS])
        over = slot_hot[:, 0].rearrange("p n e -> p (n e)").rearrange("p (e n) -> p e n", e=EXPERTS)
        slot_f = sb("slot_f", [P, 2, NTILES])
        slots = sb("slots", [P, 2, NTILES], U32)
        reached = slot_hot[0:1].rearrange("p k n e -> p (k n e)")[:, 0:ROW_TILES[0] * EXPERTS].rearrange("p (n e) -> p n e", e=EXPERTS)
        reached_n = sb("reached_n", [1, ALL_ROW_TILES])
        expert_of = sb("expert_of", [1, ALL_ROW_TILES], I32)

        def over_of(t, size):
            flat = t[:].rearrange("p " + " ".join(f"x{n}" for n in range(len(t.shape) - 1)) + " -> p ("
                                  + " ".join(f"x{n}" for n in range(len(t.shape) - 1)) + ")")
            return flat[:, 0:size]

        wmod_s = over_of(heads_ts, 6 * D)
        staged_all = over_of(v_wides, 3 * STAGE).rearrange("p (n c) -> p n c", n=3)
        staged = [staged_all[:, n] for n in range(3)]
        act_all = over_of(early_b, 2 * HID).rearrange("p (n c t) -> p n c t", n=2, c=HC)
        act = [act_all[:, n] for n in range(2)]
        small = over_of(probs, RING * ROW + RING * D + 4 * D)
        row_in_all = small[:, 0:RING * ROW].rearrange("p (n r) -> p n r", n=RING)
        row_in = [row_in_all[:, n] for n in range(RING)]
        y_out_all = small[:, RING * ROW:RING * (ROW + D)].rearrange("p (n d) -> p n d", n=RING)
        y_out = [y_out_all[:, n] for n in range(RING)]
        row_t_all = small[:, RING * (ROW + D):RING * (ROW + D) + 2 * P].rearrange("p (n d) -> p n d", n=2)
        row_t = [row_t_all[:, n] for n in range(2)]
        y_biased = [small[:, RING * (ROW + D) + (2 + n) * P:RING * (ROW + D) + (3 + n) * P] for n in range(2)]
        y_pair = [over_of(t, 8 * T).rearrange("p (b a k d) -> p b a k d", b=4, a=TILES, k=2)
                  for t in (heads_ts, early_a)]
        sums = over_of(early_c, 4 * T).rearrange("p (n a d) -> p n a d", n=4, a=TILES)
        y_sum = [sums[:, n] for n in range(2)]
        y_gated = [sums[:, 2 + n] for n in range(2)]

        misc = [psum(f"misc{n}") for n in range(2)]
        ps_max = [psum(f"ps_max{n}") for n in range(2)]
        ps_sc = [psum(f"ps_sc{n}") for n in range(2)]
        ps_pv = [psum(f"ps_pv{n}") for n in range(2)]

        gate_dram = nc.dram_tensor("gate_rows", [B, 4 * D], F32).ap()
        sorted_dram = nc.dram_tensor("sorted_rows", [ALL_ROW_TILES * P, ROW], F32).ap()
        result_dram = nc.dram_tensor("results", [B * T * 2, D], F32).ap()

        names = """loaded_a loaded_b loaded_c loaded_w gate_out gate_in zeroed
        masks_ready c_exp_done c_den_done c_sig_done silu_done mod_mm gate_mm mod_done sign_done neg_done size_done gate_done
        stats_done moments_done eps_done rstd_done z_done zt_done ht_done qkv_mm qkv_done
        rope_done roped_done q_high k_high q_low k_low k_tr q_tr k_stacked q_stacked v_done
        max_mm max_done shift_high shifts_done qm_tr qm_stacked score_mm exp_done pv_mm heads_done
        heads_tr rsum_done attn_done attn_tr attn_t_done wo_mm wo_bias wo_gated x1_done x1_kept dve_passed pool_passed
        stats2_done moments2_done eps2_done rstd2_done z2_done z2_tr h2_done router_mm logits_done
        row_scaled rows_done blank_out top_done at_done gap_done gap_exp_done route_step shared
        chosen_done rank_mm ranks_read slots_done sorted_a sorted_b expert_done
        x_turned row_t_done staged_done up_mm gelu_done down_mm y_biased y_done
        y_summed y_gated final_done written sp_passed tails_done""".split()
        S = {n: sem(n) for n in names}
        x_loaded = [sem(f"x_loaded{n}") for n in range(2)]
        xres_loaded = [sem(f"xres_loaded{n}") for n in range(2)]
        row_loaded = [sem(f"row_loaded{n}") for n in range(RING)]
        y_sent = [sem(f"y_sent{n}") for n in range(RING)]
        pairs_in = [sem(f"pairs_in{n}") for n in range(B // 4)]

        freed = {
            "qm0": ("qm_stacked", 2, 1), "qm1": ("qm_stacked", 2, 2),
            "heads0": ("attn_done", 2, 1), "heads1": ("attn_done", 2, 2),
            "k0": ("k_stacked", 2, 1), "k1": ("k_stacked", 2, 2),
            "q0": ("q_stacked", 2, 1), "q1": ("q_stacked", 2, 2),
            "attnT": ("attn_t_done", 1, 1), "zT": ("ht_done", 1, 1), "wo": ("wo_bias", 1, 1),
            "qkv0": ("qkv_done", 2, 1), "qkv1": ("qkv_done", 2, 2),
            "z2T": ("h2_done", 1, 1), "router": ("logits_done", 1, 1),
        }

        block = ctx.enter_context(nc.Block())

        x_v = x.rearrange("b (a p) d -> b p a d", p=P)
        out_v = out.rearrange("b (a p) d -> p b a d", p=P)
        rows_v = rows[:].rearrange("p (b a) r -> p b a r", a=TILES)
        pair_v = result_dram.rearrange("(b a p k) d -> p b a (k d)", a=TILES, p=P, k=2)
        iota_r = route_s[:, 0:EXPERTS]
        before_r = route_s[:, EXPERTS:EXPERTS + EXPERTS * EXPERTS]
        full_r = route_s[:, EXPERTS + EXPERTS * EXPERTS:EXPERTS + EXPERTS * EXPERTS + NTILES]
        tile_r = route_s[0:1, EXPERTS + EXPERTS * EXPERTS + NTILES:ROUTE_LEN]

        def expert_at(i, u):
            v = expert_of[:].rearrange("o (i u) -> o i u", u=RING)
            return v[:, bass.ds(i + u // RING, 1), u % RING]

        @block.sync
        def _(sp):
            for dst, src in ((c_s[:], c_t), (wmod_s, wmod)):
                sp.dma_start(dst, src).then_inc(S["loaded_a"], 16)
            sp.dma_start(ident_s[:], ident).then_inc(S["loaded_b"], 16)
            for dst, src in (
                (causal_s[:], causal), (wqkv_s[:], wqkv), (bqkv_s[:], bqkv.broadcast_to([P, 384])),
                (cos_s, cos), (sin_s, sin),
            ):
                sp.dma_start(dst, src).then_inc(S["loaded_b"], 16)

            def emit(s):
                if s.has(2):
                    s.wait(sp, S["z_done"], 0, 2, 2)
                    sp.dma_start(x_in[s.t % 2][:], s.pick(x_v, 0, 2)).then_inc(x_loaded[s.t % 2], 16)
                if s.has(-1):
                    s.wait(sp, S["x1_done"], -3, 1, 1)
                    sp.dma_start(x_res[(s.t - 1) % 2][:], s.pick(x_v, 0, -1)).then_inc(xres_loaded[(s.t - 1) % 2], 16)

            sp.dma_start(x_in[0][:], x_v[0]).then_inc(x_loaded[0], 16)
            for dst, src in ((wo_s[:], wo), (bo_s[:], bo.broadcast_to([P, D])), (router_s[:], router)):
                sp.dma_start(dst, src).then_inc(S["loaded_w"], 16)
            sp.wait_ge(S["gate_done"], 3)
            sp.dma_start(gate_dram, gate_row[:]).then_inc(S["gate_out"], 16)
            sp.wait_ge(S["gate_out"], 16)
            sp.dma_start(gates[:].rearrange("p b d -> p (b d)"),
                         gate_dram.rearrange("(o b) d -> o (b d)", o=1).broadcast_to([P, B * 4 * D])
                         ).then_inc(S["gate_in"], 16)
            for dst, src in ((route_s[:], route.broadcast_to([P, ROUTE_LEN])), (places_s[:], places),
                             (blank_s[:], blank.broadcast_to([P, ROW]))):
                sp.dma_start(dst, src).then_inc(S["loaded_w"], 16)
            for dst, src in (
                (wfc_s[:, :, 0:HID], w_fc), (wfc_s[:, :, HID:HID + HC], b_fc), (wproj_s[:], w_proj),
                (wfc_s[:, :, HID + HC:], b_proj.broadcast_to([P, EXPERTS, D])),
            ):
                sp.dma_start(dst, src).then_inc(S["loaded_c"], 16)
            sp.wait_ge(S["loaded_w"], 96)
            sp.dma_start(sorted_dram.rearrange("(p t) r -> p t r", p=P),
                         blank_s[:].bitcast(F32).rearrange("p (o r) -> p o r", o=1).broadcast_to([P, ALL_ROW_TILES, ROW])
                         ).then_inc(S["blank_out"], 16)
            steps(sp, emit)

            sorted_v = sorted_dram.rearrange("(i u p) r -> p i u r", u=RING, p=P)

            def load_row(i, u):
                if not isinstance(i, int):
                    sp.wait_ge(y_sent[u], i * 16)
                    sp.sem_inc(S["sp_passed"], 1)
                elif i > 0:
                    sp.wait_ge(y_sent[u], 16 * i)
                sp.dma_start(row_in[u], sorted_v[:, bass.ds(i, 1), u, :].rearrange("p i r -> p (i r)")
                             ).then_inc(row_loaded[u], 16)

            def load_pairs(n):
                if n >= 2:
                    sp.wait_ge(S["y_summed"], 4 * (n - 1))
                for b in range(4):
                    sp.dma_start(y_pair[n % 2][:, b].rearrange("p a k d -> p a (k d)"), pair_v[:, 4 * n + b]
                                 ).then_inc(pairs_in[n], 16)

            def store(n):
                sp.wait_ge(S["final_done"], 4 * (n + 1))
                sp.dma_start(out_v[:, 4 * n:4 * n + 4].rearrange("p b a d -> p (b a) d"),
                             x1[:, 4 * n:4 * n + 4].rearrange("p b a d -> p (b a) d")).then_inc(S["written"], 16)

            sp.wait_ge(S["sorted_a"], 16 * 2 * GROUP_TILES[0])
            sp.wait_ge(S["pv_mm"], 4 * B)
            sp.wait_ge(S["heads_tr"], 2 * B)
            sp.wait_ge(S["q_high"], 2 * B)
            sp.wait_ge(S["q_low"], B)
            for u in range(RING):
                load_row(0, u)
            with sp.Fori(1, FIRST_ROUNDS) as i:
                for u in range(RING):
                    load_row(i, u)
            sp.wait_ge(S["sorted_b"], 16 * 2 * GROUP_TILES[1])
            for i in range(FIRST_ROUNDS, ROUNDS):
                for u in range(RING):
                    load_row(i, u)
                n = i - FIRST_ROUNDS - 1
                if n >= 0:
                    load_pairs(n)
                if n >= 1:
                    store(n - 1)
            for n in range(ROUNDS - FIRST_ROUNDS - 2, B // 4 - 1):
                store(n)
            for u in range(RING):
                sp.wait_ge(y_sent[u], 16 * ROUNDS)
            load_pairs(B // 4 - 1)
            for b in range(B - 4, B):
                sp.wait_ge(S["final_done"], b + 1)
                sp.dma_start(out_v[:, b], x1[:, b]).then_inc(S["written"], 16)
            sp.wait_ge(S["written"], 16 * (B // 4 - 1 + 4))

        @block.gpsimd
        def _(pool):
            for n, (t, v) in enumerate((
                (k_parts[:].bitcast(F32), 0.0), (q_parts[:].bitcast(F32), 0.0), (v_wide[0], 0.0), (v_wide[1], 0.0),
            )):
                nc.gpsimd.memset(t, v).then_inc(S["zeroed"], 1)
            nc.gpsimd.memset(half_s[:], -0.5).then_inc(S["zeroed"], 1)
            pool.wait_ge(S["zeroed"], 5)
            nc.gpsimd.memset(k_parts[:, :, :, PARTS:PARTS + 2].bitcast(F32), 1.0).then_inc(S["zeroed"], 1)
            nc.gpsimd.memset(v_wide[0][:, :, :, DK:DK + 1], 1.0).then_inc(S["zeroed"], 1)
            nc.gpsimd.memset(v_wide[1][:, :, :, DK:DK + 1], 1.0).then_inc(S["zeroed"], 1)
            nc.gpsimd.memset(chosen[:], 0.0).then_inc(S["zeroed"], 1)
            pool.wait_ge(S["zeroed"], 9)
            pool.wait_ge(S["loaded_w"], 96)

            def tails(group, k):
                js = slice(GROUP_FROM[group], GROUP_FROM[group] + GROUP_TILES[group])
                nc.gpsimd.tensor_copy(rows[:, js, D:D + 1].rearrange("p n o -> p (n o)"), share[:, k, js]).then_inc(S["tails_done"], 1)
                nc.gpsimd.tensor_copy(rows[:, js, D + 1:D + 2].bitcast(U32).rearrange("p n o -> p (n o)"),
                                      places_s[:, k, js]).then_inc(S["tails_done"], 1)
                pool.wait_ge(S["tails_done"], 4 * group + 2 * k + 2)

            def sort_rows(group, k, signal):
                for n in range(GROUP_FROM[group], GROUP_FROM[group] + GROUP_TILES[group]):
                    nc.gpsimd.indirect_dma_start(
                        sorted_dram, bass.IndirectOffsetOnAxis(ap=slots[:, k, n:n + 1], axis=0),
                        rows[:, n, :], None).then_inc(S[signal], 16)

            def emit(s):
                if s.t == LAST + 1:
                    pool.wait_ge(S["slots_done"], 1)
                    pool.wait_ge(S["shared"], 2)
                    pool.wait_ge(S["blank_out"], 16)
                    tails(0, 0)
                    sort_rows(0, 0, "sorted_a")
                if s.t == LAST + 2:
                    pool.wait_ge(S["sorted_a"], 16 * GROUP_TILES[0])
                    tails(0, 1)
                    sort_rows(0, 1, "sorted_a")
                if s.has(0):
                    s.wait(pool, S["qkv_done"], 0, 2, 2)
                    s.hold(pool, S["pv_mm"], -2, 4, 4, S["pool_passed"])
                    if s.t < 2:
                        pool.wait_ge(S["zeroed"], 8)
                    nc.gpsimd.tensor_copy(
                        v_wide[s.t % 2][:, :, :, 0:DK],
                        qkv[:, :, 256:384].rearrange("p a (h d) -> p a h d", h=HEADS)).then_inc(S["v_done"], 1)
                if s.has(1):
                    s.hold(pool, S["moments_done"], 1, 2, 2, S["pool_passed"])
                    nc.gpsimd.tensor_scalar_add(var_eps[:], moments[:, :, 1], EPS).then_inc(S["eps_done"], 1)
                    s.wait(pool, S["eps_done"], 1, 1, 1)
                    s.wait(pool, S["z_done"], 0, 2, 2)
                    nc.gpsimd.tensor_tensor(rstd[:], var_eps[:], half_s[:], ALU.pow).then_inc(S["rstd_done"], 1)
                if s.has(-2):
                    s.hold(pool, S["x1_done"], -2, 1, 1, S["pool_passed"])
                    nc.gpsimd.tensor_copy(s.pick(x1[:], 1, -2), x1_now).then_inc(S["x1_kept"], 1)
                    s.hold(pool, S["moments2_done"], -2, 2, 2, S["pool_passed"])
                    nc.gpsimd.tensor_scalar_add(var_eps2[:], moments2[:, :, 1], EPS).then_inc(S["eps2_done"], 1)
                    s.wait(pool, S["eps2_done"], -2, 1, 1)
                    s.wait(pool, S["z2_done"], -3, 2, 2)
                    nc.gpsimd.tensor_tensor(rstd2[:], var_eps2[:], half_s[:], ALU.pow).then_inc(S["rstd2_done"], 1)
                if s.has(-2):
                    s.hold(pool, S["z2_done"], -2, 2, 2, S["pool_passed"])
                    if s.t == 2:
                        pool.wait_ge(S["gate_in"], 16)
                    m = s.pick(gates[:], 1, -2)
                    wide = [P, TILES, D]
                    nc.gpsimd.tensor_tensor(row_scaled[:], z2, m[:, 2 * D:3 * D].rearrange("p (o d) -> p o d", o=1).broadcast_to(wide),
                                            ALU.mult).then_inc(S["row_scaled"], 1)
                    s.hold(pool, S["row_scaled"], -2, 1, 1, S["pool_passed"])
                    nc.gpsimd.tensor_tensor(s.pick(rows_v, 1, -2)[:, :, 0:D], row_scaled[:],
                                            m[:, 3 * D:4 * D].rearrange("p (o d) -> p o d", o=1).broadcast_to(wide),
                                            ALU.add).then_inc(S["rows_done"], 1)

            steps(pool, emit)
            pool.wait_ge(S["slots_done"], 2)
            pool.wait_ge(S["shared"], 4)
            pool.wait_ge(S["rows_done"], B)
            tails(1, 0)
            sort_rows(1, 0, "sorted_b")
            pool.wait_ge(S["sorted_b"], 16 * GROUP_TILES[1])
            tails(1, 1)
            sort_rows(1, 1, "sorted_b")
            with pool.Fori(0, ROUNDS) as i:
                for u in range(RING):
                    pool.wait_ge(S["y_done"], i * RING + (u + 1))
                    pool.sem_inc(S["pool_passed"], 1)
                    nc.gpsimd.indirect_dma_start(
                        result_dram, bass.IndirectOffsetOnAxis(ap=row_in[u][:, D + 1:D + 2].bitcast(U32), axis=0),
                        y_out[u], None, bounds_check=B * T * 2 - 1, oob_is_err=False).then_inc(y_sent[u], 16)

        @block.scalar
        def _(act_e):
            act_e.wait_ge(S["loaded_a"], 32)
            nc.scalar.activation(c_exp[:], c_s[:], ACT.Exp, scale=-1.0).then_inc(S["c_exp_done"], 1)

            def gap_exponential(group):
                js = slice(GROUP_FROM[group], GROUP_FROM[group] + GROUP_TILES[group])
                act_e.wait_ge(S["gap_done"], group + 1)
                nc.scalar.activation(gap_exp[:, js], gap[:, js], ACT.Exp).then_inc(S["gap_exp_done"], 1)

            def emit(s):
                def high_parts():
                    s.wait(act_e, S["roped_done"], 0, 1, 1)
                    if s.t == 0:
                        act_e.wait_ge(S["zeroed"], 8)
                    for which, parts, slots, name, old in (
                        (1, k_parts, (0, 2), "k_high", "k_tr"), (0, q_parts, (0, 1), "q_high", "qm_tr"),
                    ):
                        s.wait(act_e, S[old], -1, 2, 2)
                        src = roped.rearrange("p a (w h d) -> p a w h d", w=2, h=HEADS)[:, :, which]
                        for m, slot in enumerate(slots):
                            nc.scalar.activation(parts[:, :, :, slot * DK:(slot + 1) * DK], src,
                                                 ACT.Copy).then_inc(S[name], 1)

                def exp(h):
                    s.wait(act_e, S["score_mm"], -1, 16, h + 1)
                    if h >= 8:
                        s.wait(act_e, S["pv_mm"], -1, 4, h // 4 - 1)
                    else:
                        s.wait(act_e, S["pv_mm"], -2, 4, h // 4 + 3)
                    nc.scalar.activation(probs[:, h % 8, :], ps_sc[h % 2][:, 0:384], ACT.Exp,
                                         scale=SCALE).then_inc(S["exp_done"], 1)

                def heads_out(g):
                    s.wait(act_e, S["pv_mm"], -1, 4, g + 1)
                    s.wait(act_e, S["heads_tr"], -3, 2, 2)
                    nc.scalar.activation(heads_t[(s.t - 1) % 2][:, g, :], ps_pv[g % 2][:, 0:T],
                                         ACT.Copy).then_inc(S["heads_done"], 1)

                def take_out(name):
                    bank = misc[BANK[name]]
                    if name[:2] == "qm":
                        n = int(name[2])
                        s.wait(act_e, S["qm_tr"], -1, 2, n + 1)
                        s.wait(act_e, S["score_mm"], -2, 16, 16)
                        nc.scalar.activation(qm_stack[:, 2 * n:2 * n + 2, :].rearrange("p g t -> p (g t)"),
                                             bank[:], ACT.Copy).then_inc(S["qm_stacked"], 1)
                    elif name in ("k0", "k1", "q0", "q1"):
                        which, n = name[0], int(name[1])
                        s.wait(act_e, S[f"{which}_tr"], 0, 2, n + 1)
                        dst = k_stack[s.t % 2] if which == "k" else q_stack
                        if which == "k":
                            s.wait(act_e, S["score_mm"], -2, 16, 16)
                        else:
                            s.wait(act_e, S["max_mm"], -1, 16, 16)
                        nc.scalar.activation(dst[:, 2 * n:2 * n + 2, :].rearrange("p g t -> p (g t)"),
                                             bank[:], ACT.Copy).then_inc(S[f"{which}_stacked"], 1)
                    elif name == "attnT":
                        s.wait(act_e, S["attn_tr"], -2, 1, 1)
                        s.wait(act_e, S["wo_mm"], -3, 1, 1)
                        nc.scalar.activation(attn_t[:], bank[:, 0:T], ACT.Copy).then_inc(S["attn_t_done"], 1)
                    elif name == "zT":
                        s.wait(act_e, S["zt_done"], 1, 1, 1)
                        s.wait(act_e, S["qkv_mm"], 0, 2, 2)
                        if s.t == -1:
                            act_e.wait_ge(S["mod_done"], 4)
                        m = s.pick(mod[:], 1, 1)
                        nc.scalar.activation(h_t[:], bank[:, 0:T], ACT.Identity,
                                             bias=m[:, 0:1], scale=m[:, 1:2]).then_inc(S["ht_done"], 1)
                    elif name == "z2T":
                        s.wait(act_e, S["z2_tr"], -2, 1, 1)
                        s.wait(act_e, S["router_mm"], -3, 1, 1)
                        m = s.pick(mod[:], 1, -2)
                        nc.scalar.activation(h2_now, bank[:, 0:T], ACT.Identity,
                                             bias=m[:, 2:3], scale=m[:, 3:4]).then_inc(S["h2_done"], 1)

                for h in range(-1, HEADS):
                    if h >= 0 and s.has(-1):
                        exp(h)
                        if h % 4 == 2 and h > 4:
                            heads_out(h // 4 - 1)
                    for name, d in USES.get(h, []):
                        if s.has(d):
                            take_out(name)
                    if h == 1 and s.has(0):
                        high_parts()
                if s.has(-1):
                    heads_out(3)
                if s.t == LAST:
                    gap_exponential(0)

            steps(act_e, emit)
            gap_exponential(1)

            def gelu(i, u):
                act_e.wait_ge(S["up_mm"], i * RING + (u + 1))
                act_e.wait_ge(S["down_mm"], i * RING + (u + 1))
                for hc in range(HC):
                    nc.scalar.activation(act[u % 2][:, hc, :], ps_sc[u % 2][:, hc * P:(hc + 1) * P], ACT.Gelu_apprx_tanh,
                                         bias=staged[u % 3][:, HID + hc:HID + hc + 1]).then_inc(S["gelu_done"], 1)

            act_e.wait_ge(S["x1_done"], B)
            act_e.wait_ge(S["roped_done"], B)
            with act_e.Fori(0, ROUNDS) as i:
                for u in range(RING):
                    gelu(i, u)

        @block.vector
        def _(dve):
            dve.wait_ge(S["loaded_b"], 96)
            for n in range(2):
                nc.vector.tensor_copy(mask_q[:, n, :], causal_s[:, 0, :]).then_inc(S["masks_ready"], 1)
                nc.vector.tensor_copy(mask_k[:, n, :], causal_s[:, 1, :]).then_inc(S["masks_ready"], 1)
            nc.vector.tensor_copy(ident_b[:], ident_s[:]).then_inc(S["masks_ready"], 1)
            nc.vector.tensor_scalar(strict[:], causal_s[:, 0, :], 0.0, None, ALU.is_lt).then_inc(S["masks_ready"], 1)
            nc.vector.tensor_scalar(ones[:], causal_s[:, 0, :], 0.0, None, ALU.is_le).then_inc(S["masks_ready"], 1)
            dve.wait_ge(S["c_exp_done"], 1)
            nc.vector.tensor_scalar_add(c_den[:], c_exp[:], 1.0).then_inc(S["c_den_done"], 1)
            dve.wait_ge(S["c_den_done"], 1)
            nc.vector.reciprocal(c_sig[:], c_den[:]).then_inc(S["c_sig_done"], 1)
            dve.wait_ge(S["c_sig_done"], 1)
            nc.vector.tensor_tensor(c_silu[:], c_s[:], c_sig[:], ALU.mult).then_inc(S["silu_done"], 1)
            dve.wait_ge(S["mod_mm"], 1)
            for n in range(4):
                nc.vector.tensor_scalar_add(mod[:, :, n], ps_max[0][:, n * B:(n + 1) * B],
                                            float(n % 2)).then_inc(S["mod_done"], 1)
            dve.wait_ge(S["gate_mm"], 1)
            g = ps_max[1][0:B, 0:2 * D]
            nc.vector.tensor_scalar(gate_sign[:], g, 0.0, 2.0, ALU.is_ge, ALU.mult).then_inc(S["sign_done"], 1)
            nc.vector.tensor_scalar(gate_neg[:], g, -1.0, 0.25, ALU.mult, ALU.max).then_inc(S["neg_done"], 1)
            dve.wait_ge(S["neg_done"], 1)
            nc.vector.tensor_tensor(gate_size[:], g, gate_neg[:], ALU.max).then_inc(S["size_done"], 1)
            dve.wait_ge(S["sign_done"], 1)
            dve.wait_ge(S["size_done"], 1)
            nc.vector.tensor_scalar_add(gate_row[:, 2 * D:3 * D], ps_max[1][0:B, 2 * D:3 * D], 1.0).then_inc(S["gate_done"], 1)
            nc.vector.tensor_copy(gate_row[:, 3 * D:4 * D], ps_max[1][0:B, 3 * D:4 * D]).then_inc(S["gate_done"], 1)
            nc.vector.scalar_tensor_tensor(out=gate_row[:, 0:2 * D], in0=gate_sign[:], scalar=-1.0, in1=gate_size[:],
                                           op0=ALU.add, op1=ALU.mult).then_inc(S["gate_done"], 1)

            def statistics(s, d, src, st, mo, sd, md):
                for a in range(TILES):
                    nc.vector.bn_stats(st[:, a, :], src[:, a, :]).then_inc(S[sd], 1)
                s.hold(dve, S[sd], d, 2, 2, S["dve_passed"])
                for a in range(TILES):
                    nc.vector.bn_aggr(mo[:, a, :], st[:, a, :]).then_inc(S[md], 1)

            def normalise(s, d, src, mo, rs, zz, rd, zd, readers):
                s.wait(dve, S[rd], d, 1, 1)
                s.wait(dve, S[readers], d - 1, 1, 1)
                if readers == "z2_tr":
                    s.wait(dve, S["row_scaled"], d - 1, 1, 1)
                for a in range(TILES):
                    nc.vector.tensor_scalar(zz[:, a, :], src[:, a, :], mo[:, a, 0:1], rs[:, a:a + 1],
                                            ALU.subtract, ALU.mult).then_inc(S[zd], 1)

            def find_top(tiles):
                lg = logits[:].rearrange("p b (a e) -> p (b a) e", a=TILES)
                for n in tiles:
                    nc.vector.max(top[:, n, :], lg[:, n, :]).then_inc(S["top_done"], 1)
                dve.wait_ge(S["top_done"], tiles[-1] + 1)
                for n in tiles:
                    nc.vector.max_index(top_at[:, n, :], top[:, n, :], lg[:, n, :]).then_inc(S["at_done"], 1)

            def choose(group):
                js = slice(GROUP_FROM[group], GROUP_FROM[group] + GROUP_TILES[group])
                wide = [P, GROUP_TILES[group], EXPERTS]
                nc.vector.tensor_tensor(gap[:, js], top[:, js, 1], top[:, js, 0], ALU.subtract).then_inc(S["gap_done"], 1)
                dve.wait_ge(S["at_done"], js.stop)
                nc.vector.tensor_copy(top_f[:, js, :], top_at[:, js, 0:2]).then_inc(S["route_step"], 1)
                dve.wait_ge(S["route_step"], ROUTE_STEPS * group + 1)
                for k in range(2):
                    nc.vector.tensor_tensor(hot[:, k, js], iota_r.rearrange("p (o e) -> p o e", o=1).broadcast_to(wide),
                                            top_f[:, js, k:k + 1].broadcast_to(wide), ALU.is_equal).then_inc(S["route_step"], 1)
                dve.wait_ge(S["route_step"], ROUTE_STEPS * group + 3)
                to = slice(js.start + group, js.stop + group)
                nc.vector.tensor_tensor(chosen[:, to], hot[:, 0, js], hot[:, 1, js], ALU.add).then_inc(S["chosen_done"], 1)

            def read_ranks(group, bank):
                dve.wait_ge(S["rank_mm"], group + 1)
                n = (GROUP_TILES[group] + 1) * EXPERTS
                to = slice(GROUP_FROM[group] + group, GROUP_FROM[group] + group + GROUP_TILES[group] + 1)
                nc.vector.tensor_copy(ranks[:, to].rearrange("p n e -> p (n e)"), bank[:, RANKS_AT:RANKS_AT + n]
                                      ).then_inc(S["ranks_read"], 1)

            def place(group):
                js = slice(GROUP_FROM[group], GROUP_FROM[group] + GROUP_TILES[group])
                nt = GROUP_TILES[group]
                rk = ranks[:, js.start + group:js.stop + group + 1]
                done = ROUTE_STEPS * group + 3

                dve.wait_ge(S["gap_exp_done"], group + 1)
                nc.vector.tensor_scalar_add(gap_den[:, js], gap_exp[:, js], 1.0).then_inc(S["route_step"], 1)
                dve.wait_ge(S["ranks_read"], group + 1)
                cmp = [P, EXPERTS, nt]
                nc.vector.tensor_tensor(over[:, :, 0:nt], rk[:, nt, :].rearrange("p (e o) -> p e o", o=1).broadcast_to(cmp),
                                        full_r[:, 0:nt].rearrange("p (o n) -> p o n", o=1).broadcast_to(cmp),
                                        ALU.is_gt).then_inc(S["route_step"], 1)
                dve.wait_ge(S["route_step"], done + 2)
                first = share[:, 0, js]
                nc.vector.reciprocal(first, gap_den[:, js]).then_inc(S["shared"], 1)
                nc.vector.tensor_reduce(tiles_of[:], over[:, :, 0:nt], AX, ALU.add).then_inc(S["route_step"], 1)
                dve.wait_ge(S["shared"], 2 * group + 1)
                nc.vector.tensor_tensor(share[:, 1, js], first, gap_exp[:, js],
                                        ALU.mult).then_inc(S["shared"], 1)
                dve.wait_ge(S["route_step"], done + 3)
                sq = [P, EXPERTS, EXPERTS]
                nc.vector.tensor_tensor(ahead[:], before_r.rearrange("p (e f) -> p e f", f=EXPERTS),
                                        tiles_of[:].rearrange("p (o f) -> p o f", o=1).broadcast_to(sq),
                                        ALU.mult).then_inc(S["route_step"], 1)
                dve.wait_ge(S["route_step"], done + 4)
                nc.vector.tensor_reduce(base_0[:], ahead[:], AX, ALU.add).then_inc(S["route_step"], 1)
                dve.wait_ge(S["route_step"], done + 5)
                nc.vector.tensor_scalar_add(base[:], base_0[:], float(ROW_FROM[group])).then_inc(S["route_step"], 1)
                dve.wait_ge(S["route_step"], done + 6)
                wide = [P, nt, EXPERTS]
                nc.vector.scalar_tensor_tensor(out=slot_all[:, js], in0=base[:].rearrange("p (o e) -> p o e", o=1).broadcast_to(wide),
                                               scalar=float(P), in1=rk[:, 0:nt], op0=ALU.mult, op1=ALU.add
                                               ).then_inc(S["route_step"], 1)
                dve.wait_ge(S["route_step"], done + 7)
                for k in range(2):
                    nc.vector.tensor_tensor(slot_hot[:, k, js], slot_all[:, js], hot[:, k, js], ALU.mult).then_inc(S["route_step"], 1)
                dve.wait_ge(S["route_step"], done + 9)
                for k in range(2):
                    nc.vector.tensor_reduce(slot_f[:, k, js], slot_hot[:, k, js], AX, ALU.add).then_inc(S["route_step"], 1)
                dve.wait_ge(S["route_step"], done + 11)
                nc.vector.tensor_copy(slots[:, :, js], slot_f[:, :, js]).then_inc(S["slots_done"], 1)
                ts = slice(ROW_FROM[group], ROW_FROM[group] + ROW_TILES[group])
                wide = [1, ROW_TILES[group], EXPERTS]
                nc.vector.tensor_tensor(reached[:, 0:ROW_TILES[group]], tile_r[:, ts].rearrange("p (n o) -> p n o", o=1).broadcast_to(wide),
                                        base[0:1].rearrange("p (o e) -> p o e", o=1).broadcast_to(wide),
                                        ALU.is_ge).then_inc(S["route_step"], 1)
                dve.wait_ge(S["route_step"], done + 12)
                nc.vector.tensor_reduce(reached_n[:, ts], reached[:, 0:ROW_TILES[group]], AX, ALU.add).then_inc(S["route_step"], 1)
                dve.wait_ge(S["route_step"], done + 13)
                nc.vector.tensor_scalar_add(expert_of[:, ts], reached_n[:, ts], -1.0).then_inc(S["expert_done"], 1)

            def halves(v, m):
                return v.rearrange("p a (g f i) -> p a g f i", f=2, i=4)[:, :, :, m, :]

            def emit(s):
                def rope():
                    s.wait(dve, S["qkv_done"], 0, 2, 2)
                    qk = qkv[:, :, 0:256]
                    nc.vector.tensor_tensor(rope_a, qk, cos_s, ALU.mult).then_inc(S["rope_done"], 1)
                    for n in range(2):
                        for a in range(TILES):
                            nc.vector.tensor_tensor(halves(rope_b, n)[:, a], halves(qk, 1 - n)[:, a],
                                                    halves(sin_s, n)[:, a], ALU.mult).then_inc(S["rope_done"], 1)
                    s.wait(dve, S["rope_done"], 0, 5, 5)
                    s.wait(dve, S["q_high"], -1, 2, 2)
                    nc.vector.tensor_tensor(roped, rope_a, rope_b, ALU.add).then_inc(S["roped_done"], 1)

                def low_parts():
                    for which, parts, of, to, high, low in (
                        (1, k_parts, 0, 1, "k_high", "k_low"), (0, q_parts, 0, 2, "q_high", "q_low"),
                    ):
                        s.wait(dve, S[high], 0, 2, 2)
                        src = roped.rearrange("p a (w h d) -> p a w h d", w=2, h=HEADS)[:, :, which]
                        nc.vector.tensor_tensor(parts[:, :, :, to * DK:(to + 1) * DK], src,
                                                parts[:, :, :, of * DK:(of + 1) * DK].bitcast(F32),
                                                ALU.subtract).then_inc(S[low], 1)

                def divide(a):
                    s.wait(dve, S["heads_tr"], -2, 2, a + 1)
                    m = misc[BANK[f"heads{a}"]][:].rearrange("p (h r) -> p h r", h=HEADS)
                    nc.vector.reciprocal(rsum[:, a, :], m[:, :, DK]).then_inc(S["rsum_done"], 1)
                    s.wait(dve, S["rsum_done"], -2, 2, a + 1)
                    s.wait(dve, S["attn_tr"], -3, 1, 1)
                    nc.vector.tensor_tensor(attn[:, a], m[:, :, 0:DK],
                                            rsum[:, a, :].rearrange("p (h o) -> p h o", o=1).broadcast_to([P, HEADS, DK]),
                                            ALU.mult).then_inc(S["attn_done"], 1)

                def residual():
                    s.wait(dve, S["wo_mm"], -2, 1, 1)
                    if s.t == 2:
                        dve.wait_ge(S["loaded_w"], 48)
                        dve.wait_ge(S["gate_in"], 16)
                    bias = bo_s[:].rearrange("p (o d) -> p o d", o=1).broadcast_to([P, TILES, D])
                    gate = s.pick(gates[:], 1, -2)[:, 0:D].rearrange("p (o d) -> p o d", o=1).broadcast_to([P, TILES, D])
                    nc.vector.tensor_tensor(proj_b, misc[BANK["wo"]][:, 0:T].rearrange("p (a d) -> p a d", a=TILES),
                                            bias, ALU.add).then_inc(S["wo_bias"], 1)
                    s.wait(dve, S["wo_bias"], -2, 1, 1)
                    nc.vector.tensor_tensor(proj_g, proj_b, gate, ALU.mult).then_inc(S["wo_gated"], 1)
                    s.wait(dve, S["wo_gated"], -2, 1, 1)
                    s.slot_wait(dve, xres_loaded, -2)
                    s.wait(dve, S["x1_kept"], -3, 1, 1)
                    nc.vector.tensor_tensor(x1_now, proj_g, x_res[s.t % 2][:], ALU.add).then_inc(S["x1_done"], 1)
                    s.wait(dve, S["x1_done"], -2, 1, 1)

                def maxima_of(h):
                    s.wait(dve, S["max_mm"], 0, 16, h + 1)
                    nc.vector.tensor_reduce(maxima[:, 0, h:h + 1], ps_max[h % 2][:, 0:128], AX, ALU.max)
                    nc.vector.tensor_reduce(maxima[:, 1, h:h + 1], ps_max[h % 2][:, 128:384], AX,
                                            ALU.max).then_inc(S["max_done"], 1)

                if s.has(0):
                    rope()
                if s.has(1):
                    s.slot_wait(dve, x_loaded, 1)
                    statistics(s, 1, x_in[(s.t + 1) % 2], stats, moments, "stats_done", "moments_done")
                if s.has(-2):
                    divide(0)
                if s.has(0):
                    low_parts()
                if s.has(-2):
                    divide(1)
                if s.has(1):
                    normalise(s, 1, x_in[(s.t + 1) % 2], moments, rstd, z, "rstd_done", "z_done", "zt_done")
                for h in range(HEADS):
                    if s.has(0):
                        maxima_of(h)
                    if s.t == LAST and h < 8:
                        if h == 0:
                            dve.wait_ge(S["logits_done"], GROUP_B[0])
                        find_top(range(3 * h, 3 * h + 3))
                    if s.t == LAST and h == 8:
                        choose(0)
                    if h == 3 and s.has(-2):
                        residual()
                        statistics(s, -2, x1_now, stats2, moments2, "stats2_done", "moments2_done")
                    if h == 5 and s.has(-2):
                        normalise(s, -2, x1_now, moments2, rstd2, z2, "rstd2_done", "z2_done", "z2_tr")
                    if h in (7, 9) and s.has(1):
                        a = (h - 7) // 2
                        s.wait(dve, S["qkv_mm"], 1, 2, a + 1)
                        s.wait(dve, S["v_done"], 0, 1, 1)
                        nc.vector.tensor_tensor(qkv[:, a, :], misc[BANK[f"qkv{a}"]][:, 0:384], bqkv_s[:],
                                                ALU.add).then_inc(S["qkv_done"], 1)
                if s.has(0):
                    s.wait(dve, S["max_done"], 0, 16, 16)
                    m = maxima[:].rearrange("p a (h o) -> p (a h) o", o=1)
                    v = q_parts[:].rearrange("p a h r -> p (a h) r")
                    nc.vector.tensor_scalar(v[:, :, PARTS:PARTS + 1], m, -1.0, None, ALU.mult).then_inc(S["shift_high"], 1)
                    s.wait(dve, S["shift_high"], 0, 1, 1)
                    nc.vector.scalar_tensor_tensor(out=v[:, :, PARTS + 1:PARTS + 2], in0=m, scalar=-1.0,
                                                   in1=v[:, :, PARTS:PARTS + 1].bitcast(F32),
                                                   op0=ALU.mult, op1=ALU.subtract).then_inc(S["shifts_done"], 1)
                if s.has(-2):
                    s.wait(dve, S["router_mm"], -2, 1, 1)
                    if s.t == LAST:
                        read_ranks(0, misc[BANK["router"]])
                        place(0)
                        dve.wait_ge(S["ranks_read"], 1)
                    nc.vector.tensor_copy(s.pick(logits[:], 1, -2),
                                          misc[BANK["router"]][:, 0:TILES * EXPERTS]).then_inc(S["logits_done"], 1)

            steps(dve, emit)

            dve.wait_ge(S["pv_mm"], 4 * B)
            dve.wait_ge(S["router_mm"], B)
            dve.wait_ge(S["z2_tr"], B)
            dve.wait_ge(S["rows_done"], B)
            dve.wait_ge(S["x1_kept"], B)
            dve.wait_ge(S["logits_done"], B)
            find_top(range(GROUP_FROM[1], NTILES))
            choose(1)
            read_ranks(1, ps_max[0])
            place(1)
            dve.wait_ge(S["expert_done"], 2)
            dve.wait_ge(S["loaded_c"], 64)

            def stage(i, u):
                e = dve.value_load(expert_at(i, u), min_val=0, max_val=EXPERTS - 1)
                if not (isinstance(i, int) and i * RING + u < 3):
                    dve.wait_ge(S["gelu_done"], i * (RING * HC) + (u - 2) * HC)
                nc.vector.tensor_copy(staged[u % 3], wfc_s[:, bass.ds(e, 1), :].rearrange("p o c -> p (o c)")
                                      ).then_inc(S["staged_done"], 1)

            def turned_out(i, u):
                dve.wait_ge(S["x_turned"], i * RING + (u + 1))
                if not (isinstance(i, int) and i * RING + u < 2):
                    dve.wait_ge(S["up_mm"], i * RING + (u - 1))
                nc.vector.tensor_copy(row_t[u % 2], misc[u % 2][:, 0:P]).then_inc(S["row_t_done"], 1)

            def weighted(i, u):
                dve.wait_ge(S["down_mm"], i * RING + (u + 3))
                if not (isinstance(i, int) and i * RING + u < 2):
                    dve.wait_ge(S["y_done"], i * RING + (u - 1))
                nc.vector.tensor_tensor(y_biased[u % 2], ps_pv[u % 2][:, 0:D], staged[u % 3][:, HID + HC:], ALU.add
                                        ).then_inc(S["y_biased"], 1)
                dve.wait_ge(S["y_biased"], i * RING + (u + 1))
                if not (isinstance(i, int) and i == 0):
                    dve.wait_ge(y_sent[u], i * 16)
                nc.vector.tensor_scalar(y_out[u], y_biased[u % 2], row_in[u][:, D:D + 1], None, ALU.mult).then_inc(S["y_done"], 1)

            def final(b):
                n = b // 4
                if b % 4 == 0:
                    dve.wait_ge(pairs_in[n], 64)
                yp = y_pair[n % 2][:, b % 4]
                nc.vector.tensor_tensor(y_sum[b % 2], yp[:, :, 0, :], yp[:, :, 1, :], ALU.add).then_inc(S["y_summed"], 1)
                dve.wait_ge(S["y_summed"], b + 1)
                gate = gates[:, b, D:2 * D].rearrange("p (o d) -> p o d", o=1).broadcast_to([P, TILES, D])
                nc.vector.tensor_tensor(y_gated[b % 2], y_sum[b % 2], gate, ALU.mult).then_inc(S["y_gated"], 1)
                dve.wait_ge(S["y_gated"], b + 1)
                nc.vector.tensor_tensor(x1[:, b], y_gated[b % 2], x1[:, b], ALU.add).then_inc(S["final_done"], 1)

            def tile(i, u):
                if not (isinstance(i, int) and i * RING + u + 2 >= ALL_ROW_TILES):
                    stage(i, u + 2)
                    turned_out(i, u + 2)
                weighted(i, u)

            for u in range(2):
                stage(0, u)
                turned_out(0, u)
            for u in range(RING):
                tile(0, u)
            with dve.Fori(1, FIRST_ROUNDS + 1) as i:
                for u in range(RING):
                    tile(i, u)
            for i in range(FIRST_ROUNDS + 1, ROUNDS):
                for u in range(RING):
                    tile(i, u)
                    if u in (2, 3, 4, 5):
                        final(4 * (i - FIRST_ROUNDS - 1) + u - 2)
            for b in range(B - 4, B):
                final(b)

        @block.tensor
        def _(pe):
            def take(name, s):
                prev = before(name, s)
                if prev:
                    who, d = prev
                    sem_name, per, k = freed[who]
                    s.wait(pe, S[sem_name], d, per, k)
                return misc[BANK[name]]

            def rank(group, bank):
                pe.wait_ge(S["chosen_done"], group + 1)
                nt = GROUP_TILES[group]
                at = GROUP_FROM[group] + group
                nc.tensor.matmul(bank[:, RANKS_AT:RANKS_AT + (nt + 1) * EXPERTS], strict[:],
                                 chosen[:, at:at + nt + 1].rearrange("p n e -> p (n e)"),
                                 start=True, stop=False, skip_group_check=True)
                for n in range(nt):
                    later = nt - n
                    last = nc.tensor.matmul(
                        bank[:, RANKS_AT + (n + 1) * EXPERTS:RANKS_AT + (nt + 1) * EXPERTS].rearrange("p (n e) -> p n e", e=EXPERTS),
                        ones[:], chosen[:, at + n:at + n + 1, :].broadcast_to([P, later, EXPERTS]),
                        start=False, stop=(n == nt - 1), skip_group_check=True)
                last.then_inc(S["rank_mm"], 1)

            pe.wait_ge(S["silu_done"], 1)
            for n, j in enumerate((0, 1, 3, 4)):
                last = nc.tensor.matmul(ps_max[0][:, n * B:(n + 1) * B], wmod_s[:, j * D:(j + 1) * D], c_silu[:],
                                        start=True, stop=True)
            last.then_inc(S["mod_mm"], 1)
            for n, j in enumerate((2, 5, 4, 3)):
                last = nc.tensor.matmul(ps_max[1][0:B, n * D:(n + 1) * D], c_silu[:], wmod_s[:, j * D:(j + 1) * D],
                                        start=True, stop=True)
            last.then_inc(S["gate_mm"], 1)
            pe.wait_ge(S["masks_ready"], 7)
            pe.wait_ge(S["zeroed"], 8)

            def emit(s):
                def spread(which, n, parts, sem_name, d):
                    bank = take(f"{which}{n}", s)
                    for g in range(2):
                        for a in range(TILES):
                            src = parts[:, a, 4 * (2 * n + g):4 * (2 * n + g) + 4, :].rearrange("p h r -> p (h r)").bitcast(F32)
                            last = nc.tensor.transpose(bank[:, g * T + a * P:g * T + (a + 1) * P], src, ident_s[:])
                    last.then_inc(S[sem_name], 1)

                def scores_for_max(h):
                    if h >= 2:
                        s.wait(pe, S["max_done"], 0, 16, h - 1)
                    else:
                        s.wait(pe, S["max_done"], -1, 16, 15 + h)
                    if s.t == 0 and h == 0:
                        pe.wait_ge(S["mod_done"], 4)
                        pe.wait_ge(S["size_done"], 1)
                        pe.wait_ge(S["gate_done"], 3)
                    if h % 8 == 0:
                        s.wait(pe, S["k_stacked"], 0, 2, h // 8 + 1)
                        s.wait(pe, S["q_stacked"], 0, 2, h // 8 + 1)
                    g = h // 4
                    rows = slice(ROWS * (h % 4), ROWS * (h % 4) + PARTS)
                    ks = k_stack[s.t % 2][rows, g, :]
                    bank = ps_max[h % 2]
                    blocks = bank[:].rearrange("p (c k) -> p c k", k=P)
                    nc.tensor.matmul(blocks[:, 0:4:3, :], q_stack[rows, g, 0:P], ks.rearrange("p (c k) -> p c k", k=P),
                                     start=True, stop=False, skip_group_check=True)
                    nc.tensor.matmul(bank[:, P:3 * P], q_stack[rows, g, P:2 * P], ks,
                                     start=False, stop=False, skip_group_check=True)
                    nc.tensor.matmul(blocks[:, 0:4:2, :], ident_b[:], mask_q[:],
                                     start=False, stop=True, skip_group_check=True).then_inc(S["max_mm"], 1)

                def scores(h):
                    if h % 8 == 0:
                        s.wait(pe, S["qm_stacked"], -1, 2, h // 8 + 1)
                    if h >= 2:
                        s.wait(pe, S["exp_done"], -1, 16, h - 1)
                    else:
                        s.wait(pe, S["exp_done"], -2, 16, 15 + h)
                    g = h // 4
                    r = ROWS * (h % 4)
                    rows = slice(r, r + PARTS + 2)
                    ks = k_stack[(s.t - 1) % 2]
                    bank = ps_sc[h % 2]
                    nc.tensor.matmul(bank[:, 0:T], ks[rows, g, 0:P], qm_stack[rows, g, :],
                                     start=True, stop=False, skip_group_check=True)
                    late = qm_stack[rows, g, P:2 * P].rearrange("p (o q) -> p o q", o=1).broadcast_to([PARTS + 2, 2, P])
                    nc.tensor.matmul(bank[:, T:2 * T].rearrange("p (c k) -> p c k", k=P), ks[rows, g, P:2 * P], late,
                                     start=False, stop=False, skip_group_check=True)
                    nc.tensor.matmul(bank[:].rearrange("p (c k) -> p c k", k=P)[:, 0:4:2, :], ident_b[:], mask_k[:],
                                     start=False, stop=True, skip_group_check=True).then_inc(S["score_mm"], 1)

                def weigh(g):
                    s.wait(pe, S["exp_done"], -1, 16, 4 * g + 4)
                    if g == 0:
                        s.wait(pe, S["v_done"], -1, 1, 1)
                    if g >= 2:
                        s.wait(pe, S["heads_done"], -1, 4, g - 1)
                    else:
                        s.wait(pe, S["heads_done"], -2, 4, g + 3)
                    vw = v_wide[(s.t - 1) % 2]
                    for a in range(TILES):
                        for w in range(4):
                            h = 4 * g + w
                            rows = slice(ROWS * w, ROWS * (w + 1))
                            last = nc.tensor.matmul(
                                ps_pv[g % 2][rows, a * P:T], vw[:, a, h, :],
                                probs[:, h % 8, 0:T] if a == 0 else probs[:, h % 8, T:T + P],
                                start=(a == 0), stop=(a == 1), skip_group_check=True)
                    last.then_inc(S["pv_mm"], 1)

                def fill(name):
                    if name[:2] == "qm":
                        s.wait(pe, S["shifts_done"], -1, 1, 1)
                        spread("qm", int(name[2]), q_parts, "qm_tr", -1)
                        return
                    if name in ("k0", "k1", "q0", "q1"):
                        which = name[0]
                        s.wait(pe, S[f"{which}_low"], 0, 1, 1)
                        spread(which, int(name[1]), k_parts if which == "k" else q_parts, f"{which}_tr", 0)
                        return
                    if name[:5] == "heads":
                        a = int(name[5])
                        s.wait(pe, S["heads_done"], -2, 4, 4)
                        bank = take(name, s)
                        for g in range(GROUPS):
                            last = nc.tensor.transpose(bank[:, g * P:(g + 1) * P],
                                                       heads_t[s.t % 2][:, g, a * P:(a + 1) * P], ident_s[:])
                        last.then_inc(S["heads_tr"], 1)
                    elif name == "attnT":
                        s.wait(pe, S["attn_done"], -2, 2, 2)
                        bank = take(name, s)
                        for a in range(TILES):
                            last = nc.tensor.transpose(bank[:, a * P:(a + 1) * P],
                                                       attn[:, a].rearrange("p h d -> p (h d)"), ident_s[:])
                        last.then_inc(S["attn_tr"], 1)
                    elif name == "zT":
                        s.wait(pe, S["z_done"], 1, 2, 2)
                        bank = take(name, s)
                        for a in range(TILES):
                            last = nc.tensor.transpose(bank[:, a * P:(a + 1) * P], z[:, a, :], ident_s[:])
                        last.then_inc(S["zt_done"], 1)
                    elif name == "wo":
                        s.wait(pe, S["attn_t_done"], -2, 1, 1)
                        bank = take(name, s)
                        if s.t == 2:
                            pe.wait_ge(S["loaded_w"], 48)
                        for a in range(TILES):
                            last = nc.tensor.matmul(bank[:, a * D:(a + 1) * D], attn_t[:, a * P:(a + 1) * P], wo_s[:],
                                                    start=True, stop=True)
                        last.then_inc(S["wo_mm"], 1)
                    elif name[:3] == "qkv":
                        a = int(name[3])
                        s.wait(pe, S["ht_done"], 1, 1, 1)
                        bank = take(name, s)
                        nc.tensor.matmul(bank[:, 0:384], h_t[:, a * P:(a + 1) * P], wqkv_s[:],
                                         start=True, stop=True).then_inc(S["qkv_mm"], 1)
                    elif name == "z2T":
                        s.wait(pe, S["z2_done"], -2, 2, 2)
                        bank = take(name, s)
                        for a in range(TILES):
                            last = nc.tensor.transpose(bank[:, a * P:(a + 1) * P], z2[:, a, :], ident_s[:])
                        last.then_inc(S["z2_tr"], 1)
                    elif name == "router":
                        s.wait(pe, S["h2_done"], -2, 1, 1)
                        bank = take(name, s)
                        for a in range(TILES):
                            last = nc.tensor.matmul(bank[:, a * EXPERTS:(a + 1) * EXPERTS], h2_now[:, a * P:(a + 1) * P],
                                                    router_s[:], start=True, stop=True)
                        last.then_inc(S["router_mm"], 1)
                        if s.t == LAST:
                            rank(0, bank)

                for h in range(-1, HEADS):
                    if h >= 0 and s.has(-1):
                        scores(h)
                        if h % 4 == 1 and h > 4:
                            weigh(h // 4 - 1)
                    for name, d in USES.get(h, []):
                        if s.has(d):
                            fill(name)
                    if MAX_FROM <= h < MAX_FROM + 8 and s.has(0):
                        scores_for_max(2 * (h - MAX_FROM))
                        scores_for_max(2 * (h - MAX_FROM) + 1)
                if s.has(-1):
                    weigh(3)

            steps(pe, emit)

            rank(1, ps_max[0])

            pe.wait_ge(S["loaded_c"], 64)
            pe.wait_ge(S["expert_done"], 2)
            pe.wait_ge(S["exp_done"], B * 16)
            pe.wait_ge(S["heads_done"], B * 4)
            pe.sem_inc(S["down_mm"], 2)

            def turn(i, u):
                n = u // RING + 1
                pe.wait_ge(row_loaded[u % RING], i * 16 + 16 * n)
                if not (isinstance(i, int) and i * RING + u < 2):
                    pe.wait_ge(S["row_t_done"], i * RING + (u - 1))
                nc.tensor.transpose(misc[u % 2][:, 0:P], row_in[u % RING][:, 0:D], ident_s[:]).then_inc(S["x_turned"], 1)

            def up(i, u):
                pe.wait_ge(S["row_t_done"], i * RING + (u + 1))
                pe.wait_ge(S["staged_done"], i * RING + (u + 1))
                if not (isinstance(i, int) and i * RING + u < 2):
                    pe.wait_ge(S["gelu_done"], i * (RING * HC) + (u - 1) * HC)
                for hc in range(HC):
                    last = nc.tensor.matmul(ps_sc[u % 2][:, hc * P:(hc + 1) * P], staged[u % 3][:, hc * P:(hc + 1) * P],
                                            row_t[u % 2], start=True, stop=True)
                last.then_inc(S["up_mm"], 1)

            def down(i, u):
                e = pe.value_load(expert_at(i, u), min_val=0, max_val=EXPERTS - 1)
                if not (isinstance(i, int) and i * RING + u < 2):
                    pe.wait_ge(S["y_biased"], i * RING + (u - 1))
                for hc in range(HC):
                    pe.wait_ge(S["gelu_done"], i * (RING * HC) + (u * HC + hc + 1))
                    last = nc.tensor.matmul(ps_pv[u % 2][:, 0:D], act[u % 2][:, hc, :],
                                            wproj_s[:, bass.ds(e, 1), hc, :].rearrange("p o d -> p (o d)"),
                                            start=(hc == 0), stop=(hc == HC - 1))
                last.then_inc(S["down_mm"], 1)

            def tile(i, u):
                left = ALL_ROW_TILES - (i * RING + u) if isinstance(i, int) else ALL_ROW_TILES
                if left > 1:
                    up(i, u + 1)
                if left > 2:
                    turn(i, u + 2)
                down(i, u)

            turn(0, 0)
            turn(0, 1)
            up(0, 0)
            for u in range(RING):
                tile(0, u)
            with pe.Fori(1, ROUNDS - 1) as i:
                for u in range(RING):
                    tile(i, u)
            for u in range(RING):
                tile(ROUNDS - 1, u)


def kernel(**inputs):
    import concourse.bacc as _bacc
    from concourse.bass_utils import run_bass_kernel_spmd as _run

    f = {k: np.asarray(v) for k, v in inputs.items()}
    half = DK // 2
    freq = 1.0 / 10000.0 ** (2.0 * np.arange(half, dtype=np.float32) / DK)
    angles = np.arange(T, dtype=np.float32)[:, None] * freq[None, :].astype(np.float32)
    cos = np.cos(angles).astype(np.float32)
    sin = np.sin(angles).astype(np.float32)

    def table(first, second):
        row = np.concatenate([first, second], 1)
        return np.tile(row, (1, 2 * HEADS)).reshape(TILES, P, 256).transpose(1, 0, 2)

    after = np.triu(np.full((P, P), MASKED, np.float32), 1)
    arrays = {
        "x": f["L0_attn_x"],
        "c_t": f["L0_c"].T,
        "wmod": f["L0_wmod"],
        "wqkv": np.concatenate([f["L0_attn_WQ_w"].T, f["L0_attn_WK_w"].T, f["L0_attn_WV_w"].T], 1),
        "bqkv": np.concatenate([f["L0_attn_WQ_b"], f["L0_attn_WK_b"], f["L0_attn_WV_b"]])[None],
        "wo": f["L0_attn_Wo_w"].T,
        "bo": f["L0_attn_Wo_b"][None],
        "router": f["L0_ffn_router_w"].T,
        "w_fc": f["L0_ffn_w_fc"].transpose(1, 0, 2),
        "b_fc": f["L0_ffn_b_fc"].reshape(EXPERTS, HC, P).transpose(2, 0, 1),
        "w_proj": f["L0_ffn_w_proj"].reshape(EXPERTS, HC, P, D).transpose(2, 0, 1, 3),
        "b_proj": f["L0_ffn_b_proj"].reshape(1, EXPERTS, D),
        "cos": table(cos, cos),
        "sin": table(-sin, sin),
        "ident": np.eye(P, dtype=np.float32),
        "causal": np.stack([after, after.T], 1),
        "route": np.concatenate([
            np.arange(EXPERTS), np.tril(np.ones((EXPERTS, EXPERTS)), -1).ravel(), np.arange(NTILES) * P,
            np.arange(ALL_ROW_TILES)]).astype(np.float32)[None],
        "places": np.arange(NTILES * P * 2, dtype=np.uint32).reshape(NTILES, P, 2).transpose(1, 2, 0),
        "blank": np.array([[0] * (D + 1) + [SKIPPED]], np.uint32),
    }
    nc = _bacc.Bacc("TRN2", target_bir_lowering=False, num_devices=1)
    feeds, args = {}, []
    for name, a in arrays.items():
        a = np.ascontiguousarray(a)
        feeds[f"in_{name}"] = a
        args.append(nc.dram_tensor(f"in_{name}", a.shape, mybir.dt.from_np(a.dtype), kind="ExternalInput").ap())
    args.append(nc.dram_tensor("out", (B, T, D), F32, kind="ExternalOutput").ap())
    block_program(nc, *args)
    return _run(nc, [feeds], core_ids=[0]).results[0]["out"]
```

```python
from contextlib import ExitStack

import numpy as np

import concourse.bass as bass
from concourse import mybir

F32 = mybir.dt.float32
F32R = mybir.dt.float32r
BF16 = mybir.dt.bfloat16
U32 = mybir.dt.uint32
I32 = mybir.dt.int32
ALU = mybir.AluOpType
ACT = mybir.ActivationFunctionType
AX = mybir.AxisListType.X

B, T, D = 16, 256, 128
HEADS, DK = 16, 8
P = 128
TILES = T // P
GROUPS = HEADS // 4
ROWS = 32
PARTS = 3 * DK
EXPERTS, HID = 8, 512
HC = HID // P
NTILES = B * TILES
EPS = 1e-5
SCALE = float(DK) ** -0.5
MASKED = -1.0e30

FIRST, LAST = 4, 14
assert (LAST - FIRST) % 2 == 0

GROUP_B = (LAST - 2, B - (LAST - 2))
GROUP_TILES = [n * TILES for n in GROUP_B]
GROUP_FROM = [0, GROUP_TILES[0]]
ROW_TILES = [2 * n + EXPERTS - 1 for n in GROUP_TILES]
ROW_FROM = [0, ROW_TILES[0]]
ALL_ROW_TILES = sum(ROW_TILES)
RING = 6
ROUNDS = ALL_ROW_TILES // RING
assert ALL_ROW_TILES % RING == 0
FIRST_ROUNDS = (ROW_TILES[0] - 1) // RING
ROW = D + 2
SKIPPED = 1 << 20
ROUTE_LEN = EXPERTS + EXPERTS * EXPERTS + NTILES + ALL_ROW_TILES
RANKS_AT = 64
ROUTE_STEPS = 16
STAGE = HID + HC + D


class Step:

    def __init__(self, t, i=None, u=0):
        self.t, self.i, self.u = t, i, u

    def has(self, d):
        return 0 <= self.t + d < B

    def value(self, d, per, n):
        first = (self.t + d) * per + n
        if self.i is None:
            return first
        return self.i * (2 * per) + first

    def wait(self, eng, sem, d, per, n):
        if self.t + d >= 0:
            eng.wait_ge(sem, self.value(d, per, n))

    def slot_wait(self, eng, sems, d):
        b = self.t + d
        n = 16 * (b // 2 + 1)
        eng.wait_ge(sems[b % 2], n if self.i is None else self.i * 16 + n)

    def hold(self, eng, sem, d, per, n, passed):
        if self.t + d >= 0:
            eng.wait_ge(sem, self.value(d, per, n))
            if self.i is not None:
                eng.sem_inc(passed, 1)

    def pick(self, ap, axis, d):
        b = self.t + d
        if self.i is None:
            index = [slice(None)] * len(ap.shape)
            index[axis] = b
            return ap[tuple(index)]
        names = [f"x{n}" for n in range(len(ap.shape))]
        left = " ".join("(tt uu)" if n == axis else x for n, x in enumerate(names))
        right = " ".join("tt uu" if n == axis else x for n, x in enumerate(names))
        v = ap.rearrange(f"{left} -> {right}", uu=2)
        index = [slice(None)] * len(v.shape)
        index[axis] = bass.ds(self.i + b // 2, 1)
        index[axis + 1] = b % 2
        v = v[tuple(index)]
        names = [f"y{n}" for n in range(len(v.shape))]
        new = names[:axis] + [f"(y{axis} y{axis + 1})"] + names[axis + 2:]
        return v.rearrange(f"{' '.join(names)} -> {' '.join(new)}")


def steps(eng, emit):
    for t in range(-1, FIRST):
        emit(Step(t))
    with eng.Fori(0, (LAST - FIRST) // 2) as i:
        for u in range(2):
            emit(Step(FIRST + u, i, u))
    for t in range(LAST, B + 2):
        emit(Step(t))


USES = {
    -1: [('qm0', -1), ('qm1', -1)],
    1: [('heads0', -2)],
    2: [('heads1', -2)],
    3: [('k0', 0), ('q0', 0), ('k1', 0)],
    4: [('attnT', -2)],
    5: [('q1', 0)],
    6: [('wo', -2)],
    7: [('zT', 1)],
    8: [('qkv0', 1)],
    9: [('qkv1', 1)],
    12: [('z2T', -2)],
    14: [('router', -2)],
}
MISC = [use for slot in sorted(USES) for use in USES[slot]]
RESIDUAL_AT, QKV_AT, NORMALISE_AT = 7, (7, 8), 10
TILES_AT = max(slot for slot in USES for name, _ in USES[slot] if name == "heads1") + 1
TILES_IN = HEADS - TILES_AT
LONE = 3
assert TILES_IN + 2 < LONE * RING
MAX_AT = {5: (0, 1,), 6: (2, 3,), 7: (4, 5,), 8: (6, 7,), 9: (8, 9,), 10: (10, 11,), 11: (12, 13,), 12: (14, 15,)}
BANK = {name: n % 2 for n, (name, _) in enumerate(MISC)}


def before(name, s):
    at = [n for n, (x, _) in enumerate(MISC) if x == name][0]
    bank = at % 2
    for back in range(0, 3):
        for n in range(len(MISC) - 1, -1, -1):
            if n % 2 != bank or (back == 0 and n >= at):
                continue
            x, d = MISC[n]
            if 0 <= s.t - back + d < B:
                return x, d - back
    return None


def block_program(nc, x, c_t, wmod, wqkv, bqkv, wo, bo, router, w_fc, b_fc, w_proj, b_proj,
                  cos, sin, ident, causal, route, places, blank, out):
    with ExitStack() as ctx:
        def sb(name, shape, dt=F32):
            return ctx.enter_context(nc.sbuf_tensor(name, shape, dt))

        def psum(name):
            return ctx.enter_context(nc.psum_tensor(name, [P, 512], F32))

        def sem(name):
            return ctx.enter_context(nc.semaphore(name))

        def parted(name, shapes):
            sizes = [int(np.prod(shape)) for shape in shapes]
            whole = sb(name, [P, sum(sizes)])
            parts, at = [], 0
            for shape, size in zip(shapes, sizes):
                dims = [f"x{n}" for n in range(len(shape))]
                kw = {d: v for d, v in zip(dims[1:], shape[1:])}
                parts.append(whole[:, at:at + size].rearrange(f"p ({' '.join(dims)}) -> p {' '.join(dims)}", **kw))
                at += size
            return whole, parts

        early_a, (cos_s, rope_a, rope_b, roped) = parted("early_a", [(TILES, 256)] * 4)
        early_b, (sin_s, proj_b, proj_g, z, z2, x1_now, h2_now) = parted(
            "early_b", [(TILES, 256)] + [(TILES, D)] * 5 + [(T,)])
        ident_s = sb("ident_s", [P, P])
        ident_b = sb("ident_b", [P, P], BF16)
        causal_s = sb("causal_s", [P, 2, P])
        mask_q = sb("mask_q", [P, 2, P], BF16)
        mask_k = sb("mask_k", [P, 2, P], BF16)
        wqkv_s = sb("wqkv_s", [P, 384])
        bqkv_s = sb("bqkv_s", [P, 384])
        wo_s = sb("wo_s", [P, P])
        bo_s = sb("bo_s", [P, P])
        router_s = sb("router_s", [P, EXPERTS])
        wfc_s = sb("wfc_s", [P, EXPERTS, STAGE])
        wproj_s = sb("wproj_s", [P, EXPERTS, HC, P])
        route_s = sb("route_s", [P, ROUTE_LEN])
        places_s = sb("places_s", [P, 2, NTILES], U32)
        blank_s = sb("blank_s", [P, ROW], U32)
        half_s = sb("half_s", [P, TILES])
        c_s = sb("c_s", [P, B])
        c_exp = sb("c_exp", [P, B])
        c_den = sb("c_den", [P, B])
        c_sig = sb("c_sig", [P, B])
        c_silu = sb("c_silu", [P, B])
        mod = sb("mod", [P, B, 4])
        gate_sign = sb("gate_sign", [B, 2 * D])
        gate_neg = sb("gate_neg", [B, 2 * D])
        gate_size = sb("gate_size", [B, 2 * D])
        gate_row = sb("gate_row", [B, 4 * D])
        gates = sb("gates", [P, B, 4 * D])
        x_in = [sb(f"x_in{n}", [P, TILES, D]) for n in range(2)]
        stats = sb("stats", [P, TILES, 6])
        moments = sb("moments", [P, TILES, 2])
        var_eps = sb("var_eps", [P, TILES])
        rstd = sb("rstd", [P, TILES])
        h_t = sb("h_t", [P, T])
        qkv = sb("qkv", [P, TILES, 384])
        q_parts = sb("q_parts", [P, TILES, HEADS, ROWS], F32R)
        k_parts = sb("k_parts", [P, TILES, HEADS, ROWS], F32R)
        v_wides = sb("v_wides", [P, 2, TILES, HEADS, ROWS])
        v_wide = [v_wides[:, n] for n in range(2)]
        q_stack = sb("q_stack", [P, GROUPS, T], F32R)
        k_stacks = sb("k_stacks", [P, 2, GROUPS, T], F32R)
        k_stack = [k_stacks[:, n] for n in range(2)]
        maxima = sb("maxima", [P, TILES, HEADS])
        qm_stack = sb("qm_stack", [P, GROUPS, T], F32R)
        probs = sb("probs", [P, 8, 384])
        heads_ts = sb("heads_ts", [P, 2, GROUPS, T])
        heads_t = [heads_ts[:, n] for n in range(2)]
        x_res = [sb(f"x_res{n}", [P, TILES, D]) for n in range(2)]
        rsum = sb("rsum", [P, TILES, HEADS])
        attn = sb("attn", [P, TILES, HEADS, DK])
        attn_t = sb("attn_t", [P, T])
        x1 = sb("x1", [P, B, TILES, D])
        stats2 = sb("stats2", [P, TILES, 6])
        moments2 = sb("moments2", [P, TILES, 2])
        var_eps2 = sb("var_eps2", [P, TILES])
        rstd2 = sb("rstd2", [P, TILES])
        row_scaled = sb("row_scaled", [P, TILES, D])
        rows = sb("rows", [P, NTILES, ROW])
        logits = sb("logits", [P, B, TILES * EXPERTS])
        top = sb("top", [P, NTILES, 8])
        top_at = sb("top_at", [P, NTILES, 8], U32)
        top_f = sb("top_f", [P, NTILES, 2])
        gap = sb("gap", [P, NTILES])
        gap_exp = sb("gap_exp", [P, NTILES])
        gap_den = sb("gap_den", [P, NTILES])
        share = sb("share", [P, 2, NTILES])
        hot = sb("hot", [P, 2, NTILES, EXPERTS])
        strict = sb("strict", [P, P], BF16)
        ones = sb("ones", [P, P], BF16)
        chosen = sb("chosen", [P, NTILES + 2, EXPERTS], BF16)
        ranks = sb("ranks", [P, NTILES + 2, EXPERTS])
        tiles_of = sb("tiles_of", [P, EXPERTS])
        ahead = sb("ahead", [P, EXPERTS, EXPERTS])
        base_0 = sb("base_0", [P, EXPERTS])
        base = sb("base", [P, EXPERTS])
        slot_all = sb("slot_all", [P, NTILES, EXPERTS])
        slot_hot = sb("slot_hot", [P, 2, NTILES, EXPERTS])
        over = slot_hot[:, 0].rearrange("p n e -> p (n e)").rearrange("p (e n) -> p e n", e=EXPERTS)
        slot_f = sb("slot_f", [P, 2, NTILES])
        slots = sb("slots", [P, 2, NTILES], U32)
        reached = slot_hot[0:1].rearrange("p k n e -> p (k n e)")[:, 0:ROW_TILES[0] * EXPERTS].rearrange("p (n e) -> p n e", e=EXPERTS)
        reached_n = sb("reached_n", [1, ALL_ROW_TILES])
        expert_of = sb("expert_of", [1, ALL_ROW_TILES], I32)

        def over_of(t, size):
            flat = t[:].rearrange("p " + " ".join(f"x{n}" for n in range(len(t.shape) - 1)) + " -> p ("
                                  + " ".join(f"x{n}" for n in range(len(t.shape) - 1)) + ")")
            return flat[:, 0:size]

        wmod_s = over_of(heads_ts, 6 * D)
        staged_all = over_of(v_wides, 3 * STAGE).rearrange("p (n c) -> p n c", n=3)
        staged = [staged_all[:, n] for n in range(3)]
        act_sums = over_of(early_a, 2 * HID + 4 * T)
        act_all = act_sums[:, 0:2 * HID].rearrange("p (n c t) -> p n c t", n=2, c=HC)
        act = [act_all[:, n] for n in range(2)]
        small = over_of(probs, RING * ROW + 3 * HID)
        row_in_all = small[:, 0:RING * ROW].rearrange("p (n r) -> p n r", n=RING)
        row_in = [row_in_all[:, n] for n in range(RING)]
        proj_all = small[:, RING * ROW:].rearrange("p (n c d) -> p n c d", n=3, c=HC)
        staged_proj = [proj_all[:, n] for n in range(3)]
        y_out_all = over_of(qkv, RING * D).rearrange("p (n d) -> p n d", n=RING)
        y_out = [y_out_all[:, n] for n in range(RING)]
        row_t = [x_in[0][:, n, :] for n in range(2)]
        y_bias = [x_in[1][:, 0, :], x_in[1][:, 1, :], x_res[0][:, 0, :]]
        y_pair = [over_of(t, 8 * T).rearrange("p (b a k d) -> p b a k d", b=4, a=TILES, k=2)
                  for t in (heads_ts, early_b)]
        sums = act_sums[:, 2 * HID:].rearrange("p (n a d) -> p n a d", n=4, a=TILES)
        y_sum = [sums[:, n] for n in range(2)]
        y_gated = [sums[:, 2 + n] for n in range(2)]

        misc = [psum(f"misc{n}") for n in range(2)]
        ps_max = [psum(f"ps_max{n}") for n in range(3)]
        ps_sc = [psum(f"ps_sc{n}") for n in range(2)]
        ps_pv = psum("ps_pv")
        ps_y = [ps_pv, ps_max[1]]

        gate_dram = nc.dram_tensor("gate_rows", [B, 4 * D], F32).ap()
        sorted_dram = nc.dram_tensor("sorted_rows", [ALL_ROW_TILES * P, ROW], F32).ap()
        result_dram = nc.dram_tensor("results", [B * T * 2, D], F32).ap()

        names = """loaded_a loaded_b loaded_c loaded_o loaded_w gate_out gate_in zeroed
        masks_ready c_exp_done c_den_done c_sig_done silu_done mod_mm gate_mm mod_done sign_done neg_done size_done gate_done
        stats_done moments_done eps_done rstd_done z_done zt_done ht_done qkv_mm qkv_done
        rope_done roped_done q_high k_high q_low k_low k_tr q_tr k_stacked q_stacked v_done
        max_mm max_done shift_high shifts_done qm_tr qm_stacked score_mm exp_done pv_mm heads_done
        heads_tr rsum_done attn_done attn_tr attn_t_done wo_mm wo_bias wo_gated x1_done x1_kept dve_passed pool_passed
        stats2_done moments2_done eps2_done rstd2_done z2_done z2_tr h2_done router_mm logits_done
        row_scaled rows_done blank_out top_done at_done gap_done gap_exp_done route_step shared
        chosen_done rank_mm ranks_read slots_done sorted_a sorted_b expert_done
        staged_done x_turned row_t_done up_mm gelu_done down_mm y_done
        y_summed y_gated final_done written sp_passed tails_done""".split()
        S = {n: sem(n) for n in names}
        x_loaded = [sem(f"x_loaded{n}") for n in range(2)]
        xres_loaded = [sem(f"xres_loaded{n}") for n in range(2)]
        row_loaded = [sem(f"row_loaded{n}") for n in range(RING)]
        y_sent = [sem(f"y_sent{n}") for n in range(RING)]
        pairs_in = [sem(f"pairs_in{n}") for n in range(B // 4)]

        freed = {
            "qm0": ("qm_stacked", 2, 1), "qm1": ("qm_stacked", 2, 2),
            "heads0": ("attn_done", 2, 1), "heads1": ("attn_done", 2, 2),
            "k0": ("k_stacked", 2, 1), "k1": ("k_stacked", 2, 2),
            "q0": ("q_stacked", 2, 1), "q1": ("q_stacked", 2, 2),
            "attnT": ("attn_t_done", 1, 1), "zT": ("ht_done", 1, 1), "wo": ("wo_bias", 1, 1),
            "qkv0": ("qkv_done", 2, 1), "qkv1": ("qkv_done", 2, 2),
            "z2T": ("h2_done", 1, 1), "router": ("logits_done", 1, 1),
        }

        block = ctx.enter_context(nc.Block())

        x_v = x.rearrange("b (a p) d -> b p a d", p=P)
        out_v = out.rearrange("b (a p) d -> p b a d", p=P)
        rows_v = rows[:].rearrange("p (b a) r -> p b a r", a=TILES)
        pair_v = result_dram.rearrange("(b a p k) d -> p b a (k d)", a=TILES, p=P, k=2)
        iota_r = route_s[:, 0:EXPERTS]
        before_r = route_s[:, EXPERTS:EXPERTS + EXPERTS * EXPERTS]
        full_r = route_s[:, EXPERTS + EXPERTS * EXPERTS:EXPERTS + EXPERTS * EXPERTS + NTILES]
        tile_r = route_s[0:1, EXPERTS + EXPERTS * EXPERTS + NTILES:ROUTE_LEN]

        def expert_at(i, u):
            v = expert_of[:].rearrange("o (i u) -> o i u", u=RING)
            return v[:, bass.ds(i + u // RING, 1), u % RING]

        def halves(v, m):
            return v.rearrange("p a (g f i) -> p a g f i", f=2, i=4)[:, :, :, m, :]

        def round_of(n):
            return n // RING, n % RING

        @block.sync
        def _(sp):
            for dst, src in ((c_s[:], c_t), (wmod_s, wmod)):
                sp.dma_start(dst, src).then_inc(S["loaded_a"], 16)
            sp.dma_start(x_in[0][:], x_v[0]).then_inc(x_loaded[0], 16)
            sp.dma_start(ident_s[:], ident).then_inc(S["loaded_b"], 16)
            for dst, src in (
                (causal_s[:], causal), (wqkv_s[:], wqkv), (bqkv_s[:], bqkv.broadcast_to([P, 384])),
                (cos_s, cos), (sin_s, sin),
            ):
                sp.dma_start(dst, src).then_inc(S["loaded_b"], 16)

            def emit(s):
                if s.has(2):
                    s.wait(sp, S["z_done"], 0, 2, 2)
                    sp.dma_start(x_in[s.t % 2][:], s.pick(x_v, 0, 2)).then_inc(x_loaded[s.t % 2], 16)
                if s.has(-1):
                    s.wait(sp, S["x1_done"], -3, 1, 1)
                    sp.dma_start(x_res[(s.t - 1) % 2][:], s.pick(x_v, 0, -1)).then_inc(xres_loaded[(s.t - 1) % 2], 16)

                if s.t == -1:
                    for dst, src in ((wo_s[:], wo), (bo_s[:], bo.broadcast_to([P, D])), (router_s[:], router)):
                        sp.dma_start(dst, src).then_inc(S["loaded_o"], 16)
                    sp.wait_ge(S["gate_done"], 3)
                    sp.dma_start(gate_dram, gate_row[:]).then_inc(S["gate_out"], 16)
                if s.t == 0:
                    sp.wait_ge(S["gate_out"], 16)
                    sp.dma_start(gates[:].rearrange("p b d -> p (b d)"),
                                 gate_dram.rearrange("(o b) d -> o (b d)", o=1).broadcast_to([P, B * 4 * D])
                                 ).then_inc(S["gate_in"], 16)
                if s.t == 1:
                    for dst, src in ((route_s[:], route.broadcast_to([P, ROUTE_LEN])), (places_s[:], places),
                                     (blank_s[:], blank.broadcast_to([P, ROW]))):
                        sp.dma_start(dst, src).then_inc(S["loaded_w"], 16)
                    for dst, src in ((wfc_s[:, :, 0:HID], w_fc), (wfc_s[:, :, HID:HID + HC], b_fc)):
                        sp.dma_start(dst, src).then_inc(S["loaded_c"], 16)
                if s.t == 2:
                    for dst, src in ((wproj_s[:], w_proj), (wfc_s[:, :, HID + HC:], b_proj.broadcast_to([P, EXPERTS, D]))):
                        sp.dma_start(dst, src).then_inc(S["loaded_c"], 16)
                if s.t == 3:
                    sp.wait_ge(S["loaded_w"], 48)
                    sp.dma_start(sorted_dram.rearrange("(p t) r -> p t r", p=P),
                                 blank_s[:].bitcast(F32).rearrange("p (o r) -> p o r", o=1).broadcast_to([P, ALL_ROW_TILES, ROW])
                                 ).then_inc(S["blank_out"], 16)

            steps(sp, emit)

            sorted_v = sorted_dram.rearrange("(i u p) r -> p i u r", u=RING, p=P)

            def load_row(i, u):
                if not isinstance(i, int):
                    sp.wait_ge(y_sent[u], i * 16)
                    sp.sem_inc(S["sp_passed"], 1)
                elif i > 0:
                    sp.wait_ge(y_sent[u], 16 * i)
                sp.dma_start(row_in[u], sorted_v[:, bass.ds(i, 1), u, :].rearrange("p i r -> p (i r)")
                             ).then_inc(row_loaded[u], 16)

            def load_pairs(n):
                if n >= 2:
                    sp.wait_ge(S["y_summed"], 4 * (n - 1))
                for b in range(4):
                    sp.dma_start(y_pair[n % 2][:, b].rearrange("p a k d -> p a (k d)"), pair_v[:, 4 * n + b]
                                 ).then_inc(pairs_in[n], 16)

            def store(n):
                sp.wait_ge(S["final_done"], 4 * (n + 1))
                sp.dma_start(out_v[:, 4 * n:4 * n + 4].rearrange("p b a d -> p (b a) d"),
                             x1[:, 4 * n:4 * n + 4].rearrange("p b a d -> p (b a) d")).then_inc(S["written"], 16)

            sp.wait_ge(S["sorted_a"], 16 * 2 * GROUP_TILES[0])
            sp.wait_ge(S["pv_mm"], 4 * B)
            for u in range(RING):
                load_row(0, u)
            with sp.Fori(1, FIRST_ROUNDS) as i:
                for u in range(RING):
                    load_row(i, u)
            sp.wait_ge(S["sorted_b"], 16 * 2 * GROUP_TILES[1])
            for i in range(FIRST_ROUNDS, ROUNDS):
                for u in range(RING):
                    load_row(i, u)
                n = i - FIRST_ROUNDS - 1
                if n == 0:
                    sp.wait_ge(S["heads_tr"], 2 * B)
                    sp.wait_ge(S["router_mm"], B)
                    sp.wait_ge(S["rows_done"], B)
                if n >= 0:
                    load_pairs(n)
                if n >= 1:
                    store(n - 1)
            for n in range(ROUNDS - FIRST_ROUNDS - 2, B // 4 - 1):
                store(n)
            for u in range(RING):
                sp.wait_ge(y_sent[u], 16 * ROUNDS)
            load_pairs(B // 4 - 1)
            for b in range(B - 4, B):
                sp.wait_ge(S["final_done"], b + 1)
                sp.dma_start(out_v[:, b], x1[:, b]).then_inc(S["written"], 16)
            sp.wait_ge(S["written"], 16 * (B // 4 - 1 + 4))

        @block.gpsimd
        def _(pool):
            for n, (t, v) in enumerate((
                (k_parts[:].bitcast(F32), 0.0), (q_parts[:].bitcast(F32), 0.0), (v_wide[0], 0.0), (v_wide[1], 0.0),
            )):
                nc.gpsimd.memset(t, v).then_inc(S["zeroed"], 1)
            nc.gpsimd.memset(half_s[:], -0.5).then_inc(S["zeroed"], 1)
            pool.wait_ge(S["zeroed"], 5)
            nc.gpsimd.memset(k_parts[:, :, :, PARTS:PARTS + 2].bitcast(F32), 1.0).then_inc(S["zeroed"], 1)
            nc.gpsimd.memset(v_wide[0][:, :, :, DK:DK + 1], 1.0).then_inc(S["zeroed"], 1)
            nc.gpsimd.memset(v_wide[1][:, :, :, DK:DK + 1], 1.0).then_inc(S["zeroed"], 1)
            nc.gpsimd.memset(chosen[:], 0.0).then_inc(S["zeroed"], 1)
            pool.wait_ge(S["zeroed"], 9)

            def tails(group, k):
                js = slice(GROUP_FROM[group], GROUP_FROM[group] + GROUP_TILES[group])
                nc.gpsimd.tensor_copy(rows[:, js, D:D + 1].rearrange("p n o -> p (n o)"), share[:, k, js]).then_inc(S["tails_done"], 1)
                nc.gpsimd.tensor_copy(rows[:, js, D + 1:D + 2].bitcast(U32).rearrange("p n o -> p (n o)"),
                                      places_s[:, k, js]).then_inc(S["tails_done"], 1)
                pool.wait_ge(S["tails_done"], 4 * group + 2 * k + 2)

            def sort_rows(group, k, tiles, signal):
                for n in tiles:
                    nc.gpsimd.indirect_dma_start(
                        sorted_dram, bass.IndirectOffsetOnAxis(ap=slots[:, k, n:n + 1], axis=0),
                        rows[:, n, :], None).then_inc(S[signal], 16)

            def send(i, u):
                pool.wait_ge(S["y_done"], i * RING + (u + 1))
                if not isinstance(i, int):
                    pool.sem_inc(S["pool_passed"], 1)
                nc.gpsimd.indirect_dma_start(
                    result_dram, bass.IndirectOffsetOnAxis(ap=row_in[u][:, D + 1:D + 2].bitcast(U32), axis=0),
                    y_out[u], None, bounds_check=B * T * 2 - 1, oob_is_err=False).then_inc(y_sent[u], 16)

            def emit(s):
                if s.t == LAST + 1:
                    pool.wait_ge(S["loaded_w"], 48)
                    pool.wait_ge(S["slots_done"], 1)
                    pool.wait_ge(S["shared"], 2)
                    pool.wait_ge(S["blank_out"], 16)
                    tails(0, 0)
                    sort_rows(0, 0, range(GROUP_TILES[0]), "sorted_a")
                if s.t == LAST + 2:
                    pool.wait_ge(S["sorted_a"], 16 * GROUP_TILES[0])
                    tails(0, 1)
                    sort_rows(0, 1, range(GROUP_TILES[0]), "sorted_a")
                if s.has(0):
                    s.wait(pool, S["qkv_done"], 0, 2, 2)
                    s.hold(pool, S["pv_mm"], -2, 4, 4, S["pool_passed"])
                    if s.t < 2:
                        pool.wait_ge(S["zeroed"], 8)
                    nc.gpsimd.tensor_copy(
                        v_wide[s.t % 2][:, :, :, 0:DK],
                        qkv[:, :, 256:384].rearrange("p a (h d) -> p a h d", h=HEADS)).then_inc(S["v_done"], 1)
                if s.has(1):
                    s.hold(pool, S["moments_done"], 1, 2, 2, S["pool_passed"])
                    nc.gpsimd.tensor_scalar_add(var_eps[:], moments[:, :, 1], EPS).then_inc(S["eps_done"], 1)
                    s.wait(pool, S["eps_done"], 1, 1, 1)
                    s.wait(pool, S["z_done"], 0, 2, 2)
                    nc.gpsimd.tensor_tensor(rstd[:], var_eps[:], half_s[:], ALU.pow).then_inc(S["rstd_done"], 1)
                if s.has(-2):
                    if s.t == B + 1:
                        for n in range(RESIDUAL_AT - TILES_AT):
                            send(*round_of(n))
                    s.hold(pool, S["moments2_done"], -2, 2, 2, S["pool_passed"])
                    nc.gpsimd.tensor_scalar_add(var_eps2[:], moments2[:, :, 1], EPS).then_inc(S["eps2_done"], 1)
                    s.wait(pool, S["eps2_done"], -2, 1, 1)
                    s.wait(pool, S["z2_done"], -3, 2, 2)
                    nc.gpsimd.tensor_tensor(rstd2[:], var_eps2[:], half_s[:], ALU.pow).then_inc(S["rstd2_done"], 1)
                if s.has(-2):
                    if s.t == B + 1:
                        for n in range(RESIDUAL_AT - TILES_AT, NORMALISE_AT - TILES_AT):
                            send(*round_of(n))
                    s.hold(pool, S["x1_done"], -2, 1, 1, S["pool_passed"])
                    nc.gpsimd.tensor_copy(s.pick(x1[:], 1, -2), x1_now).then_inc(S["x1_kept"], 1)
                    s.hold(pool, S["z2_done"], -2, 2, 2, S["pool_passed"])
                    if s.t == 2:
                        pool.wait_ge(S["gate_in"], 16)
                    m = s.pick(gates[:], 1, -2)
                    wide = [P, TILES, D]
                    nc.gpsimd.tensor_tensor(row_scaled[:], z2, m[:, 2 * D:3 * D].rearrange("p (o d) -> p o d", o=1).broadcast_to(wide),
                                            ALU.mult).then_inc(S["row_scaled"], 1)
                    s.hold(pool, S["row_scaled"], -2, 1, 1, S["pool_passed"])
                    nc.gpsimd.tensor_tensor(s.pick(rows_v, 1, -2)[:, :, 0:D], row_scaled[:],
                                            m[:, 3 * D:4 * D].rearrange("p (o d) -> p o d", o=1).broadcast_to(wide),
                                            ALU.add).then_inc(S["rows_done"], 1)
                if s.has(1):
                    s.hold(pool, S["qkv_done"], 1, 2, 2, S["pool_passed"])
                    s.hold(pool, S["roped_done"], 0, 1, 1, S["pool_passed"])
                    if s.t == -1:
                        pool.wait_ge(S["loaded_b"], 96)
                    qk = qkv[:, :, 0:256]
                    nc.gpsimd.tensor_tensor(rope_a, qk, cos_s, ALU.mult).then_inc(S["rope_done"], 1)
                    for n in range(2):
                        for a in range(TILES):
                            nc.gpsimd.tensor_tensor(halves(rope_b, n)[:, a], halves(qk, 1 - n)[:, a],
                                                    halves(sin_s, n)[:, a], ALU.mult).then_inc(S["rope_done"], 1)

            steps(pool, emit)
            rest = NORMALISE_AT - TILES_AT
            for n in range(rest, TILES_IN + 1):
                send(*round_of(n))
            pool.wait_ge(S["slots_done"], 2)
            pool.wait_ge(S["shared"], 4)
            pool.wait_ge(S["rows_done"], B)
            for k in range(2):
                if k == 1:
                    pool.wait_ge(S["sorted_b"], 16 * GROUP_TILES[1])
                tails(1, k)
                for n in range(GROUP_TILES[1]):
                    sort_rows(1, k, [GROUP_FROM[1] + n], "sorted_b")
                    send(*round_of(TILES_IN + 1 + k * GROUP_TILES[1] + n))
            ahead = (TILES_IN + 1 + 2 * GROUP_TILES[1]) // RING + 1
            for n in range(TILES_IN + 1 + 2 * GROUP_TILES[1], ahead * RING):
                send(*round_of(n))
            with pool.Fori(ahead, FIRST_ROUNDS + 1) as i:
                for u in range(RING):
                    send(i, u)

            def final(b):
                pool.wait_ge(S["y_gated"], b + 1)
                nc.gpsimd.tensor_tensor(x1[:, b], y_gated[b % 2], x1[:, b], ALU.add).then_inc(S["final_done"], 1)

            for i in range(FIRST_ROUNDS + 1, ROUNDS):
                for u in range(RING):
                    send(i, u)
                    if u > 2 or (u == 0 and i > FIRST_ROUNDS + 1):
                        final(4 * (i - FIRST_ROUNDS - 1) + (u - 3 if u else -1))
            for b in range(B - 5, B):
                final(b)

        @block.scalar
        def _(act_e):
            act_e.wait_ge(S["loaded_a"], 32)
            nc.scalar.activation(c_exp[:], c_s[:], ACT.Exp, scale=-1.0).then_inc(S["c_exp_done"], 1)

            def gelu(i, u):
                act_e.wait_ge(S["up_mm"], i * RING + (u + 1))
                for hc in range(HC):
                    if hc == HC - 1:
                        nc.scalar.activation(y_bias[u % 3], staged[u % 3][:, HID + HC:], ACT.Copy, scale=row_in[u][:, D:D + 1])
                    nc.scalar.activation(act[u % 2][:, hc, :], ps_sc[u % 2][:, hc * P:(hc + 1) * P], ACT.Gelu_apprx_tanh,
                                         bias=staged[u % 3][:, HID + hc:HID + hc + 1]).then_inc(S["gelu_done"], 1)

            def turned_out(i, u):
                act_e.wait_ge(S["x_turned"], i * RING + (u + 1))
                nc.scalar.activation(row_t[u % 2], ps_max[2 * (u % 2)][:, 0:P], ACT.Copy).then_inc(S["row_t_done"], 1)

            def gelu_and_turned(i, u):
                gelu(i, u)
                if not (isinstance(i, int) and i * RING + u + 2 >= ALL_ROW_TILES):
                    turned_out(i, u + 2)

            def gap_exponential(group):
                js = slice(GROUP_FROM[group], GROUP_FROM[group] + GROUP_TILES[group])
                act_e.wait_ge(S["gap_done"], group + 1)
                nc.scalar.activation(gap_exp[:, js], gap[:, js], ACT.Exp).then_inc(S["gap_exp_done"], 1)

            def emit(s):
                def high_parts(n):
                    s.wait(act_e, S["roped_done"], 0, 1, 1)
                    if s.t == 0:
                        act_e.wait_ge(S["zeroed"], 8)
                    which, parts, slots, name, old = (
                        (1, k_parts, (0, 2), "k_high", "k_tr"), (0, q_parts, (0, 1), "q_high", "qm_tr"))[n]
                    s.wait(act_e, S[old], -1, 2, 2)
                    src = roped.rearrange("p a (w h d) -> p a w h d", w=2, h=HEADS)[:, :, which]
                    for slot in slots:
                        nc.scalar.activation(parts[:, :, :, slot * DK:(slot + 1) * DK], src,
                                             ACT.Copy).then_inc(S[name], 1)

                def exp(h):
                    s.wait(act_e, S["score_mm"], -1, 16, h + 1)
                    if h >= 8:
                        s.wait(act_e, S["pv_mm"], -1, 4, h // 4 - 1)
                    else:
                        s.wait(act_e, S["pv_mm"], -2, 4, h // 4 + 3)
                    nc.scalar.activation(probs[:, h % 8, :], ps_sc[h % 2][:, 0:384], ACT.Exp,
                                         scale=SCALE).then_inc(S["exp_done"], 1)

                def heads_out(g, d):
                    s.wait(act_e, S["pv_mm"], d, 4, g + 1)
                    s.wait(act_e, S["heads_tr"], d - 2, 2, 2)
                    nc.scalar.activation(heads_t[(s.t + d) % 2][:, g, :], ps_pv[:, 0:T],
                                         ACT.Copy).then_inc(S["heads_done"], 1)

                def take_out(name):
                    bank = misc[BANK[name]]
                    if name[:2] == "qm":
                        n = int(name[2])
                        s.wait(act_e, S["qm_tr"], -1, 2, n + 1)
                        s.wait(act_e, S["score_mm"], -2, 16, 16)
                        nc.scalar.activation(qm_stack[:, 2 * n:2 * n + 2, :].rearrange("p g t -> p (g t)"),
                                             bank[:], ACT.Copy).then_inc(S["qm_stacked"], 1)
                    elif name in ("k0", "k1", "q0", "q1"):
                        which, n = name[0], int(name[1])
                        s.wait(act_e, S[f"{which}_tr"], 0, 2, n + 1)
                        dst = k_stack[s.t % 2] if which == "k" else q_stack
                        if which == "k":
                            s.wait(act_e, S["score_mm"], -2, 16, 16)
                        else:
                            s.wait(act_e, S["max_mm"], -1, 16, 16)
                        nc.scalar.activation(dst[:, 2 * n:2 * n + 2, :].rearrange("p g t -> p (g t)"),
                                             bank[:], ACT.Copy).then_inc(S[f"{which}_stacked"], 1)
                    elif name == "attnT":
                        s.wait(act_e, S["attn_tr"], -2, 1, 1)
                        s.wait(act_e, S["wo_mm"], -3, 1, 1)
                        nc.scalar.activation(attn_t[:], bank[:, 0:T], ACT.Copy).then_inc(S["attn_t_done"], 1)
                    elif name == "zT":
                        s.wait(act_e, S["zt_done"], 1, 1, 1)
                        s.wait(act_e, S["qkv_mm"], 0, 2, 2)
                        if s.t == -1:
                            act_e.wait_ge(S["mod_done"], 4)
                        m = s.pick(mod[:], 1, 1)
                        nc.scalar.activation(h_t[:], bank[:, 0:T], ACT.Identity,
                                             bias=m[:, 0:1], scale=m[:, 1:2]).then_inc(S["ht_done"], 1)
                    elif name == "z2T":
                        s.wait(act_e, S["z2_tr"], -2, 1, 1)
                        s.wait(act_e, S["router_mm"], -3, 1, 1)
                        m = s.pick(mod[:], 1, -2)
                        nc.scalar.activation(h2_now, bank[:, 0:T], ACT.Identity,
                                             bias=m[:, 2:3], scale=m[:, 3:4]).then_inc(S["h2_done"], 1)

                for h in range(-1, HEADS):
                    if s.t == B + 1 and h >= TILES_AT:
                        if h == TILES_AT:
                            act_e.wait_ge(S["q_low"], B)
                            act_e.wait_ge(S["k_low"], B)
                            act_e.wait_ge(S["z_done"], 2 * B)
                            for u in range(2):
                                turned_out(0, u)
                        gelu_and_turned(*round_of(h - TILES_AT))
                    if h >= 0 and s.has(-1):
                        exp(h)
                        if h % 4 == 2 and h > 4:
                            heads_out(h // 4 - 1, -1)
                    for name, d in USES.get(h, []):
                        if s.has(d):
                            take_out(name)
                        if name == "qm0" and s.has(-2):
                            heads_out(3, -2)
                    if h in (0, 1) and s.has(0):
                        high_parts(h)
                if s.t == LAST:
                    gap_exponential(0)

            steps(act_e, emit)
            gelu_and_turned(*round_of(TILES_IN))
            gap_exponential(1)
            for n in range(TILES_IN + 1, LONE * RING):
                gelu_and_turned(*round_of(n))
            with act_e.Fori(LONE, ROUNDS - 1) as i:
                for u in range(RING):
                    gelu_and_turned(i, u)
            for u in range(RING):
                gelu_and_turned(ROUNDS - 1, u)

        @block.vector
        def _(dve):
            dve.wait_ge(S["loaded_b"], 96)
            for n in range(2):
                nc.vector.tensor_copy(mask_q[:, n, :], causal_s[:, 0, :]).then_inc(S["masks_ready"], 1)
                nc.vector.tensor_copy(mask_k[:, n, :], causal_s[:, 1, :]).then_inc(S["masks_ready"], 1)
            nc.vector.tensor_copy(ident_b[:], ident_s[:]).then_inc(S["masks_ready"], 1)
            nc.vector.tensor_scalar(strict[:], causal_s[:, 0, :], 0.0, None, ALU.is_lt).then_inc(S["masks_ready"], 1)
            nc.vector.tensor_scalar(ones[:], causal_s[:, 0, :], 0.0, None, ALU.is_le).then_inc(S["masks_ready"], 1)
            dve.wait_ge(S["c_exp_done"], 1)
            nc.vector.tensor_scalar_add(c_den[:], c_exp[:], 1.0).then_inc(S["c_den_done"], 1)
            dve.wait_ge(S["c_den_done"], 1)
            nc.vector.reciprocal(c_sig[:], c_den[:]).then_inc(S["c_sig_done"], 1)
            dve.wait_ge(S["c_sig_done"], 1)
            nc.vector.tensor_tensor(c_silu[:], c_s[:], c_sig[:], ALU.mult).then_inc(S["silu_done"], 1)
            dve.wait_ge(S["mod_mm"], 1)
            for n in range(4):
                nc.vector.tensor_scalar_add(mod[:, :, n], ps_max[0][:, n * B:(n + 1) * B],
                                            float(n % 2)).then_inc(S["mod_done"], 1)
            dve.wait_ge(S["gate_mm"], 1)
            g = ps_max[1][0:B, 0:2 * D]
            nc.vector.tensor_scalar(gate_sign[:], g, 0.0, 2.0, ALU.is_ge, ALU.mult).then_inc(S["sign_done"], 1)
            nc.vector.tensor_scalar(gate_neg[:], g, -1.0, 0.25, ALU.mult, ALU.max).then_inc(S["neg_done"], 1)
            dve.wait_ge(S["neg_done"], 1)
            nc.vector.tensor_tensor(gate_size[:], g, gate_neg[:], ALU.max).then_inc(S["size_done"], 1)
            dve.wait_ge(S["sign_done"], 1)
            dve.wait_ge(S["size_done"], 1)
            nc.vector.tensor_scalar_add(gate_row[:, 2 * D:3 * D], ps_max[1][0:B, 2 * D:3 * D], 1.0).then_inc(S["gate_done"], 1)
            nc.vector.tensor_copy(gate_row[:, 3 * D:4 * D], ps_max[1][0:B, 3 * D:4 * D]).then_inc(S["gate_done"], 1)
            nc.vector.scalar_tensor_tensor(out=gate_row[:, 0:2 * D], in0=gate_sign[:], scalar=-1.0, in1=gate_size[:],
                                           op0=ALU.add, op1=ALU.mult).then_inc(S["gate_done"], 1)

            def statistics(s, d, src, st, mo, sd, md):
                for a in range(TILES):
                    nc.vector.bn_stats(st[:, a, :], src[:, a, :]).then_inc(S[sd], 1)
                s.hold(dve, S[sd], d, 2, 2, S["dve_passed"])
                for a in range(TILES):
                    nc.vector.bn_aggr(mo[:, a, :], st[:, a, :]).then_inc(S[md], 1)

            def normalise(s, d, src, mo, rs, zz, rd, zd, readers):
                s.wait(dve, S[rd], d, 1, 1)
                s.wait(dve, S[readers], d - 1, 1, 1)
                if readers == "z2_tr":
                    s.wait(dve, S["row_scaled"], d - 1, 1, 1)
                for a in range(TILES):
                    nc.vector.tensor_scalar(zz[:, a, :], src[:, a, :], mo[:, a, 0:1], rs[:, a:a + 1],
                                            ALU.subtract, ALU.mult).then_inc(S[zd], 1)

            def stage(i, u):
                e = dve.value_load(expert_at(i, u), min_val=0, max_val=EXPERTS - 1)
                nc.vector.tensor_copy(staged[u % 3], wfc_s[:, bass.ds(e, 1), :].rearrange("p o c -> p (o c)"))
                nc.vector.tensor_copy(staged_proj[u % 3].rearrange("p c d -> p (c d)"),
                                      wproj_s[:, bass.ds(e, 1)].rearrange("p o c d -> p (o c d)")
                                      ).then_inc(S["staged_done"], 1)

            def weighted(i, u):
                dve.wait_ge(S["down_mm"], i * RING + (u + 1))
                nc.vector.scalar_tensor_tensor(out=y_out[u], in0=ps_y[u % 2][:, 0:D], scalar=row_in[u][:, D:D + 1],
                                               in1=y_bias[u % 3], op0=ALU.mult, op1=ALU.add).then_inc(S["y_done"], 1)

            def final(b):
                n = b // 4
                if b % 4 == 0:
                    dve.wait_ge(pairs_in[n], 64)
                yp = y_pair[n % 2][:, b % 4]
                nc.vector.tensor_tensor(y_sum[b % 2], yp[:, :, 0, :], yp[:, :, 1, :], ALU.add).then_inc(S["y_summed"], 1)
                dve.wait_ge(S["y_summed"], b + 1)
                gate = gates[:, b, D:2 * D].rearrange("p (o d) -> p o d", o=1).broadcast_to([P, TILES, D])
                if b >= 2:
                    dve.wait_ge(S["final_done"], b - 1)
                nc.vector.tensor_tensor(y_gated[b % 2], y_sum[b % 2], gate, ALU.mult).then_inc(S["y_gated"], 1)
                dve.wait_ge(S["y_gated"], b + 1)

            def tile(i, u):
                left = ALL_ROW_TILES - (i * RING + u) if isinstance(i, int) else ALL_ROW_TILES
                weighted(i, u)
                if left > 3:
                    stage(i, u + 3)

            def first_tile():
                dve.wait_ge(S["pv_mm"], 4 * B)
                dve.wait_ge(S["expert_done"], 1)
                dve.wait_ge(S["loaded_c"], 64)
                dve.wait_ge(S["v_done"], B)
                for u in range(3):
                    stage(0, u)

            def find_top(tiles):
                lg = logits[:].rearrange("p b (a e) -> p (b a) e", a=TILES)
                for n in tiles:
                    nc.vector.max(top[:, n, :], lg[:, n, :]).then_inc(S["top_done"], 1)
                dve.wait_ge(S["top_done"], tiles[-1] + 1)
                for n in tiles:
                    nc.vector.max_index(top_at[:, n, :], top[:, n, :], lg[:, n, :]).then_inc(S["at_done"], 1)

            def choose(group):
                js = slice(GROUP_FROM[group], GROUP_FROM[group] + GROUP_TILES[group])
                wide = [P, GROUP_TILES[group], EXPERTS]
                nc.vector.tensor_tensor(gap[:, js], top[:, js, 1], top[:, js, 0], ALU.subtract).then_inc(S["gap_done"], 1)
                dve.wait_ge(S["at_done"], js.stop)
                nc.vector.tensor_copy(top_f[:, js, :], top_at[:, js, 0:2]).then_inc(S["route_step"], 1)
                dve.wait_ge(S["route_step"], ROUTE_STEPS * group + 1)
                for k in range(2):
                    nc.vector.tensor_tensor(hot[:, k, js], iota_r.rearrange("p (o e) -> p o e", o=1).broadcast_to(wide),
                                            top_f[:, js, k:k + 1].broadcast_to(wide), ALU.is_equal).then_inc(S["route_step"], 1)
                dve.wait_ge(S["route_step"], ROUTE_STEPS * group + 3)
                to = slice(js.start + group, js.stop + group)
                nc.vector.tensor_tensor(chosen[:, to], hot[:, 0, js], hot[:, 1, js], ALU.add).then_inc(S["chosen_done"], 1)

            def read_ranks(group, bank):
                dve.wait_ge(S["rank_mm"], group + 1)
                n = (GROUP_TILES[group] + 1) * EXPERTS
                to = slice(GROUP_FROM[group] + group, GROUP_FROM[group] + group + GROUP_TILES[group] + 1)
                nc.vector.tensor_copy(ranks[:, to].rearrange("p n e -> p (n e)"), bank[:, RANKS_AT:RANKS_AT + n]
                                      ).then_inc(S["ranks_read"], 1)

            def place(group):
                js = slice(GROUP_FROM[group], GROUP_FROM[group] + GROUP_TILES[group])
                nt = GROUP_TILES[group]
                rk = ranks[:, js.start + group:js.stop + group + 1]
                done = ROUTE_STEPS * group + 3

                dve.wait_ge(S["gap_exp_done"], group + 1)
                nc.vector.tensor_scalar_add(gap_den[:, js], gap_exp[:, js], 1.0).then_inc(S["route_step"], 1)
                dve.wait_ge(S["ranks_read"], group + 1)
                cmp = [P, EXPERTS, nt]
                nc.vector.tensor_tensor(over[:, :, 0:nt], rk[:, nt, :].rearrange("p (e o) -> p e o", o=1).broadcast_to(cmp),
                                        full_r[:, 0:nt].rearrange("p (o n) -> p o n", o=1).broadcast_to(cmp),
                                        ALU.is_gt).then_inc(S["route_step"], 1)
                dve.wait_ge(S["route_step"], done + 2)
                first = share[:, 0, js]
                nc.vector.reciprocal(first, gap_den[:, js]).then_inc(S["shared"], 1)
                nc.vector.tensor_reduce(tiles_of[:], over[:, :, 0:nt], AX, ALU.add).then_inc(S["route_step"], 1)
                dve.wait_ge(S["shared"], 2 * group + 1)
                nc.vector.tensor_tensor(share[:, 1, js], first, gap_exp[:, js],
                                        ALU.mult).then_inc(S["shared"], 1)
                dve.wait_ge(S["route_step"], done + 3)
                sq = [P, EXPERTS, EXPERTS]
                nc.vector.tensor_tensor(ahead[:], before_r.rearrange("p (e f) -> p e f", f=EXPERTS),
                                        tiles_of[:].rearrange("p (o f) -> p o f", o=1).broadcast_to(sq),
                                        ALU.mult).then_inc(S["route_step"], 1)
                dve.wait_ge(S["route_step"], done + 4)
                nc.vector.tensor_reduce(base_0[:], ahead[:], AX, ALU.add).then_inc(S["route_step"], 1)
                dve.wait_ge(S["route_step"], done + 5)
                nc.vector.tensor_scalar_add(base[:], base_0[:], float(ROW_FROM[group])).then_inc(S["route_step"], 1)
                dve.wait_ge(S["route_step"], done + 6)
                wide = [P, nt, EXPERTS]
                nc.vector.scalar_tensor_tensor(out=slot_all[:, js], in0=base[:].rearrange("p (o e) -> p o e", o=1).broadcast_to(wide),
                                               scalar=float(P), in1=rk[:, 0:nt], op0=ALU.mult, op1=ALU.add
                                               ).then_inc(S["route_step"], 1)
                dve.wait_ge(S["route_step"], done + 7)
                for k in range(2):
                    nc.vector.tensor_tensor(slot_hot[:, k, js], slot_all[:, js], hot[:, k, js], ALU.mult).then_inc(S["route_step"], 1)
                dve.wait_ge(S["route_step"], done + 9)
                for k in range(2):
                    nc.vector.tensor_reduce(slot_f[:, k, js], slot_hot[:, k, js], AX, ALU.add).then_inc(S["route_step"], 1)
                dve.wait_ge(S["route_step"], done + 11)
                nc.vector.tensor_copy(slots[:, :, js], slot_f[:, :, js]).then_inc(S["slots_done"], 1)
                ts = slice(ROW_FROM[group], ROW_FROM[group] + ROW_TILES[group])
                wide = [1, ROW_TILES[group], EXPERTS]
                nc.vector.tensor_tensor(reached[:, 0:ROW_TILES[group]], tile_r[:, ts].rearrange("p (n o) -> p n o", o=1).broadcast_to(wide),
                                        base[0:1].rearrange("p (o e) -> p o e", o=1).broadcast_to(wide),
                                        ALU.is_ge).then_inc(S["route_step"], 1)
                dve.wait_ge(S["route_step"], done + 12)
                nc.vector.tensor_reduce(reached_n[:, ts], reached[:, 0:ROW_TILES[group]], AX, ALU.add).then_inc(S["route_step"], 1)
                dve.wait_ge(S["route_step"], done + 13)
                nc.vector.tensor_scalar_add(expert_of[:, ts], reached_n[:, ts], -1.0).then_inc(S["expert_done"], 1)

            def emit(s):
                def rope_sum():
                    s.wait(dve, S["rope_done"], 0, 5, 5)
                    s.wait(dve, S["q_high"], -1, 2, 2)
                    nc.vector.tensor_tensor(roped, rope_a, rope_b, ALU.add).then_inc(S["roped_done"], 1)

                def low_parts(n):
                    which, parts, of, to, high, low = (
                        (1, k_parts, 0, 1, "k_high", "k_low"), (0, q_parts, 0, 2, "q_high", "q_low"))[n]
                    s.wait(dve, S[high], 0, 2, 2)
                    src = roped.rearrange("p a (w h d) -> p a w h d", w=2, h=HEADS)[:, :, which]
                    nc.vector.tensor_tensor(parts[:, :, :, to * DK:(to + 1) * DK], src,
                                            parts[:, :, :, of * DK:(of + 1) * DK].bitcast(F32),
                                            ALU.subtract).then_inc(S[low], 1)

                def divide(a):
                    s.wait(dve, S["heads_tr"], -2, 2, a + 1)
                    m = misc[BANK[f"heads{a}"]][:].rearrange("p (h r) -> p h r", h=HEADS)
                    nc.vector.reciprocal(rsum[:, a, :], m[:, :, DK]).then_inc(S["rsum_done"], 1)
                    s.wait(dve, S["rsum_done"], -2, 2, a + 1)
                    s.wait(dve, S["attn_tr"], -3, 1, 1)
                    nc.vector.tensor_tensor(attn[:, a], m[:, :, 0:DK],
                                            rsum[:, a, :].rearrange("p (h o) -> p h o", o=1).broadcast_to([P, HEADS, DK]),
                                            ALU.mult).then_inc(S["attn_done"], 1)

                def residual():
                    s.wait(dve, S["wo_mm"], -2, 1, 1)
                    if s.t == 2:
                        dve.wait_ge(S["loaded_o"], 48)
                        dve.wait_ge(S["gate_in"], 16)
                    bias = bo_s[:].rearrange("p (o d) -> p o d", o=1).broadcast_to([P, TILES, D])
                    gate = s.pick(gates[:], 1, -2)[:, 0:D].rearrange("p (o d) -> p o d", o=1).broadcast_to([P, TILES, D])
                    nc.vector.tensor_tensor(proj_b, misc[BANK["wo"]][:, 0:T].rearrange("p (a d) -> p a d", a=TILES),
                                            bias, ALU.add).then_inc(S["wo_bias"], 1)
                    s.wait(dve, S["wo_bias"], -2, 1, 1)
                    nc.vector.tensor_tensor(proj_g, proj_b, gate, ALU.mult).then_inc(S["wo_gated"], 1)
                    s.wait(dve, S["wo_gated"], -2, 1, 1)
                    s.slot_wait(dve, xres_loaded, -2)
                    s.wait(dve, S["x1_kept"], -3, 1, 1)
                    nc.vector.tensor_tensor(x1_now, proj_g, x_res[s.t % 2][:], ALU.add).then_inc(S["x1_done"], 1)
                    s.wait(dve, S["x1_done"], -2, 1, 1)

                def maxima_of(h):
                    s.wait(dve, S["max_mm"], 0, 16, h + 1)
                    nc.vector.tensor_reduce(maxima[:, 0, h:h + 1], ps_max[h % 3][:, 0:128], AX, ALU.max)
                    nc.vector.tensor_reduce(maxima[:, 1, h:h + 1], ps_max[h % 3][:, 128:384], AX,
                                            ALU.max).then_inc(S["max_done"], 1)

                if s.has(0):
                    rope_sum()
                if s.has(1):
                    s.slot_wait(dve, x_loaded, 1)
                    statistics(s, 1, x_in[(s.t + 1) % 2], stats, moments, "stats_done", "moments_done")
                if s.has(0):
                    low_parts(0)
                if s.has(-2):
                    divide(0)
                if s.has(0):
                    low_parts(1)
                if s.has(-2):
                    divide(1)
                if s.has(1):
                    normalise(s, 1, x_in[(s.t + 1) % 2], moments, rstd, z, "rstd_done", "z_done", "zt_done")
                for h in range(HEADS):
                    if s.t == B + 1 and h >= TILES_AT:
                        if h == TILES_AT:
                            first_tile()
                        tile(*round_of(h - TILES_AT))
                    if s.has(0):
                        for m in MAX_AT.get(h, ()):
                            maxima_of(m)
                    if h == RESIDUAL_AT and s.has(-2):
                        residual()
                        statistics(s, -2, x1_now, stats2, moments2, "stats2_done", "moments2_done")
                    if h in QKV_AT and s.has(1):
                        a = QKV_AT.index(h)
                        s.wait(dve, S["qkv_mm"], 1, 2, a + 1)
                        s.wait(dve, S["rope_done"], 0, 5, 5)
                        s.wait(dve, S["v_done"], 0, 1, 1)
                        nc.vector.tensor_tensor(qkv[:, a, :], misc[BANK[f"qkv{a}"]][:, 0:384], bqkv_s[:],
                                                ALU.add).then_inc(S["qkv_done"], 1)
                    if h == NORMALISE_AT and s.has(-2):
                        normalise(s, -2, x1_now, moments2, rstd2, z2, "rstd2_done", "z2_done", "z2_tr")
                    if s.t == LAST and h < 8:
                        if h == 0:
                            dve.wait_ge(S["loaded_w"], 48)
                            dve.wait_ge(S["logits_done"], GROUP_B[0])
                        find_top(range(3 * h, 3 * h + 3))
                    if s.t == LAST and h == 8:
                        choose(0)
                if s.has(0):
                    s.wait(dve, S["max_done"], 0, 16, 16)
                    m = maxima[:].rearrange("p a (h o) -> p (a h) o", o=1)
                    v = q_parts[:].rearrange("p a h r -> p (a h) r")
                    nc.vector.tensor_scalar(v[:, :, PARTS:PARTS + 1], m, -1.0, None, ALU.mult).then_inc(S["shift_high"], 1)
                    s.wait(dve, S["shift_high"], 0, 1, 1)
                    nc.vector.scalar_tensor_tensor(out=v[:, :, PARTS + 1:PARTS + 2], in0=m, scalar=-1.0,
                                                   in1=v[:, :, PARTS:PARTS + 1].bitcast(F32),
                                                   op0=ALU.mult, op1=ALU.subtract).then_inc(S["shifts_done"], 1)
                if s.has(-2):
                    s.wait(dve, S["router_mm"], -2, 1, 1)
                    if s.t == LAST:
                        read_ranks(0, misc[BANK["router"]])
                        place(0)
                        dve.wait_ge(S["ranks_read"], 1)
                    nc.vector.tensor_copy(s.pick(logits[:], 1, -2),
                                          misc[BANK["router"]][:, 0:TILES * EXPERTS]).then_inc(S["logits_done"], 1)

            steps(dve, emit)

            dve.wait_ge(S["logits_done"], B)
            find_top(range(GROUP_FROM[1], NTILES))
            choose(1)
            tile(*round_of(TILES_IN))
            read_ranks(1, misc[BANK["router"]])
            tile(*round_of(TILES_IN + 1))
            place(1)
            dve.wait_ge(S["expert_done"], 2)
            for n in range(TILES_IN + 2, LONE * RING):
                tile(*round_of(n))
            with dve.Fori(LONE, FIRST_ROUNDS + 1) as i:
                for u in range(RING):
                    tile(i, u)
            for i in range(FIRST_ROUNDS + 1, ROUNDS):
                for u in range(RING):
                    tile(i, u)
                    if u in (2, 3, 4, 5):
                        final(4 * (i - FIRST_ROUNDS - 1) + u - 2)
            for b in range(B - 4, B):
                final(b)

        @block.tensor
        def _(pe):
            def take(name, s):
                prev = before(name, s)
                if prev:
                    who, d = prev
                    sem_name, per, k = freed[who]
                    s.wait(pe, S[sem_name], d, per, k)
                return misc[BANK[name]]

            def rank(group, bank):
                pe.wait_ge(S["chosen_done"], group + 1)
                nt = GROUP_TILES[group]
                at = GROUP_FROM[group] + group
                nc.tensor.matmul(bank[:, RANKS_AT:RANKS_AT + (nt + 1) * EXPERTS], strict[:],
                                 chosen[:, at:at + nt + 1].rearrange("p n e -> p (n e)"),
                                 start=True, stop=False, skip_group_check=True)
                for n in range(nt):
                    later = nt - n
                    last = nc.tensor.matmul(
                        bank[:, RANKS_AT + (n + 1) * EXPERTS:RANKS_AT + (nt + 1) * EXPERTS].rearrange("p (n e) -> p n e", e=EXPERTS),
                        ones[:], chosen[:, at + n:at + n + 1, :].broadcast_to([P, later, EXPERTS]),
                        start=False, stop=(n == nt - 1), skip_group_check=True)
                last.then_inc(S["rank_mm"], 1)

            def turn(i, u):
                n = u // RING + 1
                pe.wait_ge(row_loaded[u % RING], i * 16 + 16 * n)
                nc.tensor.transpose(ps_max[2 * (u % 2)][:, 0:P], row_in[u % RING][:, 0:D], ident_s[:]).then_inc(S["x_turned"], 1)

            def up(i, u):
                pe.wait_ge(S["row_t_done"], i * RING + (u + 1))
                pe.wait_ge(S["staged_done"], i * RING + (u + 1))
                for hc in range(HC):
                    last = nc.tensor.matmul(ps_sc[u % 2][:, hc * P:(hc + 1) * P], staged[u % 3][:, hc * P:(hc + 1) * P],
                                            row_t[u % 2], start=True, stop=True)
                last.then_inc(S["up_mm"], 1)

            def down(i, u):
                pe.wait_ge(S["gelu_done"], i * (RING * HC) + (u + 1) * HC)
                for hc in range(HC):
                    last = nc.tensor.matmul(ps_y[u % 2][:, 0:D], act[u % 2][:, hc, :],
                                            staged_proj[u % 3][:, hc, :],
                                            start=(hc == 0), stop=(hc == HC - 1))
                last.then_inc(S["down_mm"], 1)

            def tile(i, u):
                left = ALL_ROW_TILES - (i * RING + u) if isinstance(i, int) else ALL_ROW_TILES
                if left > 1:
                    up(i, u + 1)
                if left > 2:
                    turn(i, u + 2)
                if left == 1:
                    pe.wait_ge(S["y_done"], ALL_ROW_TILES - 2)
                down(i, u)

            def first_tile():
                pe.wait_ge(S["loaded_c"], 64)
                pe.wait_ge(S["max_done"], B * 16)
                pe.wait_ge(S["exp_done"], B * 16)
                pe.wait_ge(S["heads_done"], B * 4)
                turn(0, 0)
                turn(0, 1)
                up(0, 0)

            pe.wait_ge(S["silu_done"], 1)
            for n, j in enumerate((0, 1, 3, 4)):
                last = nc.tensor.matmul(ps_max[0][:, n * B:(n + 1) * B], wmod_s[:, j * D:(j + 1) * D], c_silu[:],
                                        start=True, stop=True)
            last.then_inc(S["mod_mm"], 1)
            for n, j in enumerate((2, 5, 4, 3)):
                last = nc.tensor.matmul(ps_max[1][0:B, n * D:(n + 1) * D], c_silu[:], wmod_s[:, j * D:(j + 1) * D],
                                        start=True, stop=True)
            last.then_inc(S["gate_mm"], 1)
            pe.wait_ge(S["masks_ready"], 7)
            pe.wait_ge(S["zeroed"], 8)

            def emit(s):
                def spread(which, n, parts, sem_name, d):
                    bank = take(f"{which}{n}", s)
                    for g in range(2):
                        for a in range(TILES):
                            src = parts[:, a, 4 * (2 * n + g):4 * (2 * n + g) + 4, :].rearrange("p h r -> p (h r)").bitcast(F32)
                            last = nc.tensor.transpose(bank[:, g * T + a * P:g * T + (a + 1) * P], src, ident_s[:])
                    last.then_inc(S[sem_name], 1)

                def scores_for_max(h):
                    if h >= 3:
                        s.wait(pe, S["max_done"], 0, 16, h - 2)
                    elif h == 0:
                        s.wait(pe, S["max_done"], -1, 16, 16)
                    if s.t == 0 and h == 0:
                        pe.wait_ge(S["mod_done"], 4)
                        pe.wait_ge(S["size_done"], 1)
                        pe.wait_ge(S["gate_done"], 3)
                    if h % 8 == 0:
                        s.wait(pe, S["k_stacked"], 0, 2, h // 8 + 1)
                        s.wait(pe, S["q_stacked"], 0, 2, h // 8 + 1)
                    g = h // 4
                    rows = slice(ROWS * (h % 4), ROWS * (h % 4) + PARTS)
                    ks = k_stack[s.t % 2][rows, g, :]
                    bank = ps_max[h % 3]
                    blocks = bank[:].rearrange("p (c k) -> p c k", k=P)
                    nc.tensor.matmul(blocks[:, 0:4:3, :], q_stack[rows, g, 0:P], ks.rearrange("p (c k) -> p c k", k=P),
                                     start=True, stop=False, skip_group_check=True)
                    nc.tensor.matmul(bank[:, P:3 * P], q_stack[rows, g, P:2 * P], ks,
                                     start=False, stop=False, skip_group_check=True)
                    nc.tensor.matmul(blocks[:, 0:4:2, :], ident_b[:], mask_q[:],
                                     start=False, stop=True, skip_group_check=True).then_inc(S["max_mm"], 1)

                def scores(h):
                    if h % 8 == 0:
                        s.wait(pe, S["qm_stacked"], -1, 2, h // 8 + 1)
                    if h >= 2:
                        s.wait(pe, S["exp_done"], -1, 16, h - 1)
                    else:
                        s.wait(pe, S["exp_done"], -2, 16, 15 + h)
                    g = h // 4
                    r = ROWS * (h % 4)
                    rows = slice(r, r + PARTS + 2)
                    ks = k_stack[(s.t - 1) % 2]
                    bank = ps_sc[h % 2]
                    nc.tensor.matmul(bank[:, 0:T], ks[rows, g, 0:P], qm_stack[rows, g, :],
                                     start=True, stop=False, skip_group_check=True)
                    late = qm_stack[rows, g, P:2 * P].rearrange("p (o q) -> p o q", o=1).broadcast_to([PARTS + 2, 2, P])
                    nc.tensor.matmul(bank[:, T:2 * T].rearrange("p (c k) -> p c k", k=P), ks[rows, g, P:2 * P], late,
                                     start=False, stop=False, skip_group_check=True)
                    nc.tensor.matmul(bank[:].rearrange("p (c k) -> p c k", k=P)[:, 0:4:2, :], ident_b[:], mask_k[:],
                                     start=False, stop=True, skip_group_check=True).then_inc(S["score_mm"], 1)

                def weigh(g, d):
                    s.wait(pe, S["exp_done"], d, 16, 4 * g + 4)
                    if g == 0:
                        s.wait(pe, S["v_done"], d, 1, 1)
                    s.wait(pe, S["heads_done"], d, 4, g)
                    vw = v_wide[(s.t + d) % 2]
                    for a in range(TILES):
                        for w in range(4):
                            h = 4 * g + w
                            rows = slice(ROWS * w, ROWS * (w + 1))
                            last = nc.tensor.matmul(
                                ps_pv[rows, a * P:T], vw[:, a, h, :],
                                probs[:, h % 8, 0:T] if a == 0 else probs[:, h % 8, T:T + P],
                                start=(a == 0), stop=(a == 1), skip_group_check=True)
                    last.then_inc(S["pv_mm"], 1)

                def fill(name):
                    if name[:2] == "qm":
                        s.wait(pe, S["shifts_done"], -1, 1, 1)
                        spread("qm", int(name[2]), q_parts, "qm_tr", -1)
                        return
                    if name in ("k0", "k1", "q0", "q1"):
                        which = name[0]
                        s.wait(pe, S[f"{which}_low"], 0, 1, 1)
                        spread(which, int(name[1]), k_parts if which == "k" else q_parts, f"{which}_tr", 0)
                        return
                    if name[:5] == "heads":
                        a = int(name[5])
                        s.wait(pe, S["heads_done"], -2, 4, 4)
                        bank = take(name, s)
                        for g in range(GROUPS):
                            last = nc.tensor.transpose(bank[:, g * P:(g + 1) * P],
                                                       heads_t[s.t % 2][:, g, a * P:(a + 1) * P], ident_s[:])
                        last.then_inc(S["heads_tr"], 1)
                    elif name == "attnT":
                        s.wait(pe, S["attn_done"], -2, 2, 2)
                        bank = take(name, s)
                        for a in range(TILES):
                            last = nc.tensor.transpose(bank[:, a * P:(a + 1) * P],
                                                       attn[:, a].rearrange("p h d -> p (h d)"), ident_s[:])
                        last.then_inc(S["attn_tr"], 1)
                    elif name == "zT":
                        s.wait(pe, S["z_done"], 1, 2, 2)
                        bank = take(name, s)
                        for a in range(TILES):
                            last = nc.tensor.transpose(bank[:, a * P:(a + 1) * P], z[:, a, :], ident_s[:])
                        last.then_inc(S["zt_done"], 1)
                    elif name == "wo":
                        s.wait(pe, S["attn_t_done"], -2, 1, 1)
                        bank = take(name, s)
                        if s.t == 2:
                            pe.wait_ge(S["loaded_o"], 48)
                        for a in range(TILES):
                            last = nc.tensor.matmul(bank[:, a * D:(a + 1) * D], attn_t[:, a * P:(a + 1) * P], wo_s[:],
                                                    start=True, stop=True)
                        last.then_inc(S["wo_mm"], 1)
                    elif name[:3] == "qkv":
                        a = int(name[3])
                        s.wait(pe, S["ht_done"], 1, 1, 1)
                        bank = take(name, s)
                        nc.tensor.matmul(bank[:, 0:384], h_t[:, a * P:(a + 1) * P], wqkv_s[:],
                                         start=True, stop=True).then_inc(S["qkv_mm"], 1)
                    elif name == "z2T":
                        s.wait(pe, S["z2_done"], -2, 2, 2)
                        bank = take(name, s)
                        for a in range(TILES):
                            last = nc.tensor.transpose(bank[:, a * P:(a + 1) * P], z2[:, a, :], ident_s[:])
                        last.then_inc(S["z2_tr"], 1)
                    elif name == "router":
                        s.wait(pe, S["h2_done"], -2, 1, 1)
                        bank = take(name, s)
                        for a in range(TILES):
                            last = nc.tensor.matmul(bank[:, a * EXPERTS:(a + 1) * EXPERTS], h2_now[:, a * P:(a + 1) * P],
                                                    router_s[:], start=True, stop=True)
                        last.then_inc(S["router_mm"], 1)
                        if s.t == LAST:
                            rank(0, bank)

                for h in range(-1, HEADS):
                    if s.t == B + 1 and h >= TILES_AT:
                        if h == TILES_AT:
                            first_tile()
                        tile(*round_of(h - TILES_AT))
                    if h >= 0 and s.has(-1):
                        scores(h)
                        if h % 4 == 1 and h > 4:
                            weigh(h // 4 - 1, -1)
                    for name, d in USES.get(h, []):
                        if s.has(d):
                            fill(name)
                        if name == "qm0" and s.has(-2):
                            weigh(3, -2)
                    if s.has(0):
                        for m in MAX_AT.get(h, ()):
                            scores_for_max(m)

            steps(pe, emit)

            tile(*round_of(TILES_IN))
            rank(1, misc[BANK["router"]])
            for n in range(TILES_IN + 1, LONE * RING):
                tile(*round_of(n))
            with pe.Fori(LONE, ROUNDS - 1) as i:
                for u in range(RING):
                    tile(i, u)
            for u in range(RING):
                tile(ROUNDS - 1, u)


def kernel(**inputs):
    import concourse.bacc as _bacc
    from concourse.bass_utils import run_bass_kernel_spmd as _run

    f = {k: np.asarray(v) for k, v in inputs.items()}
    half = DK // 2
    freq = 1.0 / 10000.0 ** (2.0 * np.arange(half, dtype=np.float32) / DK)
    angles = np.arange(T, dtype=np.float32)[:, None] * freq[None, :].astype(np.float32)
    cos = np.cos(angles).astype(np.float32)
    sin = np.sin(angles).astype(np.float32)

    def table(first, second):
        row = np.concatenate([first, second], 1)
        return np.tile(row, (1, 2 * HEADS)).reshape(TILES, P, 256).transpose(1, 0, 2)

    after = np.triu(np.full((P, P), MASKED, np.float32), 1)
    arrays = {
        "x": f["L0_attn_x"],
        "c_t": f["L0_c"].T,
        "wmod": f["L0_wmod"],
        "wqkv": np.concatenate([f["L0_attn_WQ_w"].T, f["L0_attn_WK_w"].T, f["L0_attn_WV_w"].T], 1),
        "bqkv": np.concatenate([f["L0_attn_WQ_b"], f["L0_attn_WK_b"], f["L0_attn_WV_b"]])[None],
        "wo": f["L0_attn_Wo_w"].T,
        "bo": f["L0_attn_Wo_b"][None],
        "router": f["L0_ffn_router_w"].T,
        "w_fc": f["L0_ffn_w_fc"].transpose(1, 0, 2),
        "b_fc": f["L0_ffn_b_fc"].reshape(EXPERTS, HC, P).transpose(2, 0, 1),
        "w_proj": f["L0_ffn_w_proj"].reshape(EXPERTS, HC, P, D).transpose(2, 0, 1, 3),
        "b_proj": f["L0_ffn_b_proj"].reshape(1, EXPERTS, D),
        "cos": table(cos, cos),
        "sin": table(-sin, sin),
        "ident": np.eye(P, dtype=np.float32),
        "causal": np.stack([after, after.T], 1),
        "route": np.concatenate([
            np.arange(EXPERTS), np.tril(np.ones((EXPERTS, EXPERTS)), -1).ravel(), np.arange(NTILES) * P,
            np.arange(ALL_ROW_TILES)]).astype(np.float32)[None],
        "places": np.arange(NTILES * P * 2, dtype=np.uint32).reshape(NTILES, P, 2).transpose(1, 2, 0),
        "blank": np.array([[0] * (D + 1) + [SKIPPED]], np.uint32),
    }
    nc = _bacc.Bacc("TRN2", target_bir_lowering=False, num_devices=1)
    feeds, args = {}, []
    for name, a in arrays.items():
        a = np.ascontiguousarray(a)
        feeds[f"in_{name}"] = a
        args.append(nc.dram_tensor(f"in_{name}", a.shape, mybir.dt.from_np(a.dtype), kind="ExternalInput").ap())
    args.append(nc.dram_tensor("out", (B, T, D), F32, kind="ExternalOutput").ap())
    block_program(nc, *args)
    return _run(nc, [feeds], core_ids=[0]).results[0]["out"]
```
